# Optimizing a Trainium2 kernel written in Bass

```python
import numpy as np
import jax
import jax.numpy as jnp

def _softmax(x, axis=-1):
    return jax.nn.softmax(x, axis=axis)

def _gelu(x):
    return jax.nn.gelu(x, approximate=True)

def _silu(x):
    return jax.nn.silu(x)

def _sigmoid(x):
    return jax.nn.sigmoid(x)

def _layernorm(x, axis=-1, eps=1e-05):
    m = jnp.mean(x, axis=axis, keepdims=True)
    v = jnp.var(x, axis=axis, keepdims=True)
    return (x - m) / jnp.sqrt(v + eps)

def _scatter_add(tgt, idx, src, axis=0):
    return tgt.at[idx].add(src)

def _segment_sum(src, seg, n):
    return jax.ops.segment_sum(src, seg, n)
kernel_name = 'mk_hybrid_d1_jaxref_r8_085d84'

def setup_inputs(seed: int=0):
    np.random.seed(seed)
    _w = jnp.asarray

    def _L0_attn_a_setup():
        import jax, jax.numpy as jnp
        import numpy as np
        HEADS = 16
        DIM_HEAD = 64
        SEG = 32
        SCALE = DIM_HEAD ** (-0.5)
        INNER = HEADS * DIM_HEAD

        def elu1(x):
            return jax.nn.elu(x) + 1.0

        def rope(t, pos):
            d = t.shape[-1]
            freqs = 10000.0 ** (-jnp.arange(0, d, 2, dtype=jnp.float32) / d)
            ang = pos[:, None] * freqs
            cos = jnp.repeat(jnp.cos(ang), 2, axis=-1)
            sin = jnp.repeat(jnp.sin(ang), 2, axis=-1)
            t2 = t.reshape(t.shape[:-1] + (d // 2, 2))
            rot = jnp.stack((-t2[..., 1], t2[..., 0]), axis=-1).reshape(t.shape)
            return t * cos + rot * sin

        def _reference_tuple_inner(x, w_qkv, w_out, ln_g, ln_b, mem_beta):
            B, N, D = x.shape
            mu = x.mean(-1, keepdims=True)
            var = x.var(-1, keepdims=True)
            xn = (x - mu) / jnp.sqrt(var + 1e-05) * ln_g + ln_b
            qkv = xn @ w_qkv
            q, k, v = jnp.split(qkv, 3, axis=-1)

            def to_heads(t):
                return t.reshape(B, N, HEADS, DIM_HEAD).transpose(0, 2, 1, 3)
            q, k, v = map(to_heads, (q, k, v))
            next_k, next_v = (k, v)
            pos = jnp.arange(N, dtype=jnp.float32)
            qr, kr = (rope(q, pos), rope(k, pos))
            W = N // SEG

            def to_segs(t):
                return t.reshape(B, HEADS, W, SEG, DIM_HEAD).transpose(2, 0, 1, 3, 4)
            qs, ks, vs, qnope, knope = map(to_segs, (qr, kr, v, q, k))
            mask = jnp.tril(jnp.ones((SEG, SEG), bool))
            beta = jax.nn.sigmoid(mem_beta)
            mem0 = jnp.zeros((B, HEADS, DIM_HEAD, DIM_HEAD), x.dtype)
            z0 = jnp.full((B, HEADS, DIM_HEAD), 1e-06, x.dtype)

            def step(carry, inp):
                mem, z = carry
                q_s, k_s, v_s, qn_s, kn_s = inp
                scores = jnp.einsum('bhnd,bhmd->bhnm', q_s, k_s) * SCALE
                scores = jnp.where(mask, scores, -jnp.inf)
                sdpa = jnp.einsum('bhnm,bhmd->bhnd', jax.nn.softmax(scores, axis=-1), v_s)
                sq = elu1(qn_s)
                num = jnp.einsum('bhnk,bhkv->bhnv', sq, mem)
                den = jnp.einsum('bhnk,bhk->bhn', sq, z)[..., None]
                mem_out = num / (den + 1e-06)
                out = beta * mem_out + (1.0 - beta) * sdpa
                sk = elu1(kn_s)
                prev_v = jnp.einsum('bhnk,bhkv->bhnv', sk, mem) / jnp.einsum('bhnk,bhk->bhn', sk, z)[..., None]
                mem = mem + jnp.einsum('bhnk,bhnv->bhkv', sk, v_s - prev_v)
                z = z + sk.sum(axis=2)
                return ((mem, z), out)
            _, outs = jax.lax.scan(step, (mem0, z0), (qs, ks, vs, qnope, knope))
            o = outs.transpose(1, 0, 3, 2, 4).reshape(B, N, INNER)
            out = o @ w_out
            return (out, next_k, next_v)
        key = jax.random.key(seed)
        k1, k2, k3 = jax.random.split(key, 3)
        B, N, D = (4, 512, 128)
        x = jax.random.normal(k1, (B, N, D), dtype=jnp.float32)
        w_qkv = jax.random.normal(k2, (D, 3 * INNER), dtype=jnp.float32) * 0.02
        w_out = jax.random.normal(k3, (INNER, D), dtype=jnp.float32) * 0.02
        ln_g = jnp.ones((D,), jnp.float32)
        ln_b = jnp.zeros((D,), jnp.float32)
        mem_beta = jnp.zeros((1, HEADS, 1, 1), jnp.float32)
        return {'x': x, 'w_qkv': w_qkv, 'w_out': w_out, 'ln_g': ln_g, 'ln_b': ln_b, 'mem_beta': mem_beta}
    _L0_attn_a_in = _L0_attn_a_setup()

    def _L0_attn_b_setup():
        import jax, jax.numpy as jnp
        import numpy as np
        MAX_WAVELENGTH = 10000.0
        NEG_INF = -1000000000.0

        def apply_rope(x):
            S, D = (x.shape[1], x.shape[-1])
            inv_freq = 1.0 / MAX_WAVELENGTH ** (jnp.arange(0, D, 2, dtype=jnp.float32) / D)
            t = jnp.arange(S, dtype=jnp.float32)[:, None] * inv_freq[None, :]
            emb = jnp.concatenate([t, t], axis=-1)
            cos = jnp.cos(emb)[None, :, None, :].astype(x.dtype)
            sin = jnp.sin(emb)[None, :, None, :].astype(x.dtype)
            x1, x2 = jnp.split(x, 2, axis=-1)
            rotated = jnp.concatenate([-x2, x1], axis=-1)
            return x * cos + rotated * sin
        key = jax.random.key(seed)
        k1, k2, k3 = jax.random.split(key, 3)
        B, S, dim = (2, 256, 128)
        x = jax.random.normal(k1, (B, S, dim), dtype=jnp.float32)
        w_qkv = jax.random.normal(k2, (dim, 3 * dim), dtype=jnp.float32) * dim ** (-0.5)
        w_proj = jax.random.normal(k3, (dim, dim), dtype=jnp.float32) * dim ** (-0.5)
        b_proj = jnp.zeros((dim,), dtype=jnp.float32)
        return {'x': x, 'w_qkv': w_qkv, 'w_proj': w_proj, 'b_proj': b_proj}
    _L0_attn_b_in = _L0_attn_b_setup()

    def _L0_ffn_setup():
        import jax, jax.numpy as jnp
        import numpy as np
        MICRO_BATCHES = 2
        TOP_K = 2
        LN_EPS = 1e-05
        B, S, D = (4, 512, 128)
        E = 8
        DFF = 4 * D

        def _layernorm(x, g, b):
            mu = jnp.mean(x, axis=-1, keepdims=True)
            var = jnp.mean(jnp.square(x - mu), axis=-1, keepdims=True)
            return (x - mu) * jax.lax.rsqrt(var + LN_EPS) * g + b
        key = jax.random.key(seed)
        ks = jax.random.split(key, 12)
        sd = 1.0 / np.sqrt(D)
        sf = 1.0 / np.sqrt(DFF)
        return {'x': jax.random.normal(ks[0], (B, S, D), dtype=jnp.float32), 'ln_g': jnp.ones((D,), jnp.float32), 'ln_b': jnp.zeros((D,), jnp.float32), 'attn_w': jax.random.normal(ks[1], (D, D), jnp.float32) * sd, 'attn_b': jnp.zeros((D,), jnp.float32), 'gate_w': jax.random.normal(ks[2], (D, E), jnp.float32) * sd, 'w1': jax.random.normal(ks[3], (E, D, DFF), jnp.float32) * sd, 'b1': jnp.zeros((E, DFF), jnp.float32), 'w2': jax.random.normal(ks[4], (E, DFF, D), jnp.float32) * sf, 'b2': jnp.zeros((E, D), jnp.float32), 'next_w': jax.random.normal(ks[5], (D, D), jnp.float32) * sd, 'next_b': jnp.zeros((D,), jnp.float32)}
    _L0_ffn_in = _L0_ffn_setup()
    _d = {'L0_attn_a_x': _L0_attn_a_in['x'], 'L0_attn_a_w_qkv': _L0_attn_a_in['w_qkv'], 'L0_attn_a_w_out': _L0_attn_a_in['w_out'], 'L0_attn_a_ln_g': _L0_attn_a_in['ln_g'], 'L0_attn_a_ln_b': _L0_attn_a_in['ln_b'], 'L0_attn_a_mem_beta': _L0_attn_a_in['mem_beta'], 'L0_attn_b_w_qkv': _L0_attn_b_in['w_qkv'], 'L0_attn_b_w_proj': _L0_attn_b_in['w_proj'], 'L0_attn_b_b_proj': _L0_attn_b_in['b_proj'], 'L0_ffn_ln_g': _L0_ffn_in['ln_g'], 'L0_ffn_ln_b': _L0_ffn_in['ln_b'], 'L0_ffn_attn_w': _L0_ffn_in['attn_w'], 'L0_ffn_attn_b': _L0_ffn_in['attn_b'], 'L0_ffn_gate_w': _L0_ffn_in['gate_w'], 'L0_ffn_w1': _L0_ffn_in['w1'], 'L0_ffn_b1': _L0_ffn_in['b1'], 'L0_ffn_w2': _L0_ffn_in['w2'], 'L0_ffn_b2': _L0_ffn_in['b2'], 'L0_ffn_next_w': _L0_ffn_in['next_w'], 'L0_ffn_next_b': _L0_ffn_in['next_b']}
    _x0 = _d['L0_attn_a_x']
    _d['L0_attn_a_x'] = jax.random.normal(jax.random.fold_in(jax.random.key(seed), 1), (16, 512, 128), dtype=_x0.dtype)
    del _x0
    return _d

def reference(L0_attn_a_x, L0_attn_a_w_qkv, L0_attn_a_w_out, L0_attn_a_ln_g, L0_attn_a_ln_b, L0_attn_a_mem_beta, L0_attn_b_w_qkv, L0_attn_b_w_proj, L0_attn_b_b_proj, L0_ffn_ln_g, L0_ffn_ln_b, L0_ffn_attn_w, L0_ffn_attn_b, L0_ffn_gate_w, L0_ffn_w1, L0_ffn_b1, L0_ffn_w2, L0_ffn_b2, L0_ffn_next_w, L0_ffn_next_b):

    def _L0_attn_a_ref(x, w_qkv, w_out, ln_g, ln_b, mem_beta):
        import jax, jax.numpy as jnp
        import numpy as np
        HEADS = 16
        DIM_HEAD = 64
        SEG = 32
        SCALE = DIM_HEAD ** (-0.5)
        INNER = HEADS * DIM_HEAD

        def elu1(x):
            return jax.nn.elu(x) + 1.0

        def rope(t, pos):
            d = t.shape[-1]
            freqs = 10000.0 ** (-jnp.arange(0, d, 2, dtype=jnp.float32) / d)
            ang = pos[:, None] * freqs
            cos = jnp.repeat(jnp.cos(ang), 2, axis=-1)
            sin = jnp.repeat(jnp.sin(ang), 2, axis=-1)
            t2 = t.reshape(t.shape[:-1] + (d // 2, 2))
            rot = jnp.stack((-t2[..., 1], t2[..., 0]), axis=-1).reshape(t.shape)
            return t * cos + rot * sin

        def _reference_tuple_inner(x, w_qkv, w_out, ln_g, ln_b, mem_beta):
            B, N, D = x.shape
            mu = x.mean(-1, keepdims=True)
            var = x.var(-1, keepdims=True)
            xn = (x - mu) / jnp.sqrt(var + 1e-05) * ln_g + ln_b
            qkv = xn @ w_qkv
            q, k, v = jnp.split(qkv, 3, axis=-1)

            def to_heads(t):
                return t.reshape(B, N, HEADS, DIM_HEAD).transpose(0, 2, 1, 3)
            q, k, v = map(to_heads, (q, k, v))
            next_k, next_v = (k, v)
            pos = jnp.arange(N, dtype=jnp.float32)
            qr, kr = (rope(q, pos), rope(k, pos))
            W = N // SEG

            def to_segs(t):
                return t.reshape(B, HEADS, W, SEG, DIM_HEAD).transpose(2, 0, 1, 3, 4)
            qs, ks, vs, qnope, knope = map(to_segs, (qr, kr, v, q, k))
            mask = jnp.tril(jnp.ones((SEG, SEG), bool))
            beta = jax.nn.sigmoid(mem_beta)
            mem0 = jnp.zeros((B, HEADS, DIM_HEAD, DIM_HEAD), x.dtype)
            z0 = jnp.full((B, HEADS, DIM_HEAD), 1e-06, x.dtype)

            def step(carry, inp):
                mem, z = carry
                q_s, k_s, v_s, qn_s, kn_s = inp
                scores = jnp.einsum('bhnd,bhmd->bhnm', q_s, k_s) * SCALE
                scores = jnp.where(mask, scores, -jnp.inf)
                sdpa = jnp.einsum('bhnm,bhmd->bhnd', jax.nn.softmax(scores, axis=-1), v_s)
                sq = elu1(qn_s)
                num = jnp.einsum('bhnk,bhkv->bhnv', sq, mem)
                den = jnp.einsum('bhnk,bhk->bhn', sq, z)[..., None]
                mem_out = num / (den + 1e-06)
                out = beta * mem_out + (1.0 - beta) * sdpa
                sk = elu1(kn_s)
                prev_v = jnp.einsum('bhnk,bhkv->bhnv', sk, mem) / jnp.einsum('bhnk,bhk->bhn', sk, z)[..., None]
                mem = mem + jnp.einsum('bhnk,bhnv->bhkv', sk, v_s - prev_v)
                z = z + sk.sum(axis=2)
                return ((mem, z), out)
            _, outs = jax.lax.scan(step, (mem0, z0), (qs, ks, vs, qnope, knope))
            o = outs.transpose(1, 0, 3, 2, 4).reshape(B, N, INNER)
            out = o @ w_out
            return (out, next_k, next_v)
        return _reference_tuple_inner(x, w_qkv, w_out, ln_g, ln_b, mem_beta)[0]

    def _L0_attn_b_ref(x, w_qkv, w_proj, b_proj):
        import jax, jax.numpy as jnp
        import numpy as np
        MAX_WAVELENGTH = 10000.0
        NEG_INF = -1000000000.0

        def apply_rope(x):
            S, D = (x.shape[1], x.shape[-1])
            inv_freq = 1.0 / MAX_WAVELENGTH ** (jnp.arange(0, D, 2, dtype=jnp.float32) / D)
            t = jnp.arange(S, dtype=jnp.float32)[:, None] * inv_freq[None, :]
            emb = jnp.concatenate([t, t], axis=-1)
            cos = jnp.cos(emb)[None, :, None, :].astype(x.dtype)
            sin = jnp.sin(emb)[None, :, None, :].astype(x.dtype)
            x1, x2 = jnp.split(x, 2, axis=-1)
            rotated = jnp.concatenate([-x2, x1], axis=-1)
            return x * cos + rotated * sin
        B, S, dim = x.shape
        heads = 16
        head_dim = dim // heads
        scale = head_dim ** (-0.5)
        qkv = x @ w_qkv
        qkv = qkv.reshape(B, S, 3, heads, head_dim)
        Q, K, V = (qkv[:, :, 0], qkv[:, :, 1], qkv[:, :, 2])
        Q = apply_rope(Q)
        K = apply_rope(K)
        attn = jnp.einsum('bqhd,bkhd->bhqk', Q, K) * scale
        causal = jnp.tril(jnp.ones((S, S), dtype=bool))[None, None]
        attn = jnp.where(causal, attn, jnp.asarray(NEG_INF, attn.dtype))
        attn = jax.nn.softmax(attn, axis=-1)
        out = jnp.einsum('bhqk,bkhd->bqhd', attn, V).reshape(B, S, dim)
        return out @ w_proj + b_proj

    def _L0_ffn_ref(x, ln_g, ln_b, attn_w, attn_b, gate_w, w1, b1, w2, b2, next_w, next_b):
        import jax, jax.numpy as jnp
        import numpy as np
        MICRO_BATCHES = 2
        TOP_K = 2
        LN_EPS = 1e-05
        B, S, D = (4, 512, 128)
        E = 8
        DFF = 4 * D

        def _layernorm(x, g, b):
            mu = jnp.mean(x, axis=-1, keepdims=True)
            var = jnp.mean(jnp.square(x - mu), axis=-1, keepdims=True)
            return (x - mu) * jax.lax.rsqrt(var + LN_EPS) * g + b
        Bx, Sx, Dx = x.shape
        N = Bx * Sx
        x_flat = x.reshape(N, Dx)
        x_attn = _layernorm(x_flat, ln_g, ln_b) @ attn_w + attn_b + x_flat
        logits = x_attn @ gate_w
        _ = jax.lax.top_k(logits, TOP_K)
        tpe = N // (MICRO_BATCHES * E)
        g = x_attn.reshape(MICRO_BATCHES, E, tpe, Dx)
        h = jax.nn.gelu(jnp.einsum('metd,edf->metf', g, w1) + b1[None, :, None, :], approximate=False)
        y = jnp.einsum('metf,efd->metd', h, w2) + b2[None, :, None, :]
        out = jax.nn.gelu(y @ next_w + next_b, approximate=False)
        return out.reshape(Bx, Sx, Dx)
    x = L0_attn_a_x
    x = x + _L0_attn_a_ref(_layernorm(x, axis=-1), L0_attn_a_w_qkv, L0_attn_a_w_out, L0_attn_a_ln_g, L0_attn_a_ln_b, L0_attn_a_mem_beta)
    x = x + _L0_ffn_ref(_layernorm(x, axis=-1), L0_ffn_ln_g, L0_ffn_ln_b, L0_ffn_attn_w, L0_ffn_attn_b, L0_ffn_gate_w, L0_ffn_w1, L0_ffn_b1, L0_ffn_w2, L0_ffn_b2, L0_ffn_next_w, L0_ffn_next_b)
    x = x + _L0_attn_b_ref(_layernorm(x, axis=-1), L0_attn_b_w_qkv, L0_attn_b_w_proj, L0_attn_b_b_proj)
    x = x + _L0_ffn_ref(_layernorm(x, axis=-1), L0_ffn_ln_g, L0_ffn_ln_b, L0_ffn_attn_w, L0_ffn_attn_b, L0_ffn_gate_w, L0_ffn_w1, L0_ffn_b1, L0_ffn_w2, L0_ffn_b2, L0_ffn_next_w, L0_ffn_next_b)
    return x

_drawn_inputs = setup_inputs


def setup_inputs(seed=0):
    import zlib

    import numpy as np

    out = dict(_drawn_inputs(seed))
    spreads = {'L0_attn_a_ln_g': (1.0, 0.6),
     'L0_attn_a_ln_b': (0.0, 0.711),
     'L0_attn_a_mem_beta': (0.0, 0.8),
     'L0_attn_b_b_proj': (0.0, 0.1),
     'L0_ffn_ln_g': (1.0, 0.2),
     'L0_ffn_ln_b': (0.0, 0.1),
     'L0_ffn_attn_b': (0.0, 0.1),
     'L0_ffn_b1': (0.0, 0.1),
     'L0_ffn_b2': (0.0, 0.1),
     'L0_ffn_next_b': (0.0, 0.1)}
    factors = {}
    for name, (base, spread) in spreads.items():
        noise = np.random.default_rng([zlib.crc32(name.encode()), seed]).standard_normal(out[name].shape)
        drawn = base * np.exp(spread * noise) if base else spread * noise
        out[name] = jnp.asarray(drawn.astype(out[name].dtype))
    for name, factor in factors.items():
        out[name] = (out[name] * factor).astype(out[name].dtype)
    return out
```

```python
from contextlib import ExitStack

import concourse.bass as bass
import numpy as np
from concourse import mybir

F32 = mybir.dt.float32
BF16 = mybir.dt.bfloat16
ALU = mybir.AluOpType
ACT = mybir.ActivationFunctionType
AX = mybir.AxisListType

P = 128
B, N, D = 16, 512, 128
EPS = 1e-5

HA, DA, SEG = 16, 64, 32
NSEG = N // SEG
BG = P // SEG
NG = B // BG
NT = NG * NSEG
HP = HA // 2
INNER = HA * DA
MC = DA + 1


def attn_a_layer(nc, x, w_qkv, w_out, ln_g, ln_b, mem_beta, rope_cos, rope_sin, seg_mask, ident, x1):
    ctx = ExitStack()
    with ctx:
        def sb(name, shape, dt=F32):
            return ctx.enter_context(nc.sbuf_tensor(name, shape, dt))

        def sem(name):
            return ctx.enter_context(nc.semaphore(name))

        xres = sb("a_xres", [P, NT, D])
        stats = sb("a_stats", [P, NT, 6])
        mv = sb("a_mv", [P, NT, 2])
        rs = sb("a_rs", [P, NT])
        tmp = sb("a_tmp", [P, 4, NT])
        half = sb("a_half", [P, NT])
        wq = sb("a_wqkv", [P, 3 * INNER])
        wo = sb("a_wout", [P, HP, D])
        gcol = sb("a_gcol", [P, 1])
        bcol = sb("a_bcol", [P, 1])
        beta = sb("a_beta", [P, HA])
        ombeta = sb("a_ombeta", [P, HA])
        bexp = sb("a_bexp", [P, HA])
        cosb = sb("a_cos", [P, NSEG, DA])
        sinb = sb("a_sin", [P, NSEG, DA])
        idf = sb("a_idf", [P, P])
        idb = sb("a_idb", [P, P], BF16)
        maskf = sb("a_maskf", [P, HP * SEG])
        maskb = sb("a_maskb", [P, HP * SEG], BF16)
        xhat = sb("a_xhat", [P, D])
        xnT = sb("a_xnT", [P, P])
        rc = sb("a_rc", [P, 2, INNER])
        rn = sb("a_rn", [P, 2, INNER])
        ex = sb("a_ex", [P, 2, INNER])
        sq = ex[:, 0, :]
        sk = sb("a_sk", [P, 2, INNER])
        v = sb("a_v", [P, 2, INNER])
        ropeT = sb("a_ropeT", [P, 2, HP, P])
        sT = sb("a_sT", [P, 2, 2, HP, P])
        ssub = sb("a_ssub", [P, HA, SEG])
        pe_ = sb("a_pe", [P, HA, SEG])
        pn = sb("a_pn", [P, HA * SEG])
        pT = sb("a_pT", [P, 2, HA * SEG])
        mx = sb("a_mx", [P, HA])
        psum_ = sb("a_psum", [P, HA])
        pr = sb("a_pr", [P, HA])
        prs = sb("a_prs", [P, HA])
        mem = sb("a_mem", [P, NG, HP, BG, MC])
        ubd = sb("a_ubd", [P, BG, HA, MC])
        rdk = sb("a_rdk", [P, HA])
        dq = sb("a_dq", [P, 3, HA])
        pv_ = sb("a_prevv", [P, INNER])
        on = sb("a_on", [P, INNER])
        o = sb("a_o", [P, INNER])
        oT = sb("a_oT", [P, HP, P])
        y = sb("a_y", [P, 2, D])
        ps = ctx.enter_context(nc.psum_tensor("a_ps", [P, 8, 512], F32))

        s_const, s_x = sem("a_const"), sem("a_x")
        s_stats, s_mv, s_rs, s_beta, s_set = sem("a_stats_s"), sem("a_mv_s"), sem("a_rs_s"), sem("a_beta_s"), sem("a_set")
        s_xhat, s_xT, s_xnT = sem("a_xhat_s"), sem("a_xT_s"), sem("a_xnT_s")
        s_q, s_k, s_v, s_vc = sem("a_q_s"), sem("a_k_s"), sem("a_v_s"), sem("a_vc_s")
        s_rq, s_rk = sem("a_rq_s"), sem("a_rk_s")
        s_qr, s_kr = sem("a_qr_s"), sem("a_kr_s")
        s_relu = sem("a_relu_s")
        s_exq, s_exk, s_sq, s_sk = sem("a_exq_s"), sem("a_exk_s"), sem("a_sq_s"), sem("a_sk_s")
        s_tqr, s_tkr, s_tsq, s_tsk = sem("a_tqr_s"), sem("a_tkr_s"), sem("a_tsq_s"), sem("a_tsk_s")
        s_qrT, s_krT, s_sqT, s_skT = sem("a_qrT_s"), sem("a_krT_s"), sem("a_sqT_s"), sem("a_skT_s")
        s_S, s_mx, s_sub, s_pe, s_sum, s_prs, s_pn, s_pT = (sem(f"a_{n}_s") for n in ("S", "mx", "sub", "pe", "sum", "prs", "pn", "pT"))
        s_prev, s_rdk, s_tk, s_u, s_ubd = (sem(f"a_{n}_s") for n in ("prev", "rdk", "tk", "u", "ubd"))
        s_num, s_dq, s_on, s_pv, s_o = (sem(f"a_{n}_s") for n in ("num", "dq", "on", "pv", "o"))
        s_dm, s_mem = sem("a_dm_s"), sem("a_mem_s")
        s_oTp, s_oT, s_y, s_x1, s_st = (sem(f"a_{n}_s") for n in ("oTp", "oT", "y", "x1", "st"))

        def heads(ap):
            return ap.rearrange("p (h d) -> p h d", h=HA)

        def pair(ap, hp):
            return ap[:, hp * P:(hp + 1) * P]

        def of_parity(ap, a):
            return ap.rearrange("p (h a d) -> p a h d", h=HP, a=2)[:, a]

        def wide(b0):
            return ps[:, b0:b0 + 2, :].rearrange("p b c -> p (b c)")

        def mem_read(b0):
            return ps[:, b0:b0 + 4, 0:4 * MC].rearrange("p b (c m) -> p b c m", m=MC)

        def read_by(b0, scale, out):
            R = mem_read(b0)
            for a in range(2):
                last = nc.vector.tensor_tensor(of_parity(out, a).rearrange("p (b c) m -> p b c m", b=2), R[:, 2 * a:2 * a + 2, :, 0:DA],
                                               scale[:, a * HP:(a + 1) * HP].rearrange("p (b c) -> p b c", b=2).unsqueeze(3)
                                               .broadcast_to([P, 2, 4, DA]), ALU.mult)
            return last

        def by_head(ap, n):
            return ap.unsqueeze(2).broadcast_to([P, HA, n])

        block = ctx.enter_context(nc.Block())

        def run(both, stage_a, stage_b, eng):
            stage_a(0, 0, 0)
            with eng.Fori(0, NSEG - 1) as s:
                for g in range(NG):
                    t = s * NG + g
                    both(t, g, t + 1, (g + 1) % NG, s if g + 1 < NG else s + 1, True)
            for g in range(NG - 1):
                t = (NSEG - 1) * NG + g
                both(t, g, t + 1, g + 1, NSEG - 1, t + 2 < NT)
            stage_b(NT - 1, NG - 1)

        @block.sync
        def _(sp):
            for g in range(NG):
                for b in range(BG):
                    sp.dma_start(xres[SEG * b:SEG * (b + 1), :, :].rearrange("p (s g) d -> p s g d", g=NG)[:, :, g, :],
                                 x[g * BG + b].rearrange("(s n) d -> n s d", n=SEG)).then_inc(s_x, 16)
            sp.dma_start(wq[:], w_qkv).then_inc(s_const, 16)
            sp.dma_start(wo[:], w_out.rearrange("(h p) d -> p h d", p=P)).then_inc(s_const, 16)
            sp.dma_start(gcol[:], ln_g.rearrange("(p a) -> p a", a=1)).then_inc(s_const, 16)
            sp.dma_start(bcol[:], ln_b.rearrange("(p a) -> p a", a=1)).then_inc(s_const, 16)
            sp.dma_start(beta[:], mem_beta.rearrange("a h b c -> (a b c) h").broadcast_to([P, HA])).then_inc(s_const, 16)
            sp.dma_start(idf[:], ident).then_inc(s_const, 16)
            sp.dma_start(maskf[:], seg_mask).then_inc(s_const, 16)
            for b in range(2):
                sp.dma_start((cosb, sinb)[b][:], (rope_cos, rope_sin)[b]).then_inc(s_const, 16)

            def store(t, g, s):
                sp.wait_ge(s_x1, t + 2)
                for b in range(BG):
                    sp.dma_start(x1[g * BG + b, bass.ds(s * SEG, SEG), :],
                                 xres[SEG * b:SEG * (b + 1), t, :]).then_inc(s_st, 16)

            with sp.Fori(0, NSEG) as s:
                for g in range(NG):
                    store(s * NG + g, g, s)
            sp.wait_ge(s_st, 16 * BG * NT)

        CONST_ALL = 16 * 9

        @block.vector
        def _(dve):
            dve.wait_ge(s_const, CONST_ALL)
            nc.vector.tensor_copy(idb[:], idf[:]).then_inc(s_set, 1)
            nc.vector.tensor_copy(maskb[:], maskf[:]).then_inc(s_set, 1)
            nc.vector.memset(mem[:], 0.0).then_inc(s_set, 1)
            nc.vector.memset(ubd[:], 0.0).then_inc(s_set, 1)
            nc.vector.memset(half[:], -0.5).then_inc(s_set, 1)
            dve.wait_ge(s_set, 5)
            nc.vector.memset(mx[:], 0.0).then_inc(s_x1, 1)
            nc.vector.memset(mem[:, :, :, :, DA:MC].rearrange("p g h b m -> p (g h b) m"), 1e-6).then_inc(s_set, 1)
            for b in range(BG):
                nc.vector.memset(ubd[SEG * b:SEG * (b + 1), b, :, DA:MC], 1.0).then_inc(s_set, 1)
            dve.wait_ge(s_beta, 1)
            nc.vector.tensor_scalar(bexp[:], bexp[:], 1.0, None, ALU.add).then_inc(s_beta, 1)
            dve.wait_ge(s_beta, 2)
            nc.vector.reciprocal(beta[:], bexp[:]).then_inc(s_beta, 1)
            dve.wait_ge(s_beta, 3)
            nc.vector.tensor_scalar(ombeta[:], beta[:], -1.0, 1.0, ALU.mult, ALU.add).then_inc(s_beta, 1)
            dve.wait_ge(s_beta, 4)
            dve.wait_ge(s_x, 16 * B)
            for t in range(NT):
                last = nc.vector.bn_stats(stats[:, t, :], xres[:, t, :])
            last.then_inc(s_stats, 1)
            dve.wait_ge(s_stats, 1)
            for t in range(NT):
                last = nc.vector.bn_aggr(mv[:, t, :], stats[:, t, :])
            last.then_inc(s_mv, 1)
            dve.wait_ge(s_rs, 7)

            def make_xhat(t):
                nc.vector.tensor_scalar(xhat[:], xres[:, t, :], mv[:, t, 0:1], rs[:, bass.ds(t, 1)],
                                        ALU.subtract, ALU.mult).then_inc(s_xhat, 1)

            def rope_products(i, s, t):
                src = wide(2 * i)
                cos, sin = cosb[:, s, :], sinb[:, s, :]
                dve.wait_ge(s_relu, t * 2 + (i + 1))
                nc.vector.tensor_tensor(heads(rc[:, i, :]), heads(src), cos.unsqueeze(1).broadcast_to([P, HA, DA]), ALU.mult)
                for e in range(2):
                    def every(ap, k):
                        return ap.rearrange("p (h d e) -> p h d e", h=HA, e=2)[:, :, :, k]
                    sn = sin.rearrange("p (d e) -> p d e", e=2)[:, :, e].unsqueeze(1).broadcast_to([P, HA, DA // 2])
                    last = nc.vector.tensor_tensor(every(rn[:, i, :], e), every(src, 1 - e), sn, ALU.mult)
                last.then_inc((s_rq, s_rk)[i], 1)

            def elu(i, t, par):
                dve.wait_ge((s_exq, s_exk)[i], t + 1)
                nc.vector.scalar_tensor_tensor(sk[:, par, :] if i else sq, wide(2 * i), 0.0, ex[:, i, :],
                                               ALU.max, ALU.add).then_inc((s_sq, s_sk)[i], 1)

            def keep_kT(t, par):
                dve.wait_ge(s_tkr, t + 1)
                nc.vector.tensor_copy(ropeT[:, 1].rearrange("p h c -> p (h c)"), wide(2)).then_inc(s_krT, 1)
                dve.wait_ge(s_tsk, t + 1)
                nc.vector.tensor_copy(sT[:, par, 1].rearrange("p h c -> p (h c)"), wide(2)).then_inc(s_skT, 1)

            def softmax_head(t):
                S = ps[:, 0:2, 0:HP * SEG].rearrange("p b (h m) -> p b h m", m=SEG)
                mxb = mx[:].rearrange("p (b h) -> p b h", b=2)
                dve.wait_ge(s_S, t + 1)
                nc.vector.tensor_reduce(mxb, S, AX.X, ALU.max).then_inc(s_mx, 1)
                dve.wait_ge(s_mx, t + 1)
                nc.vector.tensor_tensor(ssub[:].rearrange("p (b h) m -> p b h m", b=2), S,
                                        mxb.unsqueeze(3).broadcast_to([P, 2, HP, SEG]), ALU.subtract).then_inc(s_sub, 1)

            def softmax_tail(t, par):
                dve.wait_ge(s_pe, t + 1)
                nc.vector.tensor_reduce(psum_[:], pe_[:], AX.X, ALU.add).then_inc(s_sum, 1)
                dve.wait_ge(s_sum, t * 2 + 1)
                nc.vector.reciprocal(pr[:], psum_[:]).then_inc(s_sum, 1)
                dve.wait_ge(s_sum, t * 2 + 2)
                nc.vector.tensor_tensor(prs[:], pr[:], ombeta[:], ALU.mult).then_inc(s_prs, 1)
                dve.wait_ge(s_pn, t + 1)
                nc.vector.transpose(pT[:, par, :], pn[:]).then_inc(s_pT, 1)

            def read_prev(t):
                R = mem_read(0)
                dve.wait_ge(s_prev, t + 1)
                nc.vector.reciprocal(rdk[:].rearrange("p (b c) -> p b c", b=4), R[:, :, :, DA]).then_inc(s_rdk, 1)
                dve.wait_ge(s_rdk, t + 1)
                read_by(0, rdk[:], pv_[:]).then_inc(s_tk, 1)

            def read_num(t):
                R = mem_read(4)
                dve.wait_ge(s_num, t + 1)
                nc.vector.tensor_scalar(dq[:, 0, :].rearrange("p (b c) -> p b c", b=4), R[:, :, :, DA], 1e-6, None,
                                        ALU.add).then_inc(s_dq, 1)
                dve.wait_ge(s_dq, t * 3 + 1)
                nc.vector.reciprocal(dq[:, 1, :], dq[:, 0, :]).then_inc(s_dq, 1)
                dve.wait_ge(s_dq, t * 3 + 2)
                nc.vector.tensor_tensor(dq[:, 2, :], dq[:, 1, :], beta[:], ALU.mult).then_inc(s_dq, 1)
                dve.wait_ge(s_dq, t * 3 + 3)
                read_by(4, dq[:, 2, :], on[:]).then_inc(s_on, 1)

            def make_o(t):
                dve.wait_ge(s_pv, t + 1)
                dve.wait_ge(s_on, t + 1)
                nc.vector.tensor_tensor(o[:], wide(4), on[:], ALU.add).then_inc(s_o, 1)

            def add_mem(t, g, half_):
                for hp in range(4 * half_, 4 * half_ + 4):
                    dve.wait_ge(s_dm, t * HP + (hp + 1))
                    m = mem[:, g, hp, :, :].rearrange("p b m -> p (b m)")
                    nc.vector.tensor_tensor(m, ps[:, 4 + hp % 4, 0:BG * MC], m, ALU.add).then_inc(s_mem, 1)

            def add_x(t):
                dve.wait_ge(s_y, t + 1)
                nc.vector.tensor_tensor(xres[:, t, :], ps[:, 6, 0:D], xres[:, t, :], ALU.add).then_inc(s_x1, 1)

            def stage_a(t, g, s):
                make_xhat(t)
                rope_products(0, s, t)
                elu(0, t, g % 2)
                rope_products(1, s, t)
                elu(1, t, g % 2)
                make_xhat(t + 1)
                keep_kT(t, g % 2)
                softmax_head(t)
                softmax_tail(t, g % 2)

            def stage_b(t, g):
                read_num(t)
                read_prev(t)
                make_o(t)
                add_mem(t, g, 0)
                add_mem(t, g, 1)
                add_x(t)

            def both(t, g, tn, gn, sn, ahead):
                read_num(t)
                read_prev(t)
                if ahead:
                    make_xhat(tn + 1)
                make_o(t)
                rope_products(0, sn, tn)
                elu(0, tn, gn % 2)
                rope_products(1, sn, tn)
                add_mem(t, g, 0)
                elu(1, tn, gn % 2)
                add_mem(t, g, 1)
                keep_kT(tn, gn % 2)
                softmax_head(tn)
                add_x(t)
                softmax_tail(tn, gn % 2)

            run(both, stage_a, stage_b, dve)

        @block.gpsimd
        def _(pool):
            pool.wait_ge(s_set, 5)
            pool.wait_ge(s_mv, 1)
            var = mv[:, :, 1]
            nc.gpsimd.tensor_scalar(tmp[:, 0, :], var, EPS, None, ALU.add).then_inc(s_rs, 1)
            pool.wait_ge(s_rs, 1)
            nc.gpsimd.tensor_tensor(tmp[:, 1, :], tmp[:, 0, :], half[:], ALU.pow).then_inc(s_rs, 1)
            pool.wait_ge(s_rs, 2)
            nc.gpsimd.tensor_tensor(tmp[:, 2, :], tmp[:, 1, :], tmp[:, 1, :], ALU.mult).then_inc(s_rs, 1)
            pool.wait_ge(s_rs, 3)
            nc.gpsimd.tensor_tensor(tmp[:, 3, :], tmp[:, 2, :], var, ALU.mult).then_inc(s_rs, 1)
            pool.wait_ge(s_rs, 4)
            nc.gpsimd.tensor_scalar(tmp[:, 0, :], tmp[:, 3, :], EPS, None, ALU.add).then_inc(s_rs, 1)
            pool.wait_ge(s_rs, 5)
            nc.gpsimd.tensor_tensor(tmp[:, 2, :], tmp[:, 0, :], half[:], ALU.pow).then_inc(s_rs, 1)
            pool.wait_ge(s_rs, 6)
            nc.gpsimd.tensor_tensor(rs[:], tmp[:, 1, :], tmp[:, 2, :], ALU.mult).then_inc(s_rs, 1)

            def rope_sum(i, t):
                pool.wait_ge((s_rq, s_rk)[i], t + 1)
                nc.gpsimd.tensor_tensor(rc[:, i, :], rc[:, i, :], rn[:, i, :], ALU.add).then_inc((s_qr, s_kr)[i], 1)

            def scale_p(t):
                pool.wait_ge(s_prs, t + 1)
                nc.gpsimd.tensor_tensor(pn[:].rearrange("p (h m) -> p h m", h=HA), pe_[:], by_head(prs[:], SEG),
                                        ALU.mult).then_inc(s_pn, 1)

            def make_u(t, g):
                pool.wait_ge(s_tk, t + 1)
                pool.wait_ge(s_vc, t + 1)
                nc.gpsimd.tensor_tensor(pv_[:], v[:, g % 2, :], pv_[:], ALU.subtract).then_inc(s_u, 1)

            def stage_a(t, g, s):
                rope_sum(0, t)
                rope_sum(1, t)
                scale_p(t)

            def stage_b(t, g):
                make_u(t, g)

            def both(t, g, tn, gn, sn, ahead):
                stage_b(t, g)
                stage_a(tn, gn, sn)

            run(both, stage_a, stage_b, pool)

        @block.scalar
        def _(act):
            act.wait_ge(s_const, CONST_ALL)
            nc.scalar.activation(bexp[:].rearrange("p (a h) -> p a h", a=2), beta[:].rearrange("p (h a) -> p a h", a=2),
                                 ACT.Exp, scale=-1.0).then_inc(s_beta, 1)

            def keep_xnT(t):
                act.wait_ge(s_xT, t + 1)
                nc.scalar.activation(xnT[:], ps[:, 7, 384:512], ACT.Identity, bias=bcol[:], scale=gcol[:]).then_inc(s_xnT, 1)

            def negative_exp(t):
                for i in range(2):
                    act.wait_ge((s_q, s_k)[i], t + 1)
                    nc.scalar.activation(ex[:, i, :], wide(2 * i), ACT.Relu, scale=-1.0).then_inc(s_relu, 1)
                    act.wait_ge(s_relu, t * 2 + (i + 1))
                    nc.scalar.activation(ex[:, i, :], ex[:, i, :], ACT.Exp, scale=-1.0).then_inc((s_exq, s_exk)[i], 1)

            def keep_v(t, par):
                act.wait_ge(s_v, t + 1)
                nc.scalar.activation(v[:, par, :], wide(6), ACT.Copy).then_inc(s_vc, 1)

            def keep_qT(t, par, before=None):
                act.wait_ge(s_tqr, t + 1)
                nc.scalar.activation(ropeT[:, 0].rearrange("p h c -> p (h c)"), wide(0), ACT.Copy).then_inc(s_qrT, 1)
                act.wait_ge(s_tsq, t + 1)
                nc.scalar.activation(sT[:, par, 0].rearrange("p h c -> p (h c)"), wide(0), ACT.Copy).then_inc(s_sqT, 1)
                if before is not None:
                    keep_oT(before)

            def exp(t):
                act.wait_ge(s_sub, t + 1)
                nc.scalar.activation(pe_[:], ssub[:], ACT.Exp, scale=float(DA) ** -0.5).then_inc(s_pe, 1)

            def spread_u(t):
                act.wait_ge(s_u, t + 1)
                for b in range(BG):
                    rows = slice(SEG * b, SEG * (b + 1))
                    last = nc.scalar.activation(ubd[rows, b, :, 0:DA], heads(pv_[rows, :]), ACT.Copy)
                last.then_inc(s_ubd, 1)

            def keep_oT(t):
                act.wait_ge(s_oTp, t + 1)
                nc.scalar.activation(oT[:].rearrange("p h c -> p (h c)"), wide(4), ACT.Copy).then_inc(s_oT, 1)

            def stage_a(t, g, s):
                keep_xnT(t)
                negative_exp(t)
                keep_v(t, g % 2)
                keep_qT(t, g % 2)
                exp(t)
                keep_xnT(t + 1)

            def stage_b(t, g):
                spread_u(t)
                keep_oT(t)

            def both(t, g, tn, gn, sn, ahead):
                spread_u(t)
                negative_exp(tn)
                keep_v(tn, gn % 2)
                keep_qT(tn, gn % 2, t)
                exp(tn)
                if ahead:
                    keep_xnT(tn + 1)

            run(both, stage_a, stage_b, act)

        @block.tensor
        def _(pe):
            pe.wait_ge(s_const, CONST_ALL)
            pe.wait_ge(s_set, 2)

            def transposes(src, b0, sem_):
                for hp in range(HP):
                    last = nc.tensor.transpose(ps[:, b0 + hp // 4, P * (hp % 4):P * (hp % 4 + 1)], pair(src, hp), idf[:])
                last.then_inc(sem_, 1)

            def transpose_x(t):
                pe.wait_ge(s_xhat, t + 1)
                nc.tensor.transpose(ps[:, 7, 384:512], xhat[:], idf[:]).then_inc(s_xT, 1)

            def project(i, b0, sem_):
                for j in range(2):
                    c = i * INNER + j * 512
                    last = nc.tensor.matmul(ps[:, b0 + j, :], xnT[:], wq[:, c:c + 512], start=True, stop=True)
                last.then_inc(sem_, 1)

            def project_qk(t):
                pe.wait_ge(s_xnT, t + 1)
                project(0, 0, s_q)
                project(1, 2, s_k)

            def project_v(t):
                project(2, 6, s_v)

            def read_memory(i, t, g, b0, sem_):
                for a in range(2):
                    if i == 0 and a == 1:
                        pe.wait_ge(s_x1, t + 1)
                        pe.wait_ge(s_xnT, (t + 1 if not isinstance(t, int) else min(t + 1, NT - 1)) + 1)
                    pe.nop(nofuse=True)
                    rows = slice(DA * a, DA * (a + 1))
                    for hp in range(HP):
                        for b in range(BG):
                            last = nc.tensor.matmul(ps[SEG * b:SEG * (b + 1), b0 + 2 * a + hp // 4, (hp % 4) * MC:(hp % 4 + 1) * MC],
                                                    sT[rows, g % 2, i, hp, SEG * b:SEG * (b + 1)], mem[rows, g, hp, b, :],
                                                    start=(hp % 4 == 0), stop=True, skip_group_check=True)
                last.then_inc(sem_, 1)

            def probs_v(t, g):
                pe.wait_ge(s_on, t + 1)
                pe.wait_ge(s_pT, t + 1)
                pe.wait_ge(s_vc, t + 1)
                pe.nop(nofuse=True)
                for h in range(HA):
                    for b in range(BG):
                        rows = slice(SEG * b, SEG * (b + 1))
                        last = nc.tensor.matmul(ps[rows, 4 + h // HP, (h % HP) * DA:(h % HP + 1) * DA],
                                                pT[rows, g % 2, bass.ts(h % 2 * HP + h // 2, SEG)], v[rows, g % 2, h * DA:(h + 1) * DA],
                                                start=(h % HP == 0), stop=True, skip_group_check=True)
                last.then_inc(s_pv, 1)

            def update(t, g, half_, tv=None):
                if half_ == 0:
                    pe.wait_ge(s_ubd, t + 1)
                    pe.wait_ge(s_o, t + 1)
                for hp in range(4 * half_, 4 * half_ + 4):
                    if half_ == 0 and hp == 2 and tv is not None:
                        pe.wait_ge(s_vc, tv + 1)
                    if half_:
                        pe.wait_ge(s_mem, t * HP + (hp - 3))
                    for a in range(2):
                        h = 2 * hp + a
                        last = nc.tensor.matmul(ps[DA * a:DA * (a + 1), 4 + hp % 4, 0:BG * MC], sk[:, g % 2, h * DA:(h + 1) * DA],
                                                ubd[:, :, h, :], start=True, stop=True)
                    last.then_inc(s_dm, 1)

            def transpose_rope(i, t):
                pe.wait_ge((s_sq, s_sk)[i], t + 1)
                pe.wait_ge((s_qr, s_kr)[i], t + 1)
                transposes(rc[:, i, :], 2 * i, (s_tqr, s_tkr)[i])

            def transpose_elu(i, t, g):
                pe.wait_ge((s_qrT, s_krT)[i], t + 1)
                transposes(sk[:, g % 2, :] if i else sq, 2 * i, (s_tsq, s_tsk)[i])

            def scores(t):
                pe.wait_ge(s_sqT, t + 1)
                for a in range(2):
                    nc.tensor.matmul(ps[:, a, 0:HP * SEG], idb[:], maskb[:], start=True, stop=False, skip_group_check=True)
                for a in range(2):
                    rows = slice(DA * a, DA * (a + 1))
                    for hp in range(HP):
                        for b in range(BG):
                            toks = slice(SEG * b, SEG * (b + 1))
                            last = nc.tensor.matmul(ps[toks, a, hp * SEG:(hp + 1) * SEG], ropeT[rows, 0, hp, toks],
                                                    ropeT[rows, 1, hp, toks], start=False, stop=True, skip_group_check=True)
                last.then_inc(s_S, 1)

            def transpose_o(t):
                pe.wait_ge(s_mem, t * HP + HP)
                transposes(o[:], 4, s_oTp)

            def output(t):
                pe.wait_ge(s_oT, t + 1)
                for hp in range(HP):
                    last = nc.tensor.matmul(ps[:, 6, 0:D], oT[:, hp, :], wo[:, hp, :], start=(hp == 0), stop=(hp == HP - 1))
                last.then_inc(s_y, 1)

            def stage_a(t, g, s):
                transpose_x(t)
                project_qk(t)
                project_v(t)
                for i in range(2):
                    transpose_rope(i, t)
                for i in range(2):
                    transpose_elu(i, t, g)
                pe.wait_ge(s_vc, t + 1)
                scores(t)
                transpose_x(t + 1)

            def read(t, g):
                read_memory(0, t, g, 4, s_num)
                pe.wait_ge(s_sub, t + 1)
                pe.wait_ge(s_skT, t + 1)
                read_memory(1, t, g, 0, s_prev)
                probs_v(t, g)

            def stage_b(t, g):
                read(t, g)
                update(t, g, 0)
                update(t, g, 1)
                transpose_o(t)
                output(t)

            def both(t, g, tn, gn, sn, ahead):
                read(t, g)
                pe.wait_ge(s_tk, t + 1)
                project_qk(tn)
                project_v(tn)
                update(t, g, 0, tn)
                transpose_rope(0, tn)
                update(t, g, 1)
                transpose_rope(1, tn)
                transpose_elu(0, tn, gn)
                transpose_o(t)
                transpose_elu(1, tn, gn)
                scores(tn)
                output(t)
                if ahead:
                    transpose_x(tn + 1)

            pe.wait_ge(s_set, 6 + BG)
            run(both, stage_a, stage_b, pe)


NC = N // P
E = 8
DFF = 4 * D
NF = DFF // P
HB, DB = 16, 8
SPLIT = 6
SROW = SPLIT * DB
MROW = 3
HROW = 64
HG = 4
NHG = HB // HG
VC = 32
BANK = 512


def mlp_attn_mlp_layers(nc, x1, w_qkv, w_proj, b_proj, ln_g, ln_b, attn_w, attn_b, w1, b1, w2, b2,
                        next_w, next_b, rope_cos, rope_sin, causal, ident, out):
    ctx = ExitStack()
    with ctx:
        def sb(name, shape, dt=F32):
            return ctx.enter_context(nc.sbuf_tensor(name, shape, dt))

        def sem(name):
            return ctx.enter_context(nc.semaphore("b_" + name))

        X = sb("b_x", [P, B, NC, D])
        wb = sb("b_wqkv", [P, 3 * D])
        wp = sb("b_wproj", [P, D])
        wa = sb("b_attnw", [P, D])
        wn = sb("b_nextw", [P, D])
        bp = sb("b_bproj", [P, D])
        nb = sb("b_nextb", [P, D])
        NVEC = E * NF + E + 3
        vecs = sb("b_vecs", [NVEC, D])
        cols = sb("b_cols", [P, NVEC])
        C_B2, C_G, C_B, C_AB = E * NF, E * NF + E, E * NF + E + 1, E * NF + E + 2
        cosb = sb("b_cos", [P, NC, DB])
        sinb = sb("b_sin", [P, NC, DB])
        idf = sb("b_idf", [P, P])
        idb = sb("b_idb", [P, P], BF16)
        maskf = sb("b_maskf", [P, 2, P])
        maskb = sb("b_maskb", [P, 2, P], BF16)
        half = sb("b_half", [P, NC])
        w1s = sb("b_w1", [P, 2, DFF])
        w2s = sb("b_w2", [P, 2, NF, D])
        fst = sb("b_fst", [P, NC, 6])
        fmv = sb("b_fmv", [P, NC, 2])
        ft = sb("b_ft", [P, 7, NC])
        z = sb("b_z", [P, NC, D])
        xl = sb("b_xl", [P, NC, D])
        xlT = sb("b_xlT", [P, N])
        xaT = sb("b_xaT", [P, N])
        hT = sb("b_hT", [P, NF, N])
        yT = sb("b_yT", [P, N])
        pre = sb("b_pre", [P, NC, D])
        fo = sb("b_fo", [P, NC, D])
        ast = sb("b_ast", [P, NC, 6])
        amv = sb("b_amv", [P, NC, 2])
        at_ = sb("b_at", [P, 2, NC])
        xn = sb("b_xn", [P, NC, D])
        xnT = sb("b_xnT", [P, N])
        qc = sb("b_qc", [P, NC, 2, HB, DB])
        qs = sb("b_qs", [P, NC, 2, HB, DB])
        r1 = sb("b_r1", [P, NC, 2, HB, DB])
        r2 = sb("b_r2", [P, NC, 2, HB, DB])
        st = sb("b_st", [P, NC, 2, HB, HROW], BF16)
        QT = sb("b_QT", [P, HB // 2, N], BF16)
        KT = sb("b_KT", [P, HB // 2, N], BF16)
        va = sb("b_va", [P, NC, HB, VC])
        nm = sb("b_nm", [P, 3, NC, HB])
        PT = sb("b_PT", [P, 2, HG, 1280])
        oTs = sb("b_oTs", [P, NHG, N])
        rec = sb("b_rec", [P, NC, HB])
        o2 = sb("b_o2", [P, NC, D])
        o2T = sb("b_o2T", [P, N])
        ps = ctx.enter_context(nc.psum_tensor("b_ps", [P, 8, BANK], F32))

        s_const, s_x, s_set, s_cT, s_cols = (sem(n) for n in ("const", "x", "set", "cT", "cols"))
        s_w = [sem("w0"), sem("w1")]
        s_fst, s_fmv, s_frs, s_z, s_xl = (sem(n) for n in ("fst", "fmv", "frs", "z", "xl"))
        s_zT, s_xlT, s_xlTc, s_xa, s_xac = (sem(n) for n in ("zT", "xlT", "xlTc", "xa", "xac"))
        s_h, s_hc = sem("h"), sem("hc")
        s_yT, s_yTc, s_fo, s_pre, s_foc, s_fx = (sem(n) for n in ("yT", "yTc", "fo", "pre", "foc", "fx"))
        s_ast, s_amv, s_ars, s_xn, s_xnT, s_xnTc = (sem(n) for n in ("ast", "amv", "ars", "xn", "xnT", "xnTc"))
        s_qkv, s_va, s_rp, s_rs, s_p1, s_r1, s_p2, s_r2, s_p3, s_p3a = (sem(n) for n in ("qkv", "va", "rp", "rs", "p1", "r1", "p2", "r2", "p3", "p3a"))
        s_kT, s_kTc, s_qT, s_qTc = (sem(n) for n in ("kT", "kTc", "qT", "qTc"))
        s_S, s_Sc = sem("S"), sem("Sc")
        s_nm, s_m3 = sem("nm"), sem("m3")
        s_T, s_Tc, s_pv, s_pvc = (sem(n) for n in ("T", "Tc", "pv", "pvc"))
        s_oB, s_rec, s_o2, s_o2T, s_o2Tc, s_y, s_xb, s_x3 = (sem(n) for n in ("oB", "rec", "o2", "o2T", "o2Tc", "y", "xb", "x3"))
        s_out = sem("out")

        MAX_ITEMS = ([(3, h, 1) for h in range(HB)] + [(2, h, 1) for h in range(HB)]
                     + [(1, h, 2) for h in (0, 1, 4, 5, 8, 9, 12, 13)] + [(0, h, 4) for h in (0, 1, 8, 9)])
        NMAX = len(MAX_ITEMS)
        T_ITEMS = (((0, 0, 512),), ((1, 0, 384), (3, 384, 128)), ((2, 0, 256),))
        NTI = len(T_ITEMS)
        PT_AT = (0, 512, 1024)
        KEY_AT = {0: 0, 1: 512, 3: 896, 2: 1024}

        block = ctx.enter_context(nc.Block())

        def batches(eng, mlp, attn):
            mlp(0, 0, 0)
            attn(0)
            mlp(1, 0, 1)
            with eng.Fori(1, B) as i:
                mlp(i * 2, i, 0)
                attn(i)
                mlp(i * 2 + 1, i, 1)

        @block.sync
        def _(sp):
            sp.dma_start(X[:, 0], x1[0].rearrange("(c p) d -> p c d", p=P)).then_inc(s_x, 16)
            for dst, src in ((wb, w_qkv), (wp, w_proj), (wa, attn_w), (wn, next_w), (cosb, rope_cos), (sinb, rope_sin),
                             (idf, ident), (maskf, causal)):
                sp.dma_start(dst[:], src).then_inc(s_const, 16)
            for dst, src in ((bp, b_proj), (nb, next_b)):
                sp.dma_start(dst[:], src.unsqueeze(0).broadcast_to([P, D])).then_inc(s_const, 16)
            sp.dma_start(vecs[0:E * NF, :], b1.rearrange("e (j f) -> (e j) f", f=P)).then_inc(s_const, 16)
            sp.dma_start(vecs[C_B2:C_B2 + E, :], b2).then_inc(s_const, 16)
            for c, src in ((C_G, ln_g), (C_B, ln_b), (C_AB, attn_b)):
                sp.dma_start(vecs[c:c + 1, :], src.unsqueeze(0)).then_inc(s_const, 16)
            sp.dma_start(X[:, 1:B], x1[1:B].rearrange("b (c p) d -> p b c d", p=P)).then_inc(s_x, 16)
            CONST_ALL = 15

            def mlp(n, i, par):
                e = i % E
                if not (isinstance(n, int) and n < 2):
                    sp.wait_ge(s_yT, n - 1)
                sp.dma_start(w1s[:, par, :], w1[e]).then_inc(s_w[par], 16)
                sp.dma_start(w2s[:, par, :, :], w2[e].rearrange("(j f) d -> f j d", f=P)).then_inc(s_w[par], 16)

            def store(n, i, par):
                if par == 1:
                    sp.wait_ge(s_fx, n + 1)
                    sp.dma_start(out[i].rearrange("(c p) d -> p c d", p=P), X[:, i]).then_inc(s_out, 16)

            mlp(0, 0, 0)
            mlp(1, 0, 1)
            with sp.Fori(1, B) as i:
                mlp(i * 2, i, 0)
                store(i * 2 - 1, i - 1, 1)
                mlp(i * 2 + 1, i, 1)
            store(2 * B - 1, B - 1, 1)
            sp.wait_ge(s_out, 16 * B)

        CONSTS = 15 * 16

        def chunks(ap):
            return ap.rearrange("p c d -> p (c d)")

        def tps(half_):
            b0 = (2, 4)[half_]
            return ps[:, b0:b0 + 2, :].rearrange("p b c -> p (b c)").bitcast(BF16).rearrange("p (n c) -> p n c", c=P)

        @block.vector
        def _(dve):
            dve.wait_ge(s_const, CONSTS)
            nc.vector.tensor_copy(idb[:], idf[:]).then_inc(s_set, 1)
            nc.vector.tensor_copy(maskb[:], maskf[:]).then_inc(s_set, 1)
            nc.vector.memset(half[:], -0.5).then_inc(s_set, 1)
            nc.vector.memset(va[:], 0.0).then_inc(s_set, 1)
            nc.vector.memset(st[:], 0.0).then_inc(s_set, 1)
            dve.wait_ge(s_set, 5)
            nc.vector.memset(va[:, :, :, DB:DB + 1].rearrange("p c h v -> p (c h) v"), 1.0).then_inc(s_set, 1)
            for c in range(NC):
                nc.vector.memset(st[:, c, 1, :, SROW:SROW + MROW], 1.0).then_inc(s_set, 1)
            dve.wait_ge(s_cT, 1)
            nc.vector.tensor_copy(cols[:], ps[:, 0, 0:NVEC]).then_inc(s_cols, 1)

            def row_stats(i, stats, mv, s_stats, s_mv, n):
                dve.nop(nofuse=True)
                for c in range(NC):
                    last = nc.vector.bn_stats(stats[:, c, :], X[:, i, c, :])
                last.then_inc(s_stats, 1)
                dve.wait_ge(s_stats, n + 1)
                dve.nop(nofuse=True)
                for c in range(NC):
                    last = nc.vector.bn_aggr(mv[:, c, :], stats[:, c, :])
                last.then_inc(s_mv, 1)

            def mlp(n, i, par):
                if par == 0:
                    if isinstance(n, int):
                        dve.wait_ge(s_x, 16)
                    else:
                        dve.wait_ge(s_x, 32)
                else:
                    dve.wait_ge(s_x3, i + 1)
                row_stats(i, fst, fmv, s_fst, s_fmv, n)
                dve.wait_ge(s_frs, n * 7 + 7)
                for c in range(NC):
                    last = nc.vector.tensor_scalar(z[:, c, :], X[:, i, c, :], fmv[:, c, 0:1], ft[:, 1, c:c + 1],
                                                   ALU.subtract, ALU.mult)
                last.then_inc(s_z, 1)
                for c in range(NC):
                    last = nc.vector.tensor_scalar(xl[:, c, :], X[:, i, c, :], fmv[:, c, 0:1], ft[:, 6, c:c + 1],
                                                   ALU.subtract, ALU.mult)
                last.then_inc(s_xl, 1)
                dve.wait_ge(s_fo, n + 1)
                nc.vector.tensor_tensor(pre[:], ps[:, 0, :].rearrange("p (c d) -> p c d", c=NC),
                                        nb[:].unsqueeze(1).broadcast_to([P, NC, D]), ALU.add).then_inc(s_pre, 1)

            def attn(i):
                dve.wait_ge(s_fx, i * 2 + 1)
                row_stats(i, ast, amv, s_ast, s_amv, i)
                dve.wait_ge(s_ars, i * 2 + 2)
                for c in range(NC):
                    last = nc.vector.tensor_scalar(xn[:, c, :], X[:, i, c, :], amv[:, c, 0:1], at_[:, 1, c:c + 1],
                                                   ALU.subtract, ALU.mult)
                last.then_inc(s_xn, 1)
                dve.wait_ge(s_va, i + 1)
                qk = ps[:, 2:6, 0:2 * D].rearrange("p c (h d) -> p c h d", d=DB)
                flat = lambda ap: ap.rearrange("p c a h d -> p c (a h) d")
                cs = cosb[:].unsqueeze(2).broadcast_to([P, NC, 2 * HB, DB])
                sn = sinb[:].unsqueeze(2).broadcast_to([P, NC, 2 * HB, DB])
                nc.vector.tensor_tensor(flat(qc[:]), qk, cs, ALU.mult)
                for a in range(2):
                    to, of = slice(4 * a, 4 * a + 4), slice(4 - 4 * a, 8 - 4 * a)
                    last = nc.vector.tensor_tensor(flat(qs[:])[:, :, :, to], qk[:, :, :, of], sn[:, :, :, to], ALU.mult)
                last.then_inc(s_rp, 1)
                q = lambda k: st[:, :, 0, :, k * DB:(k + 1) * DB]
                k_ = lambda k: st[:, :, 1, :, k * DB:(k + 1) * DB]
                dve.wait_ge(s_p1, i + 1)
                nc.vector.tensor_copy(q(1), q(0))
                nc.vector.tensor_copy(q(2), q(0))
                nc.vector.tensor_copy(k_(3), k_(0))
                nc.vector.tensor_copy(k_(5), k_(0))
                dve.wait_ge(s_p2, i + 1)
                nc.vector.tensor_copy(q(4), q(3))
                nc.vector.tensor_copy(k_(4), k_(1)).then_inc(s_p3, 1)
                for half_ in range(2):
                    dve.wait_ge(s_kT, i * 2 + (half_ + 1))
                    nc.vector.tensor_copy(KT[:, 4 * half_:4 * half_ + 4, :].rearrange("p h (c k) -> p (h c) k", c=NC),
                                          tps(half_)).then_inc(s_kTc, 1)
                for n_, (c, h, nh) in enumerate(MAX_ITEMS):
                    w = (c + 1) * P
                    dve.wait_ge(s_S, i * NMAX + (n_ + 1))
                    nc.vector.tensor_reduce(nm[:, 0, c, h:h + 2 * nh - 1:2], ps[:, 2 + h % 2, 0:nh * w].rearrange("p (h w) -> p h w", h=nh),
                                            AX.X, ALU.max, negate=True).then_inc(s_Sc, 1)
                dve.wait_ge(s_Sc, i * NMAX + NMAX)
                m = lambda k: st[:, :, 0, :, SROW + k]
                nc.vector.tensor_copy(m(0), nm[:, 0]).then_inc(s_nm, 1)
                dve.wait_ge(s_nm, i * 4 + 1)
                nc.vector.tensor_tensor(nm[:, 1], nm[:, 0], m(0), ALU.subtract).then_inc(s_nm, 1)
                dve.wait_ge(s_nm, i * 4 + 2)
                nc.vector.tensor_copy(m(1), nm[:, 1]).then_inc(s_nm, 1)
                dve.wait_ge(s_nm, i * 4 + 3)
                nc.vector.tensor_tensor(nm[:, 2], nm[:, 1], m(1), ALU.subtract).then_inc(s_nm, 1)
                dve.wait_ge(s_nm, i * 4 + 4)
                nc.vector.tensor_copy(m(2), nm[:, 2]).then_inc(s_m3, 1)
                for G in range(NHG):
                    dve.wait_ge(s_pv, i * NHG + (G + 1))
                    nc.vector.tensor_copy(oTs[:, G, :], ps[:, 6 + G % 2, :]).then_inc(s_pvc, 1)
                dve.wait_ge(s_oB, i + 1)
                O = ps[:, 2:6, :].rearrange("p c (h v) -> p c h v", v=VC)
                nc.vector.reciprocal(rec[:], O[:, :, :, DB]).then_inc(s_rec, 1)
                dve.wait_ge(s_rec, i + 1)
                nc.vector.tensor_tensor(o2[:].rearrange("p c (h v) -> p c h v", h=HB), O[:, :, :, 0:DB],
                                        rec[:].unsqueeze(3).broadcast_to([P, NC, HB, DB]), ALU.mult).then_inc(s_o2, 1)
                dve.wait_ge(s_y, i + 1)
                dve.wait_ge(s_xb, i + 1)
                nc.vector.tensor_tensor(chunks(X[:, i]), ps[:, 7, :], chunks(X[:, i]), ALU.add).then_inc(s_x3, 1)

            batches(dve, mlp, attn)

        @block.gpsimd
        def _(pool):
            pool.wait_ge(s_set, 3)

            def mlp(n, i, par):
                pool.wait_ge(s_fmv, n + 1)
                pool.nop(nofuse=True)
                var = fmv[:, :, 1]
                steps = ((0, var, None), (1, ft[:, 0], half[:]), (2, ft[:, 1], ft[:, 1]), (3, ft[:, 2], var), (4, ft[:, 3], None),
                         (5, ft[:, 4], half[:]), (6, ft[:, 1], ft[:, 5]))
                for k, (to, a, b) in enumerate(steps):
                    if k:
                        pool.wait_ge(s_frs, n * 7 + k)
                        pool.nop(nofuse=True)
                    if b is None:
                        nc.gpsimd.tensor_scalar(ft[:, to], a, EPS, None, ALU.add).then_inc(s_frs, 1)
                    else:
                        nc.gpsimd.tensor_tensor(ft[:, to], a, b, ALU.pow if k in (1, 5) else ALU.mult).then_inc(s_frs, 1)
                pool.wait_ge(s_foc, n + 1)
                pool.nop(nofuse=True)
                nc.gpsimd.tensor_tensor(chunks(X[:, i]), chunks(X[:, i]), chunks(fo[:]), ALU.add).then_inc(s_fx, 1)

            def attn(i):
                pool.wait_ge(s_amv, i + 1)
                pool.nop(nofuse=True)
                nc.gpsimd.tensor_scalar(at_[:, 0], amv[:, :, 1], EPS, None, ALU.add).then_inc(s_ars, 1)
                pool.wait_ge(s_ars, i * 2 + 1)
                nc.gpsimd.tensor_tensor(at_[:, 1], at_[:, 0], half[:], ALU.pow).then_inc(s_ars, 1)
                pool.wait_ge(s_xn, i + 1)
                pool.nop(nofuse=True)
                nc.gpsimd.tensor_tensor(X[:, i], X[:, i], bp[:].unsqueeze(1).broadcast_to([P, NC, D]), ALU.add).then_inc(s_xb, 1)
                pool.wait_ge(s_rp, i + 1)
                all_ = lambda ap: ap.rearrange("p c a h d -> p (c a h d)")
                nc.gpsimd.tensor_tensor(all_(qc[:]), all_(qc[:]), all_(qs[:]), ALU.add).then_inc(s_rs, 1)
                part = lambda k: st[:, :, :, :, k * DB:(k + 1) * DB].rearrange("p c a h d -> p (c a h) d")
                rows = lambda ap: ap.rearrange("p c a h d -> p (c a h) d")
                pool.wait_ge(s_p1, i + 1)
                nc.gpsimd.tensor_tensor(rows(r1[:]), rows(qc[:]), part(0), ALU.subtract).then_inc(s_r1, 1)
                pool.wait_ge(s_p2, i + 1)
                for a, k in ((0, 3), (1, 1)):
                    last = nc.gpsimd.tensor_tensor(r2[:, :, a], r1[:, :, a], st[:, :, a, :, k * DB:(k + 1) * DB], ALU.subtract)
                last.then_inc(s_r2, 1)

            batches(pool, mlp, attn)

        @block.scalar
        def _(act):
            act.wait_ge(s_cols, 1)

            def mlp(n, i, par):
                e = i % E
                act.wait_ge(s_xlT, n + 1)
                nc.scalar.activation(xlT[:], ps[:, 1, :], ACT.Identity, bias=cols[:, C_B:C_B + 1], scale=cols[:, C_G:C_G + 1]).then_inc(s_xlTc, 1)
                act.wait_ge(s_xa, n + 1)
                nc.scalar.activation(xaT[:], ps[:, 0, :], ACT.Identity, bias=cols[:, C_AB:C_AB + 1]).then_inc(s_xac, 1)
                for j in range(NF):
                    act.wait_ge(s_h, n * NF + (j + 1))
                    act.nop(nofuse=True)
                    nc.scalar.activation(hT[:, j, :], ps[:, (j + 1) % 2, :], ACT.Gelu,
                                         bias=cols[:, bass.ds(e * NF + j, 1)]).then_inc(s_hc, 1)
                act.wait_ge(s_yT, n + 1)
                act.nop(nofuse=True)
                nc.scalar.activation(yT[:], ps[:, 1, :], ACT.Identity, bias=cols[:, bass.ds(e + C_B2, 1)]).then_inc(s_yTc, 1)
                act.wait_ge(s_pre, n + 1)
                nc.scalar.activation(fo[:], pre[:], ACT.Gelu).then_inc(s_foc, 1)

            def attn(i):
                act.wait_ge(s_xnT, i + 1)
                nc.scalar.activation(xnT[:], ps[:, 6, :], ACT.Copy).then_inc(s_xnTc, 1)
                act.wait_ge(s_qkv, i + 1)
                nc.scalar.activation(va[:, :, :, 0:DB], ps[:, 2:6, 2 * D:3 * D].rearrange("p c (h d) -> p c h d", d=DB),
                                     ACT.Copy).then_inc(s_va, 1)
                part = lambda a, k: st[:, :, a, :, k * DB:(k + 1) * DB]
                act.wait_ge(s_rs, i + 1)
                for a in range(2):
                    last = nc.scalar.activation(part(a, 0), qc[:, :, a], ACT.Copy)
                last.then_inc(s_p1, 1)
                act.wait_ge(s_r1, i + 1)
                nc.scalar.activation(part(0, 3), r1[:, :, 0], ACT.Copy)
                nc.scalar.activation(part(1, 1), r1[:, :, 1], ACT.Copy).then_inc(s_p2, 1)
                act.wait_ge(s_r2, i + 1)
                nc.scalar.activation(part(0, 5), r2[:, :, 0], ACT.Copy)
                nc.scalar.activation(part(1, 2), r2[:, :, 1], ACT.Copy).then_inc(s_p3a, 1)
                for u in range(2):
                    for half_ in range(2):
                        act.wait_ge(s_qT, i * 4 + (2 * u + half_ + 1))
                        nc.scalar.activation(QT[:, 4 * half_:4 * half_ + 4, :].rearrange("p h (c k) -> p (h c) k", c=NC),
                                             tps(half_), ACT.Copy).then_inc(s_qTc, 1)
                for h in range(HB):
                    for k in range(NTI):
                        w = sum(x[2] for x in T_ITEMS[k])
                        act.wait_ge(s_T, i * (HB * NTI) + (h * NTI + k + 1))
                        nc.scalar.activation(PT[:, h // HG % 2, h % HG, PT_AT[k]:PT_AT[k] + w], ps[:, 2 + (h * NTI + k) % 4, 0:w],
                                             ACT.Exp, scale=float(DB) ** -0.5).then_inc(s_Tc, 1)
                act.wait_ge(s_o2T, i + 1)
                nc.scalar.activation(o2T[:], ps[:, 6, :], ACT.Copy).then_inc(s_o2Tc, 1)

            batches(act, mlp, attn)

        @block.tensor
        def _(pe):
            pe.wait_ge(s_const, CONSTS)
            nc.tensor.transpose(ps[:, 0, 0:NVEC], vecs[:], idf[0:NVEC, 0:NVEC]).then_inc(s_cT, 1)
            pe.wait_ge(s_set, 6 + NC)
            pe.wait_ge(s_cols, 1)

            def cols_of(c):
                return slice(c * P, (c + 1) * P)

            def mlp(n, i, par):
                pe.wait_ge(s_z, n + 1)
                for c in range(NC):
                    last = nc.tensor.matmul(ps[:, 0, cols_of(c)], z[:, c, :], idf[:], start=(c == 0), stop=False,
                                            is_transpose=True, skip_group_check=True)
                pe.wait_ge(s_xl, n + 1)
                for c in range(NC):
                    last = nc.tensor.transpose(ps[:, 1, cols_of(c)], xl[:, c, :], idf[:])
                last.then_inc(s_xlT, 1)
                pe.wait_ge(s_xlTc, n + 1)
                nc.tensor.matmul(ps[:, 0, :], wa[:], xlT[:], start=False, stop=True, skip_group_check=True).then_inc(s_xa, 1)
                pe.wait_ge(s_w[par], weights_in(i, par))
                pe.wait_ge(s_xac, n + 1)
                for j in range(NF):
                    if j >= 2:
                        pe.wait_ge(s_hc, n * NF + (j - 1))
                    nc.tensor.matmul(ps[:, (j + 1) % 2, :], w1s[:, par, cols_of(j)], xaT[:], start=True, stop=True).then_inc(s_h, 1)
                for j in range(NF):
                    pe.wait_ge(s_hc, n * NF + (max(j, 2) + 1))
                    last = nc.tensor.matmul(ps[:, 1, :], w2s[:, par, j, :], hT[:, j, :], start=(j == 0), stop=(j == NF - 1))
                last.then_inc(s_yT, 1)
                pe.wait_ge(s_yTc, n + 1)
                for c in range(NC):
                    last = nc.tensor.matmul(ps[:, 0, cols_of(c)], yT[:, cols_of(c)], wn[:], start=True, stop=True)
                last.then_inc(s_fo, 1)

            def weights_in(i, par):
                return i * 32 + 32

            def attn(i):
                pe.wait_ge(s_xn, i + 1)
                for c in range(NC):
                    last = nc.tensor.transpose(ps[:, 6, cols_of(c)], xn[:, c, :], idf[:])
                last.then_inc(s_xnT, 1)
                pe.wait_ge(s_xnTc, i + 1)
                for c in range(NC):
                    last = nc.tensor.matmul(ps[:, 2 + c, 0:3 * D], xnT[:, cols_of(c)], wb[:], start=True, stop=True)
                last.then_inc(s_qkv, 1)

                def transposed(a, half_, sem_):
                    T = tps(half_)
                    for hh in range(4):
                        hp = 4 * half_ + hh
                        for c in range(NC):
                            last = nc.tensor.transpose(T[:, hh * NC + c, :], st[:, c, a, 2 * hp:2 * hp + 2, :].rearrange("p h r -> p (h r)"), idb[:])
                    last.then_inc(sem_, 1)

                pe.wait_ge(s_p3, i + 1)
                pe.wait_ge(s_p3a, i + 1)
                transposed(1, 0, s_kT)
                transposed(1, 1, s_kT)
                pe.wait_ge(s_kTc, i * 2 + 1)
                transposed(0, 0, s_qT)
                pe.wait_ge(s_kTc, i * 2 + 2)
                transposed(0, 1, s_qT)
                pe.wait_ge(s_qTc, i * 4 + 2)
                for n_, (c, h0, nh) in enumerate(MAX_ITEMS):
                    w = (c + 1) * P
                    a = h0 % 2
                    if n_ >= 2:
                        pe.wait_ge(s_Sc, i * NMAX + (n_ - 1))
                    for k in range(nh):
                        hp = h0 // 2 + k
                        rows = slice(HROW * a, HROW * a + SROW)
                        nc.tensor.matmul(ps[:, 2 + a, k * w:(k + 1) * w], QT[rows, hp, cols_of(c)], KT[rows, hp, 0:w],
                                         start=(k == 0), stop=False, skip_group_check=True)
                    for k in range(nh):
                        last = nc.tensor.matmul(ps[:, 2 + a, k * w + c * P:(k + 1) * w], idb[:], maskb[:, 0, :],
                                                start=False, stop=True, skip_group_check=True)
                    last.then_inc(s_S, 1)
                pe.wait_ge(s_m3, i + 1)
                transposed(0, 0, s_qT)
                transposed(0, 1, s_qT)
                pe.wait_ge(s_qTc, i * 4 + 4)

                def pv(G):
                    if G >= 2:
                        pe.wait_ge(s_pvc, i * NHG + (G - 1))
                    pe.wait_ge(s_Tc, i * (HB * NTI) + (G + 1) * HG * NTI)
                    for j in range(NC):
                        for k in range(HG):
                            last = nc.tensor.matmul(ps[VC * k:VC * (k + 1), 6 + G % 2, j * P:N], va[:, j, G * HG + k, :],
                                                    PT[:, G % 2, k, KEY_AT[j]:KEY_AT[j] + N - j * P], start=(j == 0), stop=(j == NC - 1),
                                                    skip_group_check=True)
                    last.then_inc(s_pv, 1)

                for h in range(HB):
                    rows = slice(HROW * (h % 2), HROW * (h % 2) + SROW + MROW)
                    for k in range(NTI):
                        n_ = h * NTI + k
                        if n_ >= 4:
                            pe.wait_ge(s_Tc, i * (HB * NTI) + (n_ - 3))
                        bank = 2 + n_ % 4
                        for m, (j, at, w) in enumerate(T_ITEMS[k]):
                            nc.tensor.matmul(ps[:, bank, at:at + w], KT[rows, h // 2, cols_of(j)], QT[rows, h // 2, j * P:N],
                                             start=(m == 0), stop=False, skip_group_check=True)
                        for m, (j, at, w) in enumerate(T_ITEMS[k]):
                            last = nc.tensor.matmul(ps[:, bank, at:at + P], idb[:], maskb[:, 1, :],
                                                    start=False, stop=True, skip_group_check=True)
                        last.then_inc(s_T, 1)
                    if h % HG == 1 and h > HG:
                        pv(h // HG - 1)
                pv(NHG - 1)
                pe.wait_ge(s_pvc, i * NHG + NHG)
                for c in range(NC):
                    for G in range(NHG):
                        last = nc.tensor.transpose(ps[:, 2 + c, cols_of(G)], oTs[:, G, cols_of(c)], idf[:])
                last.then_inc(s_oB, 1)
                pe.wait_ge(s_o2, i + 1)
                for c in range(NC):
                    last = nc.tensor.transpose(ps[:, 6, cols_of(c)], o2[:, c, :], idf[:])
                last.then_inc(s_o2T, 1)
                pe.wait_ge(s_o2Tc, i + 1)
                for c in range(NC):
                    last = nc.tensor.matmul(ps[:, 7, cols_of(c)], o2T[:, cols_of(c)], wp[:], start=True, stop=True)
                last.then_inc(s_y, 1)

            batches(pe, mlp, attn)


_INS = ["L0_attn_a_x", "L0_attn_a_w_qkv", "L0_attn_a_w_out", "L0_attn_a_ln_g", "L0_attn_a_ln_b", "L0_attn_a_mem_beta",
        "L0_attn_b_w_qkv", "L0_attn_b_w_proj", "L0_attn_b_b_proj", "L0_ffn_ln_g", "L0_ffn_ln_b", "L0_ffn_attn_w",
        "L0_ffn_attn_b", "L0_ffn_w1", "L0_ffn_b1", "L0_ffn_w2", "L0_ffn_b2", "L0_ffn_next_w", "L0_ffn_next_b"]
MASKED = -1e30


def shape_constants():
    f32 = np.float32
    freq = (f32(10000.0) ** (-np.arange(0, DA, 2, dtype=f32) / f32(DA))).astype(f32)
    angle = np.arange(N, dtype=f32)[:, None] * freq
    cos_a = np.repeat(np.cos(angle), 2, -1)
    sin_a = np.repeat(np.sin(angle), 2, -1) * np.tile(np.array([-1, 1], f32), DA // 2)

    def by_tile(t):
        return np.ascontiguousarray(np.tile(t.reshape(NSEG, SEG, DA).transpose(1, 0, 2), (BG, 1, 1)), dtype=f32)

    seg = np.arange(SEG)
    seg_mask = np.tile(np.where(seg[None] > seg[:, None], f32(MASKED), f32(0)), (BG, HP))
    freq_b = (f32(1.0) / f32(10000.0) ** (np.arange(0, DB, 2, dtype=f32) / f32(DB))).astype(f32)
    angle_b = np.arange(N, dtype=f32)[:, None] * freq_b
    cos_b = np.concatenate([np.cos(angle_b), np.cos(angle_b)], -1)
    sin_b = np.concatenate([-np.sin(angle_b), np.sin(angle_b)], -1)

    def by_chunk(t):
        return np.ascontiguousarray(t.reshape(NC, P, DB).transpose(1, 0, 2), dtype=f32)

    row = np.arange(P)
    causal = np.where(row[None] > row[:, None], f32(MASKED), f32(0))
    return {"rope_cos_a": by_tile(cos_a), "rope_sin_a": by_tile(sin_a), "seg_mask": seg_mask.astype(f32),
            "rope_cos_b": by_chunk(cos_b), "rope_sin_b": by_chunk(sin_b),
            "causal": np.ascontiguousarray(np.stack([causal, causal.T], 1)), "ident": np.eye(P, dtype=f32)}


def kernel(**inputs):
    import concourse.bacc as bacc
    from concourse.bass_utils import run_bass_kernel_spmd

    nc = bacc.Bacc("TRN2", target_bir_lowering=False, num_devices=1)
    arrays, ap = {}, {}
    for name, a in [(n, np.ascontiguousarray(inputs[n])) for n in _INS] + list(shape_constants().items()):
        arrays[f"in_{name}_dram"] = a
        ap[name] = nc.dram_tensor(f"in_{name}_dram", a.shape, mybir.dt.from_np(a.dtype), kind="ExternalInput").ap()
    x1 = nc.dram_tensor("x1_dram", (B, N, D), F32).ap()
    out = nc.dram_tensor("out_0_dram", (B, N, D), F32, kind="ExternalOutput").ap()
    a, b, f = "L0_attn_a_", "L0_attn_b_", "L0_ffn_"
    attn_a_layer(nc, ap[a + "x"], ap[a + "w_qkv"], ap[a + "w_out"], ap[a + "ln_g"], ap[a + "ln_b"], ap[a + "mem_beta"],
                 ap["rope_cos_a"], ap["rope_sin_a"], ap["seg_mask"], ap["ident"], x1)
    mlp_attn_mlp_layers(nc, x1, ap[b + "w_qkv"], ap[b + "w_proj"], ap[b + "b_proj"], ap[f + "ln_g"], ap[f + "ln_b"],
                        ap[f + "attn_w"], ap[f + "attn_b"], ap[f + "w1"], ap[f + "b1"], ap[f + "w2"], ap[f + "b2"],
                        ap[f + "next_w"], ap[f + "next_b"], ap["rope_cos_b"], ap["rope_sin_b"], ap["causal"], ap["ident"], out)
    r = run_bass_kernel_spmd(nc, [arrays], core_ids=[0])
    return r.results[0]["out_0_dram"]
```

```python
from contextlib import ExitStack

import concourse.bass as bass
import numpy as np
from concourse import mybir

F32 = mybir.dt.float32
BF16 = mybir.dt.bfloat16
ALU = mybir.AluOpType
ACT = mybir.ActivationFunctionType
AX = mybir.AxisListType

P = 128
B, N, D = 16, 512, 128
EPS = 1e-5

HA, DA, SEG = 16, 64, 32
NSEG = N // SEG
BG = P // SEG
NG = B // BG
NT = NG * NSEG
HP = HA // 2
INNER = HA * DA
MC = DA + 1


def attn_a_layer(nc, x, w_qkv, w_out, ln_g, ln_b, mem_beta, rope_cos, rope_sin, seg_mask, ident, x1):
    ctx = ExitStack()
    with ctx:
        def sb(name, shape, dt=F32):
            return ctx.enter_context(nc.sbuf_tensor(name, shape, dt))

        def sem(name):
            return ctx.enter_context(nc.semaphore(name))

        xin = sb("a_xin", [P, NG, D])
        xout = sb("a_xout", [P, NG, D])
        stats = sb("a_stats", [P, NG, 6])
        mv = sb("a_mv", [P, NG, 2])
        rs = sb("a_rs", [P, NG])
        vs = sb("a_vs", [P, NG])
        half = sb("a_half", [P, 1])
        wq = sb("a_wqkv", [P, 3 * INNER])
        wo = sb("a_wout", [P, HP, D])
        gcol = sb("a_gcol", [P, 1])
        bcol = sb("a_bcol", [P, 1])
        beta = sb("a_beta", [P, HA])
        ombeta = sb("a_ombeta", [P, HA])
        bexp = sb("a_bexp", [P, HA])
        cosb = sb("a_cos", [P, NSEG, DA])
        sinb = sb("a_sin", [P, NSEG, DA])
        idf = sb("a_idf", [P, P])
        idb = sb("a_idb", [P, P], BF16)
        maskf = sb("a_maskf", [P, HP * SEG])
        maskb = sb("a_maskb", [P, HA * SEG], BF16)
        xhat = sb("a_xhat", [P, D])
        xnT = sb("a_xnT", [P, P])
        rc = sb("a_rc", [P, 2, INNER])
        rn = sb("a_rn", [P, 2, INNER])
        ex = sb("a_ex", [P, 2, INNER])
        sq = sb("a_sq", [P, INNER])
        sk = sb("a_sk", [P, 2, INNER])
        v = sb("a_v", [P, 2, INNER])
        qT = sb("a_qT", [P, HP, P])
        kT = sb("a_kT", [P, HP, BG, 2, SEG])
        sT = sb("a_sT", [P, 2, HP, P])
        ssub = sb("a_ssub", [P, HA, SEG])
        pe_ = sb("a_pe", [P, HA, SEG])
        pn = sb("a_pn", [P, HA * SEG])
        pT = sb("a_pT", [P, HA, P])
        mx = sb("a_mx", [P, HA])
        psum_ = sb("a_psum", [P, HA])
        pr = sb("a_pr", [P, HA])
        prs = sb("a_prs", [P, HA])
        mem = sb("a_mem", [P, NG, HP, BG, 2 * MC])
        ubd = sb("a_ubd", [P, BG, HA, MC])
        rdk = sb("a_rdk", [P, HA])
        dq = sb("a_dq", [P, 3, HA])
        pv_ = sb("a_prevv", [P, INNER])
        on = sb("a_on", [P, INNER])
        oT = sb("a_oT", [P, HP, P])
        y = sb("a_y", [P, 2, D])
        ps = ctx.enter_context(nc.psum_tensor("a_ps", [P, 8, 512], F32))

        s_const = sem("a_const")
        s_x = [sem(f"a_x{g}") for g in range(NG)]
        s_st = [sem(f"a_st{g}") for g in range(NG)]
        s_beta, s_set = sem("a_beta_s"), sem("a_set")
        s_stats, s_mv, s_vs, s_rs = sem("a_stats_s"), sem("a_mv_s"), sem("a_vs_s"), sem("a_rs_s")
        s_xhat, s_xT, s_xnT = sem("a_xhat_s"), sem("a_xT_s"), sem("a_xnT_s")
        s_q, s_k, s_v, s_vc = sem("a_q_s"), sem("a_k_s"), sem("a_v_s"), sem("a_vc_s")
        s_rq, s_rk = sem("a_rq_s"), sem("a_rk_s")
        s_qr, s_kr = sem("a_qr_s"), sem("a_kr_s")
        s_nq, s_nk = sem("a_nq_s"), sem("a_nk_s")
        s_relu = [sem("a_reluq_s"), sem("a_reluk_s")]
        s_exq, s_exk, s_sq, s_sk = sem("a_exq_s"), sem("a_exk_s"), sem("a_sq_s"), sem("a_sk_s")
        s_tqr, s_tkr, s_tsq, s_tsk = sem("a_tqr_s"), sem("a_tkr_s"), sem("a_tsq_s"), sem("a_tsk_s")
        s_qrT, s_krT, s_sqT, s_skT = sem("a_qrT_s"), sem("a_krT_s"), sem("a_sqT_s"), sem("a_skT_s")
        s_S, s_mx, s_sub, s_pe, s_sum, s_prs, s_pn, s_pT = (sem(f"a_{n}_s") for n in ("S", "mx", "sub", "pe", "sum", "prs", "pn", "pT"))
        s_prev, s_rdk, s_tk, s_u, s_ubd01, s_ubd23 = (sem(f"a_{n}_s") for n in ("prev", "rdk", "tk", "u", "ubd01", "ubd23"))
        s_num, s_dq, s_on = (sem(f"a_{n}_s") for n in ("num", "dq", "on"))
        s_dm, s_mem = sem("a_dm_s"), sem("a_mem_s")
        s_oTp, s_oT, s_y, s_x1 = (sem(f"a_{n}_s") for n in ("oTp", "oT", "y", "x1"))

        def heads(ap):
            return ap.rearrange("p (h d) -> p h d", h=HA)

        def pair(ap, hp):
            return ap[:, hp * P:(hp + 1) * P]

        def wide(b0):
            return ps[:, b0:b0 + 2, :].rearrange("p b c -> p (b c)")

        def mem_read(b0):
            return ps[:, b0:b0 + 4, 0:4 * MC].rearrange("p b (c m) -> p b c m", m=MC)

        def read_by(b0, scale, out):
            return nc.vector.tensor_tensor(out.rearrange("p (b c m) -> p b c m", b=4, c=4), mem_read(b0)[:, :, :, 0:DA],
                                           scale.rearrange("p (b c) -> p b c", b=4).unsqueeze(3).broadcast_to([P, 4, 4, DA]), ALU.mult)

        UPDATE_BANKS = (6, 4, 4, 6)

        def by_head(ap, n):
            return ap.unsqueeze(2).broadcast_to([P, HA, n])

        block = ctx.enter_context(nc.Block())

        def run(both, stage_a, stage_b, eng):
            stage_a(0, 0, 0)
            with eng.Fori(0, NSEG - 1) as s:
                for g in range(NG):
                    t = s * NG + g
                    both(t, g, s, t + 1, (g + 1) % NG, s if g + 1 < NG else s + 1, 2)
            for g in range(NG - 1):
                t = (NSEG - 1) * NG + g
                both(t, g, NSEG - 1, t + 1, g + 1, NSEG - 1, min(NT - 2 - t, 2))
            stage_b(NT - 1, NG - 1, NSEG - 1)

        @block.sync
        def _(sp):
            def rows_of(ap, g, s):
                return ap[g * BG:(g + 1) * BG, bass.ds(s * SEG, SEG) if not isinstance(s, int) else slice(s * SEG, (s + 1) * SEG), :]

            def load(g, s):
                sp.dma_start(xin[:, g, :], rows_of(x, g, s)).then_inc(s_x[g], 16)

            def store(t, g, s):
                sp.wait_ge(s_x1, t + 2)
                sp.dma_start(rows_of(x1, g, s), xout[:, g, :]).then_inc(s_st[g], 16)

            load(0, 0)
            for dst, src in ((idf, ident), (maskf, seg_mask), (wq, w_qkv)):
                sp.dma_start(dst[:], src).then_inc(s_const, 16)
            sp.dma_start(beta[:], mem_beta.rearrange("a h b c -> (a b c) h").broadcast_to([P, HA])).then_inc(s_const, 16)
            sp.dma_start(gcol[:], ln_g.rearrange("(p a) -> p a", a=1)).then_inc(s_const, 16)
            sp.dma_start(bcol[:], ln_b.rearrange("(p a) -> p a", a=1)).then_inc(s_const, 16)
            for dst, src in ((cosb, rope_cos), (sinb, rope_sin)):
                sp.dma_start(dst[:], src).then_inc(s_const, 16)
            sp.dma_start(wo[:], w_out.rearrange("(h p) d -> p h d", p=P)).then_inc(s_const, 16)
            for g in range(1, NG):
                load(g, 0)
            with sp.Fori(0, NSEG - 1) as s:
                for g in range(NG):
                    store(s * NG + g, g, s)
                    load(g, s + 1)
            for g in range(NG):
                store((NSEG - 1) * NG + g, g, NSEG - 1)
            for g in range(NG):
                sp.wait_ge(s_st[g], 16 * NSEG + 16)

        CONST_ALL = 16 * 9

        @block.vector
        def _(dve):
            dve.wait_ge(s_const, CONST_ALL)
            nc.vector.tensor_copy(idb[:], idf[:]).then_inc(s_set, 1)
            for a in range(2):
                nc.vector.tensor_copy(maskb[:, a * HP * SEG:(a + 1) * HP * SEG], maskf[:]).then_inc(s_set, 1)
            nc.vector.memset(half[:], -0.5).then_inc(s_set, 1)
            for zero in (mem, ubd, kT, pT):
                nc.vector.memset(zero[:], 0.0).then_inc(s_set, 1)
            dve.wait_ge(s_set, 8)
            nc.vector.memset(mx[:], 0.0).then_inc(s_x1, 1)
            for g in range(NG):
                nc.vector.memset(xout[:, g, :], 0.0).then_inc(s_st[g], 16)
            for a in range(2):
                nc.vector.memset(mem[DA * a:DA * (a + 1), :, :, :, (a + 1) * MC - 1:(a + 1) * MC].rearrange("p g h b m -> p (g h b) m"),
                                 1e-6).then_inc(s_set, 1)
            for b in range(BG):
                nc.vector.memset(ubd[SEG * b:SEG * (b + 1), b, :, DA:MC], 1.0).then_inc(s_set, 1)
            dve.wait_ge(s_beta, 1)
            nc.vector.tensor_scalar(bexp[:], bexp[:], 1.0, None, ALU.add).then_inc(s_beta, 1)
            dve.wait_ge(s_beta, 2)
            nc.vector.reciprocal(beta[:], bexp[:]).then_inc(s_beta, 1)
            dve.wait_ge(s_beta, 3)
            nc.vector.tensor_scalar(ombeta[:], beta[:], -1.0, 1.0, ALU.mult, ALU.add).then_inc(s_beta, 1)
            dve.wait_ge(s_beta, 4)

            def row_stats(t, g, s):
                dve.wait_ge(s_x[g], s * 16 + 16)
                dve.nop(nofuse=True)
                nc.vector.bn_stats(stats[:, g, :], xin[:, g, :]).then_inc(s_stats, 1)
                dve.wait_ge(s_stats, t + 1)
                dve.nop(nofuse=True)
                nc.vector.bn_aggr(mv[:, g, :], stats[:, g, :]).then_inc(s_mv, 1)

            def make_xhat(t, g):
                dve.wait_ge(s_rs, t + 1)
                nc.vector.tensor_scalar(xhat[:], xin[:, g, :], mv[:, g, 0:1], rs[:, g:g + 1],
                                        ALU.subtract, ALU.mult).then_inc(s_xhat, 1)

            def rope_products(i, s, t):
                src = wide(2 * i)
                cos, sin = cosb[:, s, :], sinb[:, s, :]
                dve.wait_ge(s_relu[i], t + 1)
                nc.vector.tensor_tensor(heads(rc[:, i, :]), heads(src), cos.unsqueeze(1).broadcast_to([P, HA, DA]), ALU.mult)
                for e in range(2):
                    def every(ap, k):
                        return ap.rearrange("p (h d e) -> p h d e", h=HA, e=2)[:, :, :, k]
                    sn = sin.rearrange("p (d e) -> p d e", e=2)[:, :, e].unsqueeze(1).broadcast_to([P, HA, DA // 2])
                    last = nc.vector.tensor_tensor(every(rn[:, i, :], e), every(src, 1 - e), sn, ALU.mult)
                last.then_inc((s_rq, s_rk)[i], 1)

            def softmax_head(t):
                S = ps[:, 2, :].rearrange("p (h m) -> p h m", m=SEG)
                dve.wait_ge(s_S, t + 1)
                nc.vector.tensor_reduce(mx[:], S, AX.X, ALU.max).then_inc(s_mx, 1)
                dve.wait_ge(s_mx, t + 1)
                nc.vector.tensor_tensor(ssub[:], S, by_head(mx[:], SEG), ALU.subtract).then_inc(s_sub, 1)

            def softmax_sum(t):
                dve.wait_ge(s_pe, t + 1)
                nc.vector.tensor_reduce(psum_[:], pe_[:], AX.X, ALU.add).then_inc(s_sum, 1)
                dve.wait_ge(s_sum, t * 2 + 1)
                nc.vector.reciprocal(pr[:], psum_[:]).then_inc(s_sum, 1)
                dve.wait_ge(s_sum, t * 2 + 2)
                nc.vector.tensor_tensor(prs[:], pr[:], ombeta[:], ALU.mult).then_inc(s_prs, 1)

            def transpose_p(t):
                dve.wait_ge(s_pn, t + 1)
                for b in range(BG):
                    rows = slice(SEG * b, SEG * (b + 1))
                    last = nc.vector.transpose(pT[rows, :, rows], pn[rows, :].rearrange("p (h m) -> p h m", m=SEG))
                last.then_inc(s_pT, 1)

            def spread_u(t):
                dve.wait_ge(s_u, t + 1)
                for b in (0, 1):
                    rows = slice(SEG * b, SEG * (b + 1))
                    last = nc.vector.tensor_copy(ubd[rows, b, :, 0:DA], heads(pv_[rows, :]))
                last.then_inc(s_ubd01, 1)

            def read_prev(t):
                R = mem_read(0)
                dve.wait_ge(s_prev, t + 1)
                nc.vector.reciprocal(rdk[:].rearrange("p (b c) -> p b c", b=4), R[:, :, :, DA]).then_inc(s_rdk, 1)
                dve.wait_ge(s_rdk, t + 1)
                read_by(0, rdk[:], pv_[:]).then_inc(s_tk, 1)

            def read_num(t):
                R = mem_read(4)
                dve.wait_ge(s_num, t + 1)
                nc.vector.tensor_scalar(dq[:, 0, :].rearrange("p (b c) -> p b c", b=4), R[:, :, :, DA], 1e-6, None,
                                        ALU.add).then_inc(s_dq, 1)
                dve.wait_ge(s_dq, t * 3 + 1)
                nc.vector.reciprocal(dq[:, 1, :], dq[:, 0, :]).then_inc(s_dq, 1)
                dve.wait_ge(s_dq, t * 3 + 2)
                nc.vector.tensor_tensor(dq[:, 2, :], dq[:, 1, :], beta[:], ALU.mult).then_inc(s_dq, 1)
                dve.wait_ge(s_dq, t * 3 + 3)
                read_by(4, dq[:, 2, :], on[:]).then_inc(s_on, 1)

            def add_mem(t, g, half_):
                for k in (2 * half_, 2 * half_ + 1):
                    dve.wait_ge(s_dm, t * 4 + (k + 1))
                    for a in range(2):
                        rows = slice(DA * a, DA * (a + 1))
                        m = mem[rows, g, 2 * k:2 * k + 2, :, a * MC:(a + 1) * MC]
                        b0 = UPDATE_BANKS[k]
                        last = nc.vector.tensor_tensor(m, ps[rows, b0:b0 + 2, 0:BG * MC].rearrange("p h (b m) -> p h b m", m=MC), m,
                                                       ALU.add)
                    last.then_inc(s_mem, 1)

            def add_x(t, g, s):
                dve.wait_ge(s_y, t + 1)
                dve.wait_ge(s_st[g], s * 16 + 16)
                nc.vector.tensor_tensor(xout[:, g, :], ps[:, 3, 0:D], xin[:, g, :], ALU.add).then_inc(s_x1, 1)

            def stage_a(t, g, s):
                row_stats(t, g, s)
                row_stats(t + 1, g + 1, s)
                make_xhat(t, g)
                rope_products(0, s, t)
                rope_products(1, s, t)
                make_xhat(t + 1, g + 1)
                row_stats(t + 2, g + 2, s)
                softmax_head(t)
                softmax_sum(t)

            def stage_b(t, g, s):
                read_num(t)
                read_prev(t)
                transpose_p(t)
                spread_u(t)
                add_mem(t, g, 0)
                add_mem(t, g, 1)
                add_x(t, g, s)

            def both(t, g, s, tn, gn, sn, ahead):
                read_num(t)
                read_prev(t)
                if ahead:
                    make_xhat(tn + 1, (g + 2) % NG)
                transpose_p(t)
                spread_u(t)
                rope_products(0, sn, tn)
                rope_products(1, sn, tn)
                add_mem(t, g, 0)
                add_mem(t, g, 1)
                if ahead == 2:
                    row_stats(tn + 2, (g + 3) % NG, s if g + 3 < NG else s + 1)
                softmax_head(tn)
                softmax_sum(tn)
                add_x(t, g, s)

            run(both, stage_a, stage_b, dve)

        @block.gpsimd
        def _(pool):
            pool.wait_ge(s_set, 4)

            def layernorm_scale(t, g):
                pool.wait_ge(s_mv, t + 1)
                pool.nop(nofuse=True)
                nc.gpsimd.tensor_scalar(vs[:, g:g + 1], mv[:, g, 1:2], 1.0 + EPS, EPS * EPS, ALU.mult, ALU.add).then_inc(s_vs, 1)
                pool.wait_ge(s_vs, t + 1)
                nc.gpsimd.tensor_tensor(rs[:, g:g + 1], vs[:, g:g + 1], half[:], ALU.pow).then_inc(s_rs, 1)

            def rope_sum(i, t):
                pool.wait_ge((s_rq, s_rk)[i], t + 1)
                nc.gpsimd.tensor_tensor(rc[:, i, :], rc[:, i, :], rn[:, i, :], ALU.add).then_inc((s_qr, s_kr)[i], 1)

            def elu(i, t, par):
                pool.wait_ge(s_relu[i], t + 1)
                pool.wait_ge((s_exq, s_exk)[i], t + 1)
                pool.nop(nofuse=True)
                to = sk[:, par, :] if i else sq[:]
                nc.gpsimd.tensor_tensor(to, ex[:, i, :], to, ALU.add).then_inc((s_sq, s_sk)[i], 1)

            def scale_p(t):
                pool.wait_ge(s_prs, t + 1)
                nc.gpsimd.tensor_tensor(pn[:].rearrange("p (h m) -> p h m", h=HA), pe_[:], by_head(prs[:], SEG),
                                        ALU.mult).then_inc(s_pn, 1)

            def make_u(t, g):
                pool.wait_ge(s_tk, t + 1)
                pool.wait_ge(s_vc, t + 1)
                nc.gpsimd.tensor_tensor(pv_[:], v[:, g % 2, :], pv_[:], ALU.subtract).then_inc(s_u, 1)

            def stage_a(t, g, s):
                layernorm_scale(t, g)
                layernorm_scale(t + 1, g + 1)
                rope_sum(0, t)
                rope_sum(1, t)
                elu(0, t, g % 2)
                elu(1, t, g % 2)
                layernorm_scale(t + 2, g + 2)
                scale_p(t)

            def stage_b(t, g, s):
                make_u(t, g)

            def both(t, g, s, tn, gn, sn, ahead):
                make_u(t, g)
                rope_sum(0, tn)
                rope_sum(1, tn)
                elu(0, tn, gn % 2)
                elu(1, tn, gn % 2)
                if ahead == 2:
                    layernorm_scale(tn + 2, (g + 3) % NG)
                scale_p(tn)

            run(both, stage_a, stage_b, pool)

        @block.scalar
        def _(act):
            act.wait_ge(s_const, CONST_ALL)
            nc.scalar.activation(bexp[:], beta[:], ACT.Exp, scale=-1.0).then_inc(s_beta, 1)
            act.wait_ge(s_set, 8)

            def keep_xnT(t):
                act.wait_ge(s_xT, t + 1)
                nc.scalar.activation(xnT[:], ps[:, 3, 0:P], ACT.Identity, bias=bcol[:], scale=gcol[:]).then_inc(s_xnT, 1)

            def relus(i, t, par):
                act.wait_ge((s_q, s_k)[i], t + 1)
                nc.scalar.activation(ex[:, i, :], wide(2 * i), ACT.Relu, scale=-1.0).then_inc((s_nq, s_nk)[i], 1)
                nc.scalar.activation(sk[:, par, :] if i else sq[:], wide(2 * i), ACT.Relu).then_inc(s_relu[i], 1)

            def negative_exp(i, t):
                act.wait_ge((s_nq, s_nk)[i], t + 1)
                nc.scalar.activation(ex[:, i, :], ex[:, i, :], ACT.Exp, scale=-1.0).then_inc((s_exq, s_exk)[i], 1)

            def keep_v(t, par):
                act.wait_ge(s_v, t + 1)
                nc.scalar.activation(v[:, par, :], wide(6), ACT.Copy).then_inc(s_vc, 1)

            def keep_ropes(t):
                act.wait_ge(s_tqr, t + 1)
                nc.scalar.activation(qT[:].rearrange("p h c -> p (h c)"), wide(0), ACT.Copy).then_inc(s_qrT, 1)
                act.wait_ge(s_tkr, t + 1)
                for a in range(2):
                    rows = slice(DA * a, DA * (a + 1))
                    last = nc.scalar.activation(kT[rows, :, :, a, :].rearrange("p h b m -> p (h b) m"),
                                                wide(2)[rows].rearrange("p (c m) -> p c m", m=SEG), ACT.Copy)
                last.then_inc(s_krT, 1)

            def keep_eluT(i, t):
                act.wait_ge((s_tsq, s_tsk)[i], t + 1)
                nc.scalar.activation(sT[:, i].rearrange("p h c -> p (h c)"), wide(0), ACT.Copy).then_inc((s_sqT, s_skT)[i], 1)

            def exp(t):
                act.wait_ge(s_sub, t + 1)
                nc.scalar.activation(pe_[:], ssub[:], ACT.Exp, scale=float(DA) ** -0.5).then_inc(s_pe, 1)

            def spread_u(t):
                act.wait_ge(s_u, t + 1)
                for b in (2, 3):
                    rows = slice(SEG * b, SEG * (b + 1))
                    last = nc.scalar.activation(ubd[rows, b, :, 0:DA], heads(pv_[rows, :]), ACT.Copy)
                last.then_inc(s_ubd23, 1)

            def keep_oT(t):
                act.wait_ge(s_oTp, t + 1)
                nc.scalar.activation(oT[:].rearrange("p h c -> p (h c)"), wide(4), ACT.Copy).then_inc(s_oT, 1)

            def stage_a(t, g, s):
                keep_xnT(t)
                keep_v(t, g % 2)
                relus(0, t, g % 2)
                relus(1, t, g % 2)
                negative_exp(0, t)
                negative_exp(1, t)
                keep_ropes(t)
                keep_xnT(t + 1)
                keep_eluT(0, t)
                exp(t)
                keep_eluT(1, t)

            def stage_b(t, g, s):
                spread_u(t)
                keep_oT(t)

            def both(t, g, s, tn, gn, sn, ahead):
                keep_v(tn, gn % 2)
                relus(0, tn, gn % 2)
                relus(1, tn, gn % 2)
                spread_u(t)
                keep_oT(t)
                negative_exp(0, tn)
                negative_exp(1, tn)
                keep_ropes(tn)
                if ahead:
                    keep_xnT(tn + 1)
                keep_eluT(0, tn)
                exp(tn)
                keep_eluT(1, tn)

            run(both, stage_a, stage_b, act)

        @block.tensor
        def _(pe):
            pe.wait_ge(s_const, CONST_ALL)
            pe.wait_ge(s_set, 3)

            def transposes(src, b0, sem_):
                for hp in range(HP):
                    last = nc.tensor.transpose(ps[:, b0 + hp // 4, P * (hp % 4):P * (hp % 4 + 1)], pair(src, hp), idf[:])
                last.then_inc(sem_, 1)

            def transpose_x(t):
                pe.wait_ge(s_xhat, t + 1)
                nc.tensor.transpose(ps[:, 3, 0:P], xhat[:], idf[:]).then_inc(s_xT, 1)

            def project(i, b0, sem_):
                for j in range(2):
                    c = i * INNER + j * 512
                    last = nc.tensor.matmul(ps[:, b0 + j, :], xnT[:], wq[:, c:c + 512], start=True, stop=True)
                last.then_inc(sem_, 1)

            def project_qk(t):
                project(0, 0, s_q)
                project(1, 2, s_k)

            def project_v(t):
                pe.wait_ge(s_xnT, t + 1)
                project(2, 6, s_v)

            def read_memory(i, t, g, b0, sem_):
                for hp in range(HP):
                    for b in range(BG):
                        rows = slice(SEG * b, SEG * (b + 1))
                        last = nc.tensor.matmul(ps[rows, b0 + hp // 2, (hp % 2) * 2 * MC:(hp % 2 + 1) * 2 * MC],
                                                sT[:, i, hp, rows], mem[:, g, hp, b, :],
                                                start=(hp % 2 == 0), stop=True, skip_group_check=True)
                last.then_inc(sem_, 1)

            def attend(t, g):
                pe.wait_ge(s_on, t + 1)
                for hp in range(HP):
                    nc.tensor.matmul(ps[:, 4 + hp // 4, P * (hp % 4):P * (hp % 4 + 1)], pair(on, hp), idf[:],
                                     start=(hp % 4 == 0), stop=False, is_transpose=True, skip_group_check=True)
                pe.wait_ge(s_pT, t + 1)
                for h in range(HA):
                    rows = slice(DA * (h % 2), DA * (h % 2 + 1))
                    hp = h // 2
                    last = nc.tensor.matmul(ps[rows, 4 + hp // 4, P * (hp % 4):P * (hp % 4 + 1)], v[:, g % 2, h * DA:(h + 1) * DA],
                                            pT[:, h, :], start=False, stop=True, skip_group_check=True)
                last.then_inc(s_oTp, 1)

            def update(t, g, half_, tv=None):
                if half_ == 0:
                    pe.wait_ge(s_ubd01, t + 1)
                    pe.wait_ge(s_ubd23, t + 1)
                    if tv is not None:
                        pe.wait_ge(s_vc, tv + 1)
                for k in (2 * half_, 2 * half_ + 1):
                    if k == 1:
                        pe.wait_ge(s_oT, t + 1)
                    if half_:
                        pe.wait_ge(s_mem, t * 4 + 2)
                    for hp in (2 * k, 2 * k + 1):
                        for a in range(2):
                            h = 2 * hp + a
                            last = nc.tensor.matmul(ps[DA * a:DA * (a + 1), UPDATE_BANKS[k] + hp % 2, 0:BG * MC], sk[:, g % 2, h * DA:(h + 1) * DA],
                                                    ubd[:, :, h, :], start=True, stop=True)
                    last.then_inc(s_dm, 1)

            def transpose_rope(i, t):
                pe.wait_ge((s_qr, s_kr)[i], t + 1)
                transposes(rc[:, i, :], 2 * i, (s_tqr, s_tkr)[i])

            def transpose_elu(i, t, g):
                pe.wait_ge((s_sq, s_sk)[i], t + 1)
                transposes(sk[:, g % 2, :] if i else sq[:], 0, (s_tsq, s_tsk)[i])

            def scores(t):
                pe.wait_ge(s_krT, t + 1)
                nc.tensor.matmul(ps[:, 2, :], idb[:], maskb[:], start=True, stop=False, skip_group_check=True)
                for hp in range(HP):
                    for b in range(BG):
                        toks = slice(SEG * b, SEG * (b + 1))
                        last = nc.tensor.matmul(ps[toks, 2, hp * 2 * SEG:(hp + 1) * 2 * SEG], qT[:, hp, toks],
                                                kT[:, hp, b, :, :].rearrange("p a m -> p (a m)"), start=False, stop=True,
                                                skip_group_check=True)
                last.then_inc(s_S, 1)

            def output(t):
                pe.wait_ge(s_oT, t + 1)
                for hp in range(HP):
                    last = nc.tensor.matmul(ps[:, 3, 0:D], oT[:, hp, :], wo[:, hp, :], start=(hp == 0), stop=(hp == HP - 1))
                last.then_inc(s_y, 1)

            def stage_a(t, g, s):
                transpose_x(t)
                project_v(t)
                project_qk(t)
                for i in range(2):
                    transpose_rope(i, t)
                scores(t)
                transpose_x(t + 1)
                transpose_elu(0, t, g)
                pe.wait_ge(s_sqT, t + 1)
                transpose_elu(1, t, g)
                pe.wait_ge(s_vc, t + 1)

            def read_num(t, g):
                pe.wait_ge(s_sqT, t + 1)
                pe.nop(nofuse=True)
                read_memory(0, t, g, 4, s_num)

            def read_prev(t, g):
                pe.wait_ge(s_x1, t + 1)
                pe.wait_ge(s_sub, t + 1)
                pe.wait_ge(s_skT, t + 1)
                pe.nop(nofuse=True)
                read_memory(1, t, g, 0, s_prev)

            def stage_b(t, g, s):
                read_num(t, g)
                read_prev(t, g)
                pe.wait_ge(s_on, t + 1)
                attend(t, g)
                update(t, g, 0)
                update(t, g, 1)
                output(t)

            def both(t, g, s, tn, gn, sn, ahead):
                read_num(t, g)
                read_prev(t, g)
                pe.wait_ge(s_on, t + 1)
                project_v(tn)
                pe.wait_ge(s_tk, t + 1)
                project_qk(tn)
                attend(t, g)
                update(t, g, 0, tn)
                transpose_rope(0, tn)
                transpose_rope(1, tn)
                update(t, g, 1)
                scores(tn)
                if ahead:
                    transpose_x(tn + 1)
                transpose_elu(0, tn, gn)
                pe.wait_ge(s_xnT, tn + (2 if ahead else 1))
                output(t)
                pe.wait_ge(s_sqT, tn + 1)
                transpose_elu(1, tn, gn)
                pe.wait_ge(s_mem, t * 4 + 4)

            pe.wait_ge(s_set, 10 + BG)
            run(both, stage_a, stage_b, pe)


NC = N // P
E = 8
DFF = 4 * D
NF = DFF // P
HB, DB = 16, 8
SPLIT = 6
SROW = SPLIT * DB
MROW = 3
HROW = 64
HG = 4
NHG = HB // HG
VC = 32
BANK = 512


def mlp_attn_mlp_layers(nc, x1, w_qkv, w_proj, b_proj, ln_g, ln_b, attn_w, attn_b, w1, b1, w2, b2,
                        next_w, next_b, rope_cos, rope_sin, causal, ident, out):
    ctx = ExitStack()
    with ctx:
        def sb(name, shape, dt=F32):
            return ctx.enter_context(nc.sbuf_tensor(name, shape, dt))

        def sem(name):
            return ctx.enter_context(nc.semaphore("b_" + name))

        X = sb("b_x", [P, B, NC, D])
        wb = sb("b_wqkv", [P, 3 * D])
        wp = sb("b_wproj", [P, D])
        wa = sb("b_attnw", [P, D])
        wn = sb("b_nextw", [P, D])
        bp = sb("b_bproj", [P, D])
        nb = sb("b_nextb", [P, D])
        NVEC = E * NF + E + 3
        vecs = sb("b_vecs", [NVEC, D])
        cols = sb("b_cols", [P, NVEC])
        C_B2, C_G, C_B, C_AB = E * NF, E * NF + E, E * NF + E + 1, E * NF + E + 2
        cosb = sb("b_cos", [P, NC, DB])
        sinb = sb("b_sin", [P, NC, DB])
        idf = sb("b_idf", [P, P])
        idb = sb("b_idb", [P, P], BF16)
        maskf = sb("b_maskf", [P, 2, P])
        maskb = sb("b_maskb", [P, 2, P], BF16)
        half = sb("b_half", [P, NC])
        w1s = sb("b_w1", [P, 2, DFF])
        w2s = sb("b_w2", [P, 2, NF, D])
        fst = sb("b_fst", [P, NC, 6])
        fmv = sb("b_fmv", [P, NC, 2])
        ft = sb("b_ft", [P, 4, NC])
        z = sb("b_z", [P, NC, D])
        xl = sb("b_xl", [P, NC, D])
        xlT = sb("b_xlT", [P, N])
        xaT = sb("b_xaT", [P, N])
        hT = sb("b_hT", [P, NF, N])
        yT = sb("b_yT", [P, N])
        pre = sb("b_pre", [P, NC, D])
        fo = sb("b_fo", [P, NC, D])
        ast = sb("b_ast", [P, NC, 6])
        amv = sb("b_amv", [P, NC, 2])
        at_ = sb("b_at", [P, 2, NC])
        xn = sb("b_xn", [P, NC, D])
        xnT = sb("b_xnT", [P, N])
        qc = sb("b_qc", [P, NC, 2, HB, DB])
        qs = sb("b_qs", [P, NC, 2, HB, DB])
        r1 = sb("b_r1", [P, NC, 2, HB, DB])
        r2 = sb("b_r2", [P, NC, 2, HB, DB])
        st = sb("b_st", [P, NC, 2, HB, HROW], BF16)
        QT = sb("b_QT", [P, HB, N], BF16)
        KT = sb("b_KT", [P, HB // 2, N], BF16)
        va = sb("b_va", [P, NC, HB, VC])
        nm = sb("b_nm", [P, 3, NC, HB])
        mb = sb("b_mb", [P, NC, 2, MROW, HB // 2], BF16)
        MB = 2 * MROW * HB // 2
        mT = sb("b_mT", [MB, N], BF16)
        PT = sb("b_PT", [P, 2, HG, 1280])
        oTs = sb("b_oTs", [P, NHG, N])
        rec = sb("b_rec", [P, NC, HB])
        o2 = sb("b_o2", [P, NC, D])
        o2T = sb("b_o2T", [P, N])
        ps = ctx.enter_context(nc.psum_tensor("b_ps", [P, 8, BANK], F32))

        s_const, s_x, s_set, s_cT, s_cols = (sem(n) for n in ("const", "x", "set", "cT", "cols"))
        s_w = [sem("w0"), sem("w1")]
        s_fst, s_fmv, s_frs, s_z, s_xl = (sem(n) for n in ("fst", "fmv", "frs", "z", "xl"))
        s_zT, s_xlT, s_xlTc, s_xa, s_xac = (sem(n) for n in ("zT", "xlT", "xlTc", "xa", "xac"))
        s_h, s_hc = sem("h"), sem("hc")
        s_yT, s_yTc, s_fo, s_pre, s_foc, s_fx = (sem(n) for n in ("yT", "yTc", "fo", "pre", "foc", "fx"))
        s_ast, s_amv, s_ars, s_xn, s_xnT, s_xnTc = (sem(n) for n in ("ast", "amv", "ars", "xn", "xnT", "xnTc"))
        s_qkv, s_va, s_rp, s_rs, s_p1, s_r1, s_p2, s_r2, s_p3, s_p3a = (sem(n) for n in ("qkv", "va", "rp", "rs", "p1", "r1", "p2", "r2", "p3", "p3a"))
        s_kT, s_kTc, s_qT, s_qTe, s_qTo = (sem(n) for n in ("kT", "kTc", "qT", "qTe", "qTo"))
        s_S, s_Sc = sem("S"), sem("Sc")
        s_nm, s_m3, s_mT, s_mTc, s_mq = (sem(n) for n in ("nm", "m3", "mT", "mTc", "mq"))
        s_T, s_Tc, s_pv, s_pvc = (sem(n) for n in ("T", "Tc", "pv", "pvc"))
        s_oB, s_rec, s_o2, s_o2T, s_o2Tc, s_y, s_xb, s_x3 = (sem(n) for n in ("oB", "rec", "o2", "o2T", "o2Tc", "y", "xb", "x3"))
        s_out = sem("out")

        MAX_ITEMS = [(c, h, nh) for c, nh in ((3, 2), (2, 2), (1, 4), (0, 8)) for h in range(0, HB, nh)]
        NMAX = len(MAX_ITEMS)
        MLP_AT = {1: 2, 3: 3, 5: 4, 7: 5, 9: 6, 11: 7, 13: 8, 15: 9, 17: 10}
        T_ITEMS = (((0, 0, 512),), ((1, 0, 384), (3, 384, 128)), ((2, 0, 256),))
        NTI = len(T_ITEMS)
        PT_AT = (0, 512, 1024)
        KEY_AT = {0: 0, 1: 512, 3: 896, 2: 1024}

        block = ctx.enter_context(nc.Block())

        def iteration(mlp, attn, i, first, second, nxt):
            def mlp_behind(*steps):
                if first is not None:
                    for step in steps:
                        mlp(step, 0, *first)

            def mlp_before(*steps):
                if second is not None:
                    for step in steps:
                        mlp(step, 1, *second)

            mlp_behind(2)
            attn("rope", i)
            if second is not None:
                attn("add", i - 1)
            mlp_behind(3, 4)
            attn("part 1", i)
            mlp_before(0)
            mlp_behind(5)
            attn("part 2", i)
            mlp_before(1)
            mlp_behind(6, 7)
            attn("part 3", i)
            mlp_behind(8, 9)
            attn("transpose", i)
            mlp_behind(10, 11, 12, 13)
            for m in range(NMAX):
                attn("max", i, m)
                if m in MLP_AT:
                    mlp_before(MLP_AT[m])
            attn("shift", i)
            mlp_before(11, 12, 13)
            if first is not None:
                attn("norm", i + 1, first[0])
            if nxt is not None:
                mlp(0, 0, *nxt)
                mlp(1, 0, *nxt)
            attn("heads", i)
            if first is not None:
                attn("rows", i + 1)
            attn("gather", i)
            if first is not None:
                attn("project", i + 1)
            attn("out", i)

        def batches(eng, mlp, attn):
            for step in range(14):
                mlp(step, 0, 0, 0, 0)
            attn("norm", 0, 0)
            mlp(0, 0, 1, 1, 1)
            mlp(1, 0, 1, 1, 1)
            attn("rows", 0)
            attn("project", 0)
            iteration(mlp, attn, 0, (1, 1, 1), None, (2, 2, 0))
            with eng.Fori(1, B - 2) as i:
                iteration(mlp, attn, i, (i * 2, i + 1, 0), (i * 2 + 1, i - 1, 1), (i * 2 + 2, i + 2, 0))
            i = B - 2
            iteration(mlp, attn, i, (i * 2, i + 1, 0), (i * 2 + 1, i - 1, 1), None)
            i = B - 1
            iteration(mlp, attn, i, None, (i * 2, i - 1, 0), None)
            attn("add", i)
            for step in range(14):
                mlp(step, 1, 2 * B - 1, B - 1, 1)

        @block.sync
        def _(sp):
            sp.dma_start(X[:, 0], x1[0].rearrange("(c p) d -> p c d", p=P)).then_inc(s_x, 16)
            for dst, src in ((wb, w_qkv), (wp, w_proj), (wa, attn_w), (wn, next_w), (cosb, rope_cos), (sinb, rope_sin),
                             (idf, ident), (maskf, causal)):
                sp.dma_start(dst[:], src).then_inc(s_const, 16)
            for dst, src in ((bp, b_proj), (nb, next_b)):
                sp.dma_start(dst[:], src.unsqueeze(0).broadcast_to([P, D])).then_inc(s_const, 16)
            sp.dma_start(vecs[0:E * NF, :], b1.rearrange("e (j f) -> (e j) f", f=P)).then_inc(s_const, 16)
            sp.dma_start(vecs[C_B2:C_B2 + E, :], b2).then_inc(s_const, 16)
            for c, src in ((C_G, ln_g), (C_B, ln_b), (C_AB, attn_b)):
                sp.dma_start(vecs[c:c + 1, :], src.unsqueeze(0)).then_inc(s_const, 16)
            sp.dma_start(X[:, 1:B], x1[1:B].rearrange("b (c p) d -> p b c d", p=P)).then_inc(s_x, 16)
            CONST_ALL = 15

            def weights(n, e, par):
                if not (isinstance(n, int) and n < 2):
                    sp.wait_ge(s_yT, n - 1)
                sp.dma_start(w1s[:, par, :], w1[e]).then_inc(s_w[par], 16)
                sp.dma_start(w2s[:, par, :, :], w2[e].rearrange("(j f) d -> f j d", f=P)).then_inc(s_w[par], 16)

            def shift(i):
                sp.wait_ge(s_mTc, i + 1)
                for a in range(2):
                    for k in range(MROW):
                        row, of = HROW * a + SROW + k, (a * MROW + k) * (HB // 2)
                        sp.dma_start(QT[row:row + 1, a:HB:2, :], mT[of:of + HB // 2, :]).then_inc(s_mq, 16)

            def store(n, i):
                sp.wait_ge(s_fx, n + 1)
                sp.dma_start(out[i].rearrange("(c p) d -> p c d", p=P), X[:, i]).then_inc(s_out, 16)

            for n, e in ((0, 0), (1, 1), (2, 2), (3, 0)):
                weights(n, e, n % 2)
            shift(0)
            with sp.Fori(1, B - 2) as i:
                weights(i * 2 + 2, (i + 2) % E, 0)
                shift(i)
                weights(i * 2 + 3, i % E, 1)
                store(i * 2 + 1, i - 1)
            weights(2 * B - 2, (B - 2) % E, 0)
            shift(B - 2)
            weights(2 * B - 1, (B - 1) % E, 1)
            store(2 * B - 3, B - 3)
            shift(B - 1)
            store(2 * B - 2, B - 2)
            store(2 * B - 1, B - 1)
            sp.wait_ge(s_out, 16 * B)

        CONSTS = 15 * 16

        def chunks(ap):
            return ap.rearrange("p c d -> p (c d)")

        K_BANKS, Q_BANKS = (2, 4), (6, 2)

        def tps(b0):
            return ps[:, b0:b0 + 2, :].rearrange("p b c -> p (b c)").bitcast(BF16).rearrange("p (n c) -> p n c", c=P)

        mps = ps[0:MB, 2, :].bitcast(BF16)[:, 0:N]

        def q_rows(half_, a):
            return (QT[HROW * a:HROW * (a + 1), 8 * half_ + a:8 * half_ + 8:2, :].rearrange("p h (c k) -> p h c k", c=NC))

        def tps_rows(half_, a):
            return tps(Q_BANKS[half_])[HROW * a:HROW * (a + 1)].rearrange("p (h c) k -> p h c k", c=NC)

        @block.vector
        def _(dve):
            dve.wait_ge(s_const, CONSTS)
            nc.vector.tensor_copy(idb[:], idf[:]).then_inc(s_set, 1)
            nc.vector.tensor_copy(maskb[:], maskf[:]).then_inc(s_set, 1)
            nc.vector.memset(half[:], -0.5).then_inc(s_set, 1)
            nc.vector.memset(va[:], 0.0).then_inc(s_set, 1)
            nc.vector.memset(st[:], 0.0).then_inc(s_set, 1)
            nc.vector.memset(QT[:], 0.0).then_inc(s_set, 1)
            dve.wait_ge(s_set, 6)
            nc.vector.memset(va[:, :, :, DB:DB + 1].rearrange("p c h v -> p (c h) v"), 1.0).then_inc(s_set, 1)
            for c in range(NC):
                nc.vector.memset(st[:, c, 1, :, SROW:SROW + MROW], 1.0).then_inc(s_set, 1)
            dve.wait_ge(s_cT, 1)
            nc.vector.tensor_copy(cols[:], ps[:, 0, 0:NVEC]).then_inc(s_cols, 1)

            def row_stats(i, stats, mv, s_stats, s_mv, n):
                dve.nop(nofuse=True)
                for c in range(NC):
                    last = nc.vector.bn_stats(stats[:, c, :], X[:, i, c, :])
                last.then_inc(s_stats, 1)
                dve.wait_ge(s_stats, n + 1)
                dve.nop(nofuse=True)
                for c in range(NC):
                    last = nc.vector.bn_aggr(mv[:, c, :], stats[:, c, :])
                last.then_inc(s_mv, 1)

            def mlp(step, second, n, i, par):
                if step == 0:
                    if second:
                        dve.wait_ge(s_x3, i + 1)
                    elif isinstance(n, int) and n == 0:
                        dve.wait_ge(s_x, 16)
                    else:
                        dve.wait_ge(s_x, 32)
                    row_stats(i, fst, fmv, s_fst, s_fmv, n)
                elif step == 1:
                    dve.wait_ge(s_frs, n * 4 + 4)
                    if not (isinstance(n, int) and n == 0):
                        dve.wait_ge(s_xlT, n)
                    for c in range(NC):
                        last = nc.vector.tensor_scalar(z[:, c, :], X[:, i, c, :], fmv[:, c, 0:1], ft[:, 1, c:c + 1],
                                                       ALU.subtract, ALU.mult)
                    last.then_inc(s_z, 1)
                    for c in range(NC):
                        last = nc.vector.tensor_scalar(xl[:, c, :], X[:, i, c, :], fmv[:, c, 0:1], ft[:, 3, c:c + 1],
                                                       ALU.subtract, ALU.mult)
                    last.then_inc(s_xl, 1)
                elif step == 12:
                    if not (isinstance(n, int) and n == 0):
                        dve.wait_ge(s_foc, n)
                    dve.wait_ge(s_fo, n + 1)
                    nc.vector.tensor_tensor(pre[:], ps[:, 0, :].rearrange("p (c d) -> p c d", c=NC),
                                            nb[:].unsqueeze(1).broadcast_to([P, NC, D]), ALU.add).then_inc(s_pre, 1)

            def row_norm(i, n):
                dve.wait_ge(s_fx, n + 1)
                if not (isinstance(i, int) and i == 0):
                    dve.wait_ge(s_xnT, i)
                row_stats(i, ast, amv, s_ast, s_amv, i)
                dve.wait_ge(s_ars, i * 2 + 2)
                for c in range(NC):
                    last = nc.vector.tensor_scalar(xn[:, c, :], X[:, i, c, :], amv[:, c, 0:1], at_[:, 1, c:c + 1],
                                                   ALU.subtract, ALU.mult)
                last.then_inc(s_xn, 1)

            def rope(i):
                dve.wait_ge(s_va, i + 1)
                qk = ps[:, 2:6, 0:2 * D].rearrange("p c (h d) -> p c h d", d=DB)
                flat = lambda ap: ap.rearrange("p c a h d -> p c (a h) d")
                cs = cosb[:].unsqueeze(2).broadcast_to([P, NC, 2 * HB, DB])
                sn = sinb[:].unsqueeze(2).broadcast_to([P, NC, 2 * HB, DB])
                nc.vector.tensor_tensor(flat(qc[:]), qk, cs, ALU.mult)
                for a in range(2):
                    to, of = slice(4 * a, 4 * a + 4), slice(4 - 4 * a, 8 - 4 * a)
                    last = nc.vector.tensor_tensor(flat(qs[:])[:, :, :, to], qk[:, :, :, of], sn[:, :, :, to], ALU.mult)
                last.then_inc(s_rp, 1)
                dve.wait_ge(s_rp, i + 1)
                nc.vector.tensor_tensor(rows(qc[:]), rows(qc[:]), rows(qs[:]), ALU.add).then_inc(s_rs, 1)

            def rows(ap):
                return ap.rearrange("p c a h d -> p (c a h) d")

            q = lambda k: st[:, :, 0, :, k * DB:(k + 1) * DB]
            k_ = lambda k: st[:, :, 1, :, k * DB:(k + 1) * DB]

            def part_1(i):
                dve.wait_ge(s_p1, i + 1)
                nc.vector.tensor_tensor(rows(r1[:]), rows(qc[:]), rows(st[:, :, :, :, 0:DB]), ALU.subtract).then_inc(s_r1, 1)
                nc.vector.tensor_copy(q(1), q(0))
                nc.vector.tensor_copy(q(2), q(0))
                nc.vector.tensor_copy(k_(3), k_(0))
                nc.vector.tensor_copy(k_(5), k_(0))

            def part_2(i):
                dve.wait_ge(s_p2, i + 1)
                for a, k in ((0, 3), (1, 1)):
                    last = nc.vector.tensor_tensor(r2[:, :, a], r1[:, :, a], st[:, :, a, :, k * DB:(k + 1) * DB], ALU.subtract)
                last.then_inc(s_r2, 1)
                nc.vector.tensor_copy(q(4), q(3))
                nc.vector.tensor_copy(k_(4), k_(1)).then_inc(s_p3, 1)

            def keep_transposed(i):
                for half_ in range(2):
                    dve.wait_ge(s_kT, i * 2 + (half_ + 1))
                    nc.vector.tensor_copy(KT[:, 4 * half_:4 * half_ + 4, :].rearrange("p h (c k) -> p (h c) k", c=NC),
                                          tps(K_BANKS[half_])).then_inc(s_kTc, 1)
                for half_ in range(2):
                    dve.wait_ge(s_qT, i * 2 + (half_ + 1))
                    nc.vector.tensor_copy(q_rows(half_, 1), tps_rows(half_, 1)).then_inc(s_qTo, 1)

            def maximum(i, m):
                c, h, nh = MAX_ITEMS[m]
                w = (c + 1) * P
                b0 = 2 + 2 * (m % 2)
                dve.wait_ge(s_S, i * NMAX + (m + 1))
                S = ps[:, b0:b0 + 2, 0:nh // 2 * w].rearrange("p b (h w) -> p b h w", w=w)
                nc.vector.tensor_reduce(nm[:, 0, c, h:h + nh].rearrange("p (b h) -> p b h", b=2), S,
                                        AX.X, ALU.max, negate=True).then_inc(s_Sc, 1)

            def shift(i):
                m = lambda k: mb[:, :, :, k, :]
                f = lambda k: nm[:, k].rearrange("p c (h a) -> p c a h", a=2)
                dve.wait_ge(s_Sc, i * NMAX + NMAX)
                nc.vector.tensor_copy(m(0), f(0)).then_inc(s_nm, 1)
                dve.wait_ge(s_nm, i * 4 + 1)
                nc.vector.tensor_tensor(f(1), f(0), m(0), ALU.subtract).then_inc(s_nm, 1)
                dve.wait_ge(s_nm, i * 4 + 2)
                nc.vector.tensor_copy(m(1), f(1)).then_inc(s_nm, 1)
                dve.wait_ge(s_nm, i * 4 + 3)
                nc.vector.tensor_tensor(f(2), f(1), m(1), ALU.subtract).then_inc(s_nm, 1)
                dve.wait_ge(s_nm, i * 4 + 4)
                nc.vector.tensor_copy(m(2), f(2)).then_inc(s_m3, 1)

            def heads(i):
                for G in range(NHG):
                    dve.wait_ge(s_pv, i * NHG + (G + 1))
                    nc.vector.tensor_copy(oTs[:, G, :], ps[:, 6 + G % 2, :]).then_inc(s_pvc, 1)

            def gather(i):
                dve.wait_ge(s_oB, i + 1)
                O = ps[:, 2:6, :].rearrange("p c (h v) -> p c h v", v=VC)
                nc.vector.reciprocal(rec[:], O[:, :, :, DB]).then_inc(s_rec, 1)
                dve.wait_ge(s_rec, i + 1)
                nc.vector.tensor_tensor(o2[:].rearrange("p c (h v) -> p c h v", h=HB), O[:, :, :, 0:DB],
                                        rec[:].unsqueeze(3).broadcast_to([P, NC, HB, DB]), ALU.mult).then_inc(s_o2, 1)

            def add(i):
                dve.wait_ge(s_y, i + 1)
                dve.wait_ge(s_xb, i + 1)
                nc.vector.tensor_tensor(chunks(X[:, i]), ps[:, 6, :], chunks(X[:, i]), ALU.add).then_inc(s_x3, 1)

            def attn(part, i, m=None):
                if part == "norm":
                    row_norm(i, m)
                elif part == "rope":
                    rope(i)
                elif part == "part 1":
                    part_1(i)
                elif part == "part 2":
                    part_2(i)
                elif part == "transpose":
                    keep_transposed(i)
                elif part == "max":
                    maximum(i, m)
                elif part == "shift":
                    shift(i)
                elif part == "heads":
                    heads(i)
                elif part == "gather":
                    gather(i)
                elif part == "add":
                    add(i)

            batches(dve, mlp, attn)

        @block.gpsimd
        def _(pool):
            pool.wait_ge(s_set, 3)

            def mlp(step, second, n, i, par):
                if step == 0:
                    pool.wait_ge(s_fmv, n + 1)
                    pool.nop(nofuse=True)
                    var = fmv[:, :, 1]
                    nc.gpsimd.tensor_scalar(ft[:, 0], var, EPS, None, ALU.add).then_inc(s_frs, 1)
                    nc.gpsimd.tensor_scalar(ft[:, 2], var, 1.0 + EPS, EPS * EPS, ALU.mult, ALU.add).then_inc(s_frs, 1)
                    for k in range(2):
                        pool.wait_ge(s_frs, n * 4 + 2)
                        pool.nop(nofuse=True)
                        nc.gpsimd.tensor_tensor(ft[:, 2 * k + 1], ft[:, 2 * k], half[:], ALU.pow).then_inc(s_frs, 1)
                elif step == 13:
                    pool.wait_ge(s_foc, n + 1)
                    pool.nop(nofuse=True)
                    nc.gpsimd.tensor_tensor(chunks(X[:, i]), chunks(X[:, i]), chunks(fo[:]), ALU.add).then_inc(s_fx, 1)

            def attn(part, i, m=None):
                if part == "norm":
                    pool.wait_ge(s_amv, i + 1)
                    pool.nop(nofuse=True)
                    nc.gpsimd.tensor_scalar(at_[:, 0], amv[:, :, 1], EPS, None, ALU.add).then_inc(s_ars, 1)
                    pool.wait_ge(s_ars, i * 2 + 1)
                    nc.gpsimd.tensor_tensor(at_[:, 1], at_[:, 0], half[:], ALU.pow).then_inc(s_ars, 1)
                    pool.wait_ge(s_xn, i + 1)
                    pool.nop(nofuse=True)
                    nc.gpsimd.tensor_tensor(X[:, i], X[:, i], bp[:].unsqueeze(1).broadcast_to([P, NC, D]), ALU.add).then_inc(s_xb, 1)

            batches(pool, mlp, attn)

        @block.scalar
        def _(act):
            act.wait_ge(s_cols, 1)

            def mlp(step, second, n, i, par):
                if step == 2:
                    act.wait_ge(s_xlT, n + 1)
                    nc.scalar.activation(xlT[:], ps[:, 1, :], ACT.Identity, bias=cols[:, C_B:C_B + 1], scale=cols[:, C_G:C_G + 1]).then_inc(s_xlTc, 1)
                elif step == 3:
                    act.wait_ge(s_xa, n + 1)
                    nc.scalar.activation(xaT[:], ps[:, 0, :], ACT.Identity, bias=cols[:, C_AB:C_AB + 1]).then_inc(s_xac, 1)
                elif 4 <= step <= 7:
                    j = step - 4
                    act.wait_ge(s_h, n * NF + (j + 1))
                    act.nop(nofuse=True)
                    nc.scalar.activation(hT[:, j, :], ps[:, (j + 1) % 2, :], ACT.Gelu,
                                         bias=cols[:, bass.ds(i % E * NF + j, 1)]).then_inc(s_hc, 1)
                elif step == 11:
                    act.wait_ge(s_yT, n + 1)
                    act.nop(nofuse=True)
                    nc.scalar.activation(yT[:], ps[:, 1, :], ACT.Identity, bias=cols[:, bass.ds(i % E + C_B2, 1)]).then_inc(s_yTc, 1)
                elif step == 13:
                    if not (isinstance(n, int) and n == 0):
                        act.wait_ge(s_fx, n)
                    act.wait_ge(s_pre, n + 1)
                    nc.scalar.activation(fo[:], pre[:], ACT.Gelu).then_inc(s_foc, 1)

            def part(a, k):
                return st[:, :, a, :, k * DB:(k + 1) * DB]

            def rows(i):
                act.wait_ge(s_xnT, i + 1)
                nc.scalar.activation(xnT[:], ps[:, 6, :], ACT.Copy).then_inc(s_xnTc, 1)

            def project(i):
                act.wait_ge(s_qkv, i + 1)
                nc.scalar.activation(va[:, :, :, 0:DB], ps[:, 2:6, 2 * D:3 * D].rearrange("p c (h d) -> p c h d", d=DB),
                                     ACT.Copy).then_inc(s_va, 1)

            def part_1(i):
                act.wait_ge(s_rs, i + 1)
                for a in range(2):
                    last = nc.scalar.activation(part(a, 0), qc[:, :, a], ACT.Copy)
                last.then_inc(s_p1, 1)

            def part_2(i):
                act.wait_ge(s_r1, i + 1)
                nc.scalar.activation(part(0, 3), r1[:, :, 0], ACT.Copy)
                nc.scalar.activation(part(1, 1), r1[:, :, 1], ACT.Copy).then_inc(s_p2, 1)

            def part_3(i):
                act.wait_ge(s_r2, i + 1)
                nc.scalar.activation(part(0, 5), r2[:, :, 0], ACT.Copy)
                nc.scalar.activation(part(1, 2), r2[:, :, 1], ACT.Copy).then_inc(s_p3a, 1)

            def keep_transposed(i):
                for half_ in range(2):
                    act.wait_ge(s_qT, i * 2 + (half_ + 1))
                    nc.scalar.activation(q_rows(half_, 0), tps_rows(half_, 0), ACT.Copy).then_inc(s_qTe, 1)

            def shift(i):
                act.wait_ge(s_mT, i + 1)
                nc.scalar.activation(mT[:], mps, ACT.Copy).then_inc(s_mTc, 1)

            def heads(i):
                for h in range(HB):
                    for k in range(NTI):
                        w = sum(x[2] for x in T_ITEMS[k])
                        act.wait_ge(s_T, i * (HB * NTI) + (h * NTI + k + 1))
                        nc.scalar.activation(PT[:, h // HG % 2, h % HG, PT_AT[k]:PT_AT[k] + w], ps[:, 2 + (h * NTI + k) % 4, 0:w],
                                             ACT.Exp, scale=float(DB) ** -0.5).then_inc(s_Tc, 1)

            def gather(i):
                act.wait_ge(s_o2T, i + 1)
                nc.scalar.activation(o2T[:], ps[:, 7, :], ACT.Copy).then_inc(s_o2Tc, 1)

            def attn(part, i, m=None):
                if part == "rows":
                    rows(i)
                elif part == "project":
                    project(i)
                elif part == "part 1":
                    part_1(i)
                elif part == "part 2":
                    part_2(i)
                elif part == "part 3":
                    part_3(i)
                elif part == "transpose":
                    keep_transposed(i)
                elif part == "shift":
                    shift(i)
                elif part == "heads":
                    heads(i)
                elif part == "gather":
                    gather(i)

            batches(act, mlp, attn)

        @block.tensor
        def _(pe):
            pe.wait_ge(s_const, CONSTS)
            nc.tensor.transpose(ps[:, 0, 0:NVEC], vecs[:], idf[0:NVEC, 0:NVEC]).then_inc(s_cT, 1)
            pe.wait_ge(s_set, 7 + NC)
            pe.wait_ge(s_cols, 1)

            def cols_of(c):
                return slice(c * P, (c + 1) * P)

            def mlp(step, second, n, i, par):
                if step == 2:
                    if not (isinstance(n, int) and n == 0):
                        pe.wait_ge(s_pre, n)
                    pe.wait_ge(s_z, n + 1)
                    for c in range(NC):
                        last = nc.tensor.matmul(ps[:, 0, cols_of(c)], z[:, c, :], idf[:], start=(c == 0), stop=False,
                                                is_transpose=True, skip_group_check=True)
                    pe.wait_ge(s_xl, n + 1)
                    for c in range(NC):
                        last = nc.tensor.transpose(ps[:, 1, cols_of(c)], xl[:, c, :], idf[:])
                    last.then_inc(s_xlT, 1)
                elif step == 3:
                    pe.wait_ge(s_xlTc, n + 1)
                    nc.tensor.matmul(ps[:, 0, :], wa[:], xlT[:], start=False, stop=True, skip_group_check=True).then_inc(s_xa, 1)
                elif 4 <= step <= 7:
                    j = step - 4
                    if j == 0:
                        pe.wait_ge(s_w[par], (n - par) * 16 + 32)
                        pe.wait_ge(s_xac, n + 1)
                    if j >= 2:
                        pe.wait_ge(s_hc, n * NF + (j - 1))
                    nc.tensor.matmul(ps[:, (j + 1) % 2, :], w1s[:, par, cols_of(j)], xaT[:], start=True, stop=True).then_inc(s_h, 1)
                elif 8 <= step <= 11:
                    j = step - 8
                    pe.wait_ge(s_hc, n * NF + (max(j, 2) + 1))
                    last = nc.tensor.matmul(ps[:, 1, :], w2s[:, par, j, :], hT[:, j, :], start=(j == 0), stop=(j == NF - 1))
                    if j == NF - 1:
                        last.then_inc(s_yT, 1)
                elif step == 12:
                    pe.wait_ge(s_yTc, n + 1)
                    for c in range(NC):
                        last = nc.tensor.matmul(ps[:, 0, cols_of(c)], yT[:, cols_of(c)], wn[:], start=True, stop=True)
                    last.then_inc(s_fo, 1)

            def rows(i):
                pe.wait_ge(s_xn, i + 1)
                if not (isinstance(i, int) and i == 0):
                    pe.wait_ge(s_pvc, i * NHG - 1)
                for c in range(NC):
                    last = nc.tensor.transpose(ps[:, 6, cols_of(c)], xn[:, c, :], idf[:])
                last.then_inc(s_xnT, 1)

            def project(i):
                pe.wait_ge(s_xnTc, i + 1)
                for c in range(NC):
                    last = nc.tensor.matmul(ps[:, 2 + c, 0:3 * D], xnT[:, cols_of(c)], wb[:], start=True, stop=True)
                last.then_inc(s_qkv, 1)

            def transposed(a, half_, sem_):
                T = tps((Q_BANKS, K_BANKS)[a][half_])
                for hh in range(4):
                    hp = 4 * half_ + hh
                    for c in range(NC):
                        last = nc.tensor.transpose(T[:, hh * NC + c, :], st[:, c, a, 2 * hp:2 * hp + 2, :].rearrange("p h r -> p (h r)"), idb[:])
                last.then_inc(sem_, 1)

            def transpose(i):
                pe.wait_ge(s_p3, i + 1)
                pe.wait_ge(s_p3a, i + 1)
                transposed(1, 0, s_kT)
                transposed(1, 1, s_kT)
                if not (isinstance(i, int) and i == 0):
                    pe.wait_ge(s_x3, i)
                transposed(0, 0, s_qT)
                pe.wait_ge(s_kTc, i * 2 + 1)
                transposed(0, 1, s_qT)

            def maximum(i, m):
                c, h0, nh = MAX_ITEMS[m]
                w = (c + 1) * P
                b0 = 2 + 2 * (m % 2)
                if m == 0:
                    pe.wait_ge(s_kTc, i * 2 + 2)
                    pe.wait_ge(s_qTe, i * 2 + 2)
                    pe.wait_ge(s_qTo, i * 2 + 2)
                if m >= 2:
                    pe.wait_ge(s_Sc, i * NMAX + (m - 1))
                for b in range(2):
                    each = [(h0 + b * (nh // 2) + k, k * w) for k in range(nh // 2)]
                    for h, at in each:
                        nc.tensor.matmul(ps[:, b0 + b, at:at + w], QT[:, h, cols_of(c)], KT[:, h // 2, 0:w],
                                         start=(at == 0), stop=False, skip_group_check=True)
                    for h, at in each:
                        last = nc.tensor.matmul(ps[:, b0 + b, at + c * P:at + w], idb[:], maskb[:, 0, :],
                                                start=False, stop=True, skip_group_check=True)
                last.then_inc(s_S, 1)

            def shift(i):
                pe.wait_ge(s_m3, i + 1)
                pe.nop(nofuse=True)
                for c in range(NC):
                    last = nc.tensor.transpose(mps[:, cols_of(c)], mb[:, c].rearrange("p a k h -> p (a k h)"), idb[:])
                last.then_inc(s_mT, 1)

            def pv(i, G, j):
                if j == 0:
                    if G >= 2:
                        pe.wait_ge(s_pvc, i * NHG + (G - 1))
                    pe.wait_ge(s_Tc, i * (HB * NTI) + (G + 1) * HG * NTI)
                for k in range(HG):
                    last = nc.tensor.matmul(ps[VC * k:VC * (k + 1), 6 + G % 2, j * P:N], va[:, j, G * HG + k, :],
                                            PT[:, G % 2, k, KEY_AT[j]:KEY_AT[j] + N - j * P], start=(j == 0), stop=(j == NC - 1),
                                            skip_group_check=True)
                if j == NC - 1:
                    last.then_inc(s_pv, 1)

            def heads(i):
                pe.wait_ge(s_mTc, i + 1)
                pe.wait_ge(s_mq, i * 96 + 96)
                for h in range(HB):
                    for k in range(NTI):
                        n_ = h * NTI + k
                        if n_ >= 4:
                            pe.wait_ge(s_Tc, i * (HB * NTI) + (n_ - 3))
                        bank = 2 + n_ % 4
                        for m, (j, at, w) in enumerate(T_ITEMS[k]):
                            nc.tensor.matmul(ps[:, bank, at:at + w], KT[:, h // 2, cols_of(j)], QT[:, h, j * P:N],
                                             start=(m == 0), stop=False, skip_group_check=True)
                        for m, (j, at, w) in enumerate(T_ITEMS[k]):
                            last = nc.tensor.matmul(ps[:, bank, at:at + P], idb[:], maskb[:, 1, :],
                                                    start=False, stop=True, skip_group_check=True)
                        last.then_inc(s_T, 1)
                    if h > HG:
                        G = h // HG - 1
                        for j in {1: (0,), 2: (1,), 3: (2, 3)}.get(h % HG, ()):
                            pv(i, G, j)
                for j in range(NC):
                    pv(i, NHG - 1, j)

            def gather(i):
                pe.wait_ge(s_pvc, i * NHG + NHG)
                for c in range(NC):
                    for G in range(NHG):
                        last = nc.tensor.transpose(ps[:, 2 + c, cols_of(G)], oTs[:, G, cols_of(c)], idf[:])
                last.then_inc(s_oB, 1)
                pe.wait_ge(s_o2, i + 1)
                for c in range(NC):
                    last = nc.tensor.transpose(ps[:, 7, cols_of(c)], o2[:, c, :], idf[:])
                last.then_inc(s_o2T, 1)

            def output(i):
                pe.wait_ge(s_o2Tc, i + 1)
                for c in range(NC):
                    last = nc.tensor.matmul(ps[:, 6, cols_of(c)], o2T[:, cols_of(c)], wp[:], start=True, stop=True)
                last.then_inc(s_y, 1)

            def attn(part, i, m=None):
                if part == "rows":
                    rows(i)
                elif part == "project":
                    project(i)
                elif part == "transpose":
                    transpose(i)
                elif part == "max":
                    maximum(i, m)
                elif part == "shift":
                    shift(i)
                elif part == "heads":
                    heads(i)
                elif part == "gather":
                    gather(i)
                elif part == "out":
                    output(i)

            batches(pe, mlp, attn)


_INS = ["L0_attn_a_x", "L0_attn_a_w_qkv", "L0_attn_a_w_out", "L0_attn_a_ln_g", "L0_attn_a_ln_b", "L0_attn_a_mem_beta",
        "L0_attn_b_w_qkv", "L0_attn_b_w_proj", "L0_attn_b_b_proj", "L0_ffn_ln_g", "L0_ffn_ln_b", "L0_ffn_attn_w",
        "L0_ffn_attn_b", "L0_ffn_w1", "L0_ffn_b1", "L0_ffn_w2", "L0_ffn_b2", "L0_ffn_next_w", "L0_ffn_next_b"]
MASKED = -1e30


def shape_constants():
    f32 = np.float32
    freq = (f32(10000.0) ** (-np.arange(0, DA, 2, dtype=f32) / f32(DA))).astype(f32)
    angle = np.arange(N, dtype=f32)[:, None] * freq
    cos_a = np.repeat(np.cos(angle), 2, -1)
    sin_a = np.repeat(np.sin(angle), 2, -1) * np.tile(np.array([-1, 1], f32), DA // 2)

    def by_tile(t):
        return np.ascontiguousarray(np.tile(t.reshape(NSEG, SEG, DA).transpose(1, 0, 2), (BG, 1, 1)), dtype=f32)

    seg = np.arange(SEG)
    seg_mask = np.tile(np.where(seg[None] > seg[:, None], f32(MASKED), f32(0)), (BG, HP))
    freq_b = (f32(1.0) / f32(10000.0) ** (np.arange(0, DB, 2, dtype=f32) / f32(DB))).astype(f32)
    angle_b = np.arange(N, dtype=f32)[:, None] * freq_b
    cos_b = np.concatenate([np.cos(angle_b), np.cos(angle_b)], -1)
    sin_b = np.concatenate([-np.sin(angle_b), np.sin(angle_b)], -1)

    def by_chunk(t):
        return np.ascontiguousarray(t.reshape(NC, P, DB).transpose(1, 0, 2), dtype=f32)

    row = np.arange(P)
    causal = np.where(row[None] > row[:, None], f32(MASKED), f32(0))
    return {"rope_cos_a": by_tile(cos_a), "rope_sin_a": by_tile(sin_a), "seg_mask": seg_mask.astype(f32),
            "rope_cos_b": by_chunk(cos_b), "rope_sin_b": by_chunk(sin_b),
            "causal": np.ascontiguousarray(np.stack([causal, causal.T], 1)), "ident": np.eye(P, dtype=f32)}


def kernel(**inputs):
    import concourse.bacc as bacc
    from concourse.bass_utils import run_bass_kernel_spmd

    nc = bacc.Bacc("TRN2", target_bir_lowering=False, num_devices=1)
    arrays, ap = {}, {}
    for name, a in [(n, np.ascontiguousarray(inputs[n])) for n in _INS] + list(shape_constants().items()):
        arrays[f"in_{name}_dram"] = a
        ap[name] = nc.dram_tensor(f"in_{name}_dram", a.shape, mybir.dt.from_np(a.dtype), kind="ExternalInput").ap()
    x1 = nc.dram_tensor("x1_dram", (B, N, D), F32).ap()
    out = nc.dram_tensor("out_0_dram", (B, N, D), F32, kind="ExternalOutput").ap()
    a, b, f = "L0_attn_a_", "L0_attn_b_", "L0_ffn_"
    attn_a_layer(nc, ap[a + "x"], ap[a + "w_qkv"], ap[a + "w_out"], ap[a + "ln_g"], ap[a + "ln_b"], ap[a + "mem_beta"],
                 ap["rope_cos_a"], ap["rope_sin_a"], ap["seg_mask"], ap["ident"], x1)
    mlp_attn_mlp_layers(nc, x1, ap[b + "w_qkv"], ap[b + "w_proj"], ap[b + "b_proj"], ap[f + "ln_g"], ap[f + "ln_b"],
                        ap[f + "attn_w"], ap[f + "attn_b"], ap[f + "w1"], ap[f + "b1"], ap[f + "w2"], ap[f + "b2"],
                        ap[f + "next_w"], ap[f + "next_b"], ap["rope_cos_b"], ap["rope_sin_b"], ap["causal"], ap["ident"], out)
    r = run_bass_kernel_spmd(nc, [arrays], core_ids=[0])
    return r.results[0]["out_0_dram"]
```

```python
from contextlib import ExitStack

import concourse.bass as bass
import numpy as np
from concourse import mybir

F32 = mybir.dt.float32
BF16 = mybir.dt.bfloat16
ALU = mybir.AluOpType
ACT = mybir.ActivationFunctionType
AX = mybir.AxisListType

P = 128
B, N, D = 16, 512, 128
EPS = 1e-5

HA, DA, SEG = 16, 64, 32
NSEG = N // SEG
BG = P // SEG
NG = B // BG
NT = NG * NSEG
HP = HA // 2
INNER = HA * DA
MC = DA + 1


def attn_a_layer(nc, x, w_qkv, w_out, ln_g, ln_b, mem_beta, rope_cos, rope_sin, seg_mask, ident, x1):
    ctx = ExitStack()
    with ctx:
        def sb(name, shape, dt=F32):
            return ctx.enter_context(nc.sbuf_tensor(name, shape, dt))

        def sem(name):
            return ctx.enter_context(nc.semaphore(name))

        xin = sb("a_xin", [P, NG, D])
        xout = sb("a_xout", [P, NG, D])
        stats = sb("a_stats", [P, NG, 6])
        mv = sb("a_mv", [P, NG, 2])
        rs = sb("a_rs", [P, NG])
        vs = sb("a_vs", [P, NG])
        half = sb("a_half", [P, 1])
        wq = sb("a_wqkv", [P, 3 * INNER])
        wo = sb("a_wout", [P, HP, D])
        gcol = sb("a_gcol", [P, 1])
        bcol = sb("a_bcol", [P, 1])
        beta = sb("a_beta", [P, HA])
        ombeta = sb("a_ombeta", [P, HA])
        bexp = sb("a_bexp", [P, HA])
        cosb = sb("a_cos", [P, NSEG, DA])
        sinb = sb("a_sin", [P, NSEG, DA])
        idf = sb("a_idf", [P, P])
        idb = sb("a_idb", [P, P], BF16)
        maskf = sb("a_maskf", [P, HP * SEG])
        maskb = sb("a_maskb", [P, HA * SEG], BF16)
        xhat = sb("a_xhat", [P, D])
        xnT = sb("a_xnT", [P, P])
        rc = sb("a_rc", [P, 2, INNER])
        rn = sb("a_rn", [P, 2, INNER])
        ex = sb("a_ex", [P, 2, INNER])
        sq = sb("a_sq", [P, INNER])
        sk = sb("a_sk", [P, 2, INNER])
        v = sb("a_v", [P, 2, INNER])
        qT = sb("a_qT", [P, HP, P])
        kT = sb("a_kT", [P, HP, BG, 2, SEG])
        sT = sb("a_sT", [P, 2, HP, P])
        ssub = sb("a_ssub", [P, HA, SEG])
        pe_ = sb("a_pe", [P, HA, SEG])
        pn = sb("a_pn", [P, HA * SEG])
        pT = sb("a_pT", [P, HA, P])
        mx = sb("a_mx", [P, HA])
        psum_ = sb("a_psum", [P, HA])
        pr = sb("a_pr", [P, HA])
        prs = sb("a_prs", [P, HA])
        mem = sb("a_mem", [P, NG, HP, BG, 2 * MC])
        ubd = sb("a_ubd", [P, BG, HA, MC])
        rdk = sb("a_rdk", [P, HA])
        dq = sb("a_dq", [P, 3, HA])
        pv_ = sb("a_prevv", [P, INNER])
        on = sb("a_on", [P, INNER])
        oT = sb("a_oT", [P, HP, P])
        y = sb("a_y", [P, 2, D])
        ps = ctx.enter_context(nc.psum_tensor("a_ps", [P, 8, 512], F32))

        s_const, s_late, s_fill = sem("a_const"), sem("a_late"), sem("a_fill")
        s_x = [sem(f"a_x{g}") for g in range(NG)]
        s_st = [sem(f"a_st{g}") for g in range(NG)]
        s_beta, s_set = sem("a_beta_s"), sem("a_set")
        s_clear = [sem("a_clear0"), sem("a_clear1")]
        s_stats, s_mv, s_vs, s_rs = sem("a_stats_s"), sem("a_mv_s"), sem("a_vs_s"), sem("a_rs_s")
        s_xhat, s_xT, s_xnT = sem("a_xhat_s"), sem("a_xT_s"), sem("a_xnT_s")
        s_q, s_k, s_v, s_vc = sem("a_q_s"), sem("a_k_s"), sem("a_v_s"), sem("a_vc_s")
        s_rq, s_rk = sem("a_rq_s"), sem("a_rk_s")
        s_qr, s_kr = sem("a_qr_s"), sem("a_kr_s")
        s_nq, s_nk = sem("a_nq_s"), sem("a_nk_s")
        s_relu = [sem("a_reluq_s"), sem("a_reluk_s")]
        s_exq, s_exk, s_sq, s_sk = sem("a_exq_s"), sem("a_exk_s"), sem("a_sq_s"), sem("a_sk_s")
        s_tqr, s_tkr, s_tsq, s_tsk = sem("a_tqr_s"), sem("a_tkr_s"), sem("a_tsq_s"), sem("a_tsk_s")
        s_qrT, s_krT, s_sqT, s_skT = sem("a_qrT_s"), sem("a_krT_s"), sem("a_sqT_s"), sem("a_skT_s")
        s_S, s_mx, s_sub, s_pe, s_sum, s_prs, s_pn, s_pT = (sem(f"a_{n}_s") for n in ("S", "mx", "sub", "pe", "sum", "prs", "pn", "pT"))
        s_prev, s_rdk, s_tk, s_u, s_ubd01, s_ubd2, s_ubd3 = (sem(f"a_{n}_s") for n in ("prev", "rdk", "tk", "u", "ubd01", "ubd2", "ubd3"))
        s_num, s_dq, s_on = (sem(f"a_{n}_s") for n in ("num", "dq", "on"))
        s_dm, s_mem = sem("a_dm_s"), sem("a_mem_s")
        s_oTp, s_oT, s_y, s_x1 = (sem(f"a_{n}_s") for n in ("oTp", "oT", "y", "x1"))

        def heads(ap):
            return ap.rearrange("p (h d) -> p h d", h=HA)

        def pair(ap, hp):
            return ap[:, hp * P:(hp + 1) * P]

        def wide(b0):
            return ps[:, b0:b0 + 2, :].rearrange("p b c -> p (b c)")

        def mem_read(b0):
            return ps[:, b0:b0 + 4, 0:4 * MC].rearrange("p b (c m) -> p b c m", m=MC)

        def read_by(b0, scale, out):
            return nc.vector.tensor_tensor(out.rearrange("p (b c m) -> p b c m", b=4, c=4), mem_read(b0)[:, :, :, 0:DA],
                                           scale.rearrange("p (b c) -> p b c", b=4).unsqueeze(3).broadcast_to([P, 4, 4, DA]), ALU.mult)

        UPDATE_BANKS = (6, 4, 4, 6)

        def by_head(ap, n):
            return ap.unsqueeze(2).broadcast_to([P, HA, n])

        def clear_memory(eng, ns, half_):
            gs = slice(half_ * NG // 2, (half_ + 1) * NG // 2)
            ns.memset(mem[:, gs], 0.0).then_inc(s_clear[half_], 1)
            for a in range(2):
                eng.wait_ge(s_clear[half_], a + 1)
                ns.memset(mem[DA * a:DA * (a + 1), gs, :, :, (a + 1) * MC - 1:(a + 1) * MC].rearrange("p g h b m -> p (g h b) m"),
                          1e-6).then_inc(s_clear[half_], 1)

        block = ctx.enter_context(nc.Block())

        def run(both, stage_a, stage_b, eng):
            stage_a(0, 0, 0)
            with eng.Fori(0, NSEG - 1) as s:
                for g in range(NG):
                    t = s * NG + g
                    both(t, g, s, t + 1, (g + 1) % NG, s if g + 1 < NG else s + 1, 2)
            for g in range(NG - 1):
                t = (NSEG - 1) * NG + g
                both(t, g, NSEG - 1, t + 1, g + 1, NSEG - 1, min(NT - 2 - t, 2))
            stage_b(NT - 1, NG - 1, NSEG - 1)

        @block.sync
        def _(sp):
            def rows_of(ap, g, s):
                return ap[g * BG:(g + 1) * BG, bass.ds(s * SEG, SEG) if not isinstance(s, int) else slice(s * SEG, (s + 1) * SEG), :]

            def load(g, s):
                sp.dma_start(xin[:, g, :], rows_of(x, g, s)).then_inc(s_x[g], 16)

            def store(t, g, s):
                sp.wait_ge(s_x1, t + 2)
                sp.dma_start(rows_of(x1, g, s), xout[:, g, :]).then_inc(s_st[g], 16)

            load(0, 0)
            for dst, src in ((idf, ident), (maskf, seg_mask), (wq, w_qkv)):
                sp.dma_start(dst[:], src).then_inc(s_const, 16)
            sp.dma_start(beta[:], mem_beta.rearrange("a h b c -> (a b c) h").broadcast_to([P, HA])).then_inc(s_const, 16)
            sp.dma_start(gcol[:], ln_g.rearrange("(p a) -> p a", a=1)).then_inc(s_const, 16)
            sp.dma_start(bcol[:], ln_b.rearrange("(p a) -> p a", a=1)).then_inc(s_const, 16)
            for dst, src in ((cosb, rope_cos), (sinb, rope_sin)):
                sp.dma_start(dst[:], src).then_inc(s_late, 16)
            sp.dma_start(wo[:], w_out.rearrange("(h p) d -> p h d", p=P)).then_inc(s_late, 16)
            for g in range(1, NG):
                load(g, 0)
            with sp.Fori(0, NSEG - 1) as s:
                for g in range(NG):
                    store(s * NG + g, g, s)
                    load(g, s + 1)
            for g in range(NG):
                store((NSEG - 1) * NG + g, g, NSEG - 1)
            for g in range(NG):
                sp.wait_ge(s_st[g], 16 * NSEG + 16)

        CONST_ALL = 16 * 6
        LATE_ALL = 16 * 3

        @block.vector
        def _(dve):
            nc.vector.memset(half[:], -0.5).then_inc(s_set, 1)
            for zero in (kT, pT):
                nc.vector.memset(zero[:], 0.0).then_inc(s_fill, 1)
            nc.vector.memset(mx[:], 0.0).then_inc(s_x1, 1)
            for g in range(NG):
                nc.vector.memset(xout[:, g, :], 0.0).then_inc(s_st[g], 16)
            dve.wait_ge(s_const, CONST_ALL)
            nc.vector.tensor_copy(idb[:], idf[:]).then_inc(s_set, 1)
            for a in range(2):
                nc.vector.tensor_copy(maskb[:, a * HP * SEG:(a + 1) * HP * SEG], maskf[:]).then_inc(s_set, 1)
            dve.wait_ge(s_beta, 1)
            nc.vector.tensor_scalar(bexp[:], bexp[:], 1.0, None, ALU.add).then_inc(s_beta, 1)
            dve.wait_ge(s_beta, 2)
            nc.vector.reciprocal(beta[:], bexp[:]).then_inc(s_beta, 1)
            dve.wait_ge(s_beta, 3)
            nc.vector.tensor_scalar(ombeta[:], beta[:], -1.0, 1.0, ALU.mult, ALU.add).then_inc(s_beta, 1)
            dve.wait_ge(s_beta, 4)

            def fill():
                nc.vector.memset(ubd[:], 0.0).then_inc(s_fill, 1)
                dve.wait_ge(s_fill, 3)
                for b in range(BG):
                    nc.vector.memset(ubd[SEG * b:SEG * (b + 1), b, :, DA:MC], 1.0).then_inc(s_fill, 1)

            def row_stats(t, g, s):
                dve.wait_ge(s_x[g], s * 16 + 16)
                dve.nop(nofuse=True)
                nc.vector.bn_stats(stats[:, g, :], xin[:, g, :]).then_inc(s_stats, 1)
                dve.wait_ge(s_stats, t + 1)
                dve.nop(nofuse=True)
                nc.vector.bn_aggr(mv[:, g, :], stats[:, g, :]).then_inc(s_mv, 1)

            def make_xhat(t, g):
                dve.wait_ge(s_rs, t + 1)
                nc.vector.tensor_scalar(xhat[:], xin[:, g, :], mv[:, g, 0:1], rs[:, g:g + 1],
                                        ALU.subtract, ALU.mult).then_inc(s_xhat, 1)

            def rope_products(i, s, t):
                src = wide(2 * i)
                cos, sin = cosb[:, s, :], sinb[:, s, :]
                dve.wait_ge(s_relu[i], t + 1)
                nc.vector.tensor_tensor(heads(rc[:, i, :]), heads(src), cos.unsqueeze(1).broadcast_to([P, HA, DA]), ALU.mult)
                for e in range(2):
                    def every(ap, k):
                        return ap.rearrange("p (h d e) -> p h d e", h=HA, e=2)[:, :, :, k]
                    sn = sin.rearrange("p (d e) -> p d e", e=2)[:, :, e].unsqueeze(1).broadcast_to([P, HA, DA // 2])
                    last = nc.vector.tensor_tensor(every(rn[:, i, :], e), every(src, 1 - e), sn, ALU.mult)
                last.then_inc((s_rq, s_rk)[i], 1)

            def softmax_head(t):
                S = ps[:, 2, :].rearrange("p (h m) -> p h m", m=SEG)
                dve.wait_ge(s_S, t + 1)
                nc.vector.tensor_reduce(mx[:], S, AX.X, ALU.max).then_inc(s_mx, 1)
                dve.wait_ge(s_mx, t + 1)
                nc.vector.tensor_tensor(ssub[:], S, by_head(mx[:], SEG), ALU.subtract).then_inc(s_sub, 1)

            def softmax_sum(t):
                dve.wait_ge(s_pe, t + 1)
                nc.vector.tensor_reduce(psum_[:], pe_[:], AX.X, ALU.add).then_inc(s_sum, 1)
                dve.wait_ge(s_sum, t * 2 + 1)
                nc.vector.reciprocal(pr[:], psum_[:]).then_inc(s_sum, 1)
                dve.wait_ge(s_sum, t * 2 + 2)
                nc.vector.tensor_tensor(prs[:], pr[:], ombeta[:], ALU.mult).then_inc(s_prs, 1)

            def transpose_p(t):
                dve.wait_ge(s_pn, t + 1)
                for b in range(BG):
                    rows = slice(SEG * b, SEG * (b + 1))
                    last = nc.vector.transpose(pT[rows, :, rows], pn[rows, :].rearrange("p (h m) -> p h m", m=SEG))
                last.then_inc(s_pT, 1)

            def spread_u(t):
                dve.wait_ge(s_u, t + 1)
                for b in (0, 1):
                    rows = slice(SEG * b, SEG * (b + 1))
                    last = nc.vector.tensor_copy(ubd[rows, b, :, 0:DA], heads(pv_[rows, :]))
                last.then_inc(s_ubd01, 1)

            def read_prev(t):
                R = mem_read(0)
                dve.wait_ge(s_prev, t + 1)
                nc.vector.reciprocal(rdk[:].rearrange("p (b c) -> p b c", b=4), R[:, :, :, DA]).then_inc(s_rdk, 1)
                dve.wait_ge(s_rdk, t + 1)
                read_by(0, rdk[:], pv_[:]).then_inc(s_tk, 1)

            def read_num(t):
                R = mem_read(4)
                dve.wait_ge(s_num, t + 1)
                nc.vector.tensor_scalar(dq[:, 0, :].rearrange("p (b c) -> p b c", b=4), R[:, :, :, DA], 1e-6, None,
                                        ALU.add).then_inc(s_dq, 1)
                dve.wait_ge(s_dq, t * 3 + 1)
                nc.vector.reciprocal(dq[:, 1, :], dq[:, 0, :]).then_inc(s_dq, 1)
                dve.wait_ge(s_dq, t * 3 + 2)
                nc.vector.tensor_tensor(dq[:, 2, :], dq[:, 1, :], beta[:], ALU.mult).then_inc(s_dq, 1)
                dve.wait_ge(s_dq, t * 3 + 3)
                read_by(4, dq[:, 2, :], on[:]).then_inc(s_on, 1)

            def add_mem(t, g, half_):
                for k in (2 * half_, 2 * half_ + 1):
                    dve.wait_ge(s_dm, t * 4 + (k + 1))
                    for a in range(2):
                        rows = slice(DA * a, DA * (a + 1))
                        m = mem[rows, g, 2 * k:2 * k + 2, :, a * MC:(a + 1) * MC]
                        b0 = UPDATE_BANKS[k]
                        last = nc.vector.tensor_tensor(m, ps[rows, b0:b0 + 2, 0:BG * MC].rearrange("p h (b m) -> p h b m", m=MC), m,
                                                       ALU.add)
                    last.then_inc(s_mem, 1)

            def add_x(t, g, s):
                dve.wait_ge(s_y, t + 1)
                dve.wait_ge(s_st[g], s * 16 + 16)
                nc.vector.tensor_tensor(xout[:, g, :], ps[:, 5, 3 * P:], xin[:, g, :], ALU.add).then_inc(s_x1, 1)

            def stage_a(t, g, s):
                row_stats(t, g, s)
                make_xhat(t, g)
                fill()
                row_stats(t + 1, g + 1, s)
                dve.wait_ge(s_late, LATE_ALL)
                rope_products(0, s, t)
                rope_products(1, s, t)
                make_xhat(t + 1, g + 1)
                row_stats(t + 2, g + 2, s)
                softmax_head(t)
                softmax_sum(t)

            def stage_b(t, g, s):
                read_num(t)
                read_prev(t)
                transpose_p(t)
                spread_u(t)
                add_mem(t, g, 0)
                add_x(t, g, s)
                add_mem(t, g, 1)

            def both(t, g, s, tn, gn, sn, ahead):
                read_num(t)
                read_prev(t)
                if ahead:
                    make_xhat(tn + 1, (g + 2) % NG)
                transpose_p(t)
                spread_u(t)
                rope_products(0, sn, tn)
                rope_products(1, sn, tn)
                add_mem(t, g, 0)
                add_x(t, g, s)
                add_mem(t, g, 1)
                if ahead == 2:
                    row_stats(tn + 2, (g + 3) % NG, s if g + 3 < NG else s + 1)
                softmax_head(tn)
                softmax_sum(tn)

            run(both, stage_a, stage_b, dve)

        @block.gpsimd
        def _(pool):
            clear_memory(pool, nc.gpsimd, 0)
            pool.wait_ge(s_clear[0], 3)
            pool.wait_ge(s_set, 1)

            def layernorm_scale(t, g):
                pool.wait_ge(s_mv, t + 1)
                pool.nop(nofuse=True)
                nc.gpsimd.tensor_scalar(vs[:, g:g + 1], mv[:, g, 1:2], 1.0 + EPS, EPS * EPS, ALU.mult, ALU.add).then_inc(s_vs, 1)
                pool.wait_ge(s_vs, t + 1)
                nc.gpsimd.tensor_tensor(rs[:, g:g + 1], vs[:, g:g + 1], half[:], ALU.pow).then_inc(s_rs, 1)

            def rope_sum(i, t):
                pool.wait_ge((s_rq, s_rk)[i], t + 1)
                nc.gpsimd.tensor_tensor(rc[:, i, :], rc[:, i, :], rn[:, i, :], ALU.add).then_inc((s_qr, s_kr)[i], 1)

            def elu(i, t, par):
                pool.wait_ge(s_relu[i], t + 1)
                pool.wait_ge((s_exq, s_exk)[i], t + 1)
                pool.nop(nofuse=True)
                to = sk[:, par, :] if i else sq[:]
                nc.gpsimd.tensor_tensor(to, ex[:, i, :], to, ALU.add).then_inc((s_sq, s_sk)[i], 1)

            def scale_p(t):
                pool.wait_ge(s_prs, t + 1)
                nc.gpsimd.tensor_tensor(pn[:].rearrange("p (h m) -> p h m", h=HA), pe_[:], by_head(prs[:], SEG),
                                        ALU.mult).then_inc(s_pn, 1)

            def make_u(t, g):
                pool.wait_ge(s_tk, t + 1)
                pool.wait_ge(s_vc, t + 1)
                nc.gpsimd.tensor_tensor(pv_[:], v[:, g % 2, :], pv_[:], ALU.subtract).then_inc(s_u, 1)
                pool.wait_ge(s_u, t + 1)
                pool.nop(nofuse=True)
                rows = slice(3 * SEG, P)
                nc.gpsimd.tensor_copy(ubd[rows, 3, :, 0:DA], heads(pv_[rows, :])).then_inc(s_ubd3, 1)
                pool.wait_ge(s_ubd3, t + 1)

            def stage_a(t, g, s):
                layernorm_scale(t, g)
                clear_memory(pool, nc.gpsimd, 1)
                pool.wait_ge(s_clear[1], 3)
                layernorm_scale(t + 1, g + 1)
                rope_sum(0, t)
                rope_sum(1, t)
                elu(0, t, g % 2)
                elu(1, t, g % 2)
                layernorm_scale(t + 2, g + 2)
                scale_p(t)
                pool.wait_ge(s_fill, 3 + BG)

            def stage_b(t, g, s):
                make_u(t, g)

            def both(t, g, s, tn, gn, sn, ahead):
                make_u(t, g)
                rope_sum(0, tn)
                rope_sum(1, tn)
                elu(0, tn, gn % 2)
                elu(1, tn, gn % 2)
                if ahead == 2:
                    layernorm_scale(tn + 2, (g + 3) % NG)
                scale_p(tn)

            run(both, stage_a, stage_b, pool)

        @block.scalar
        def _(act):
            act.wait_ge(s_const, CONST_ALL)
            nc.scalar.activation(bexp[:], beta[:], ACT.Exp, scale=-1.0).then_inc(s_beta, 1)

            def keep_xnT(t):
                act.wait_ge(s_xT, t + 1)
                nc.scalar.activation(xnT[:], ps[:, 3, 0:P], ACT.Identity, bias=bcol[:], scale=gcol[:]).then_inc(s_xnT, 1)

            def relus(i, t, par):
                act.wait_ge((s_q, s_k)[i], t + 1)
                nc.scalar.activation(ex[:, i, :], wide(2 * i), ACT.Relu, scale=-1.0).then_inc((s_nq, s_nk)[i], 1)
                nc.scalar.activation(sk[:, par, :] if i else sq[:], wide(2 * i), ACT.Relu).then_inc(s_relu[i], 1)

            def negative_exp(i, t):
                act.wait_ge((s_nq, s_nk)[i], t + 1)
                nc.scalar.activation(ex[:, i, :], ex[:, i, :], ACT.Exp, scale=-1.0).then_inc((s_exq, s_exk)[i], 1)

            def keep_v(t, par):
                act.wait_ge(s_v, t + 1)
                nc.scalar.activation(v[:, par, :], wide(6), ACT.Copy).then_inc(s_vc, 1)

            def keep_ropes(t):
                act.wait_ge(s_tqr, t + 1)
                nc.scalar.activation(qT[:].rearrange("p h c -> p (h c)"), wide(0), ACT.Copy).then_inc(s_qrT, 1)
                act.wait_ge(s_tkr, t + 1)
                for a in range(2):
                    rows = slice(DA * a, DA * (a + 1))
                    last = nc.scalar.activation(kT[rows, :, :, a, :].rearrange("p h b m -> p (h b) m"),
                                                wide(2)[rows].rearrange("p (c m) -> p c m", m=SEG), ACT.Copy)
                last.then_inc(s_krT, 1)

            def keep_eluT(i, t):
                act.wait_ge((s_tsq, s_tsk)[i], t + 1)
                nc.scalar.activation(sT[:, i].rearrange("p h c -> p (h c)"), wide(0), ACT.Copy).then_inc((s_sqT, s_skT)[i], 1)

            def exp(t):
                act.wait_ge(s_sub, t + 1)
                nc.scalar.activation(pe_[:], ssub[:], ACT.Exp, scale=float(DA) ** -0.5).then_inc(s_pe, 1)

            def spread_u(t):
                act.wait_ge(s_u, t + 1)
                rows = slice(2 * SEG, 3 * SEG)
                nc.scalar.activation(ubd[rows, 2, :, 0:DA], heads(pv_[rows, :]), ACT.Copy).then_inc(s_ubd2, 1)

            def keep_oT(t):
                act.wait_ge(s_oTp, t + 1)
                nc.scalar.activation(oT[:].rearrange("p h c -> p (h c)"), wide(4), ACT.Copy).then_inc(s_oT, 1)

            def stage_a(t, g, s):
                keep_xnT(t)
                relus(0, t, g % 2)
                relus(1, t, g % 2)
                keep_v(t, g % 2)
                negative_exp(0, t)
                negative_exp(1, t)
                act.wait_ge(s_fill, 3 + BG)
                keep_ropes(t)
                keep_xnT(t + 1)
                keep_eluT(0, t)
                exp(t)
                keep_eluT(1, t)

            def stage_b(t, g, s):
                spread_u(t)
                keep_oT(t)

            def both(t, g, s, tn, gn, sn, ahead):
                keep_v(tn, gn % 2)
                relus(0, tn, gn % 2)
                relus(1, tn, gn % 2)
                spread_u(t)
                keep_oT(t)
                negative_exp(0, tn)
                negative_exp(1, tn)
                keep_ropes(tn)
                keep_eluT(0, tn)
                if ahead:
                    keep_xnT(tn + 1)
                exp(tn)
                keep_eluT(1, tn)

            run(both, stage_a, stage_b, act)

        @block.tensor
        def _(pe):
            pe.wait_ge(s_const, CONST_ALL)
            pe.wait_ge(s_set, 4)

            def transposes(src, b0, sem_):
                for hp in range(HP):
                    last = nc.tensor.transpose(ps[:, b0 + hp // 4, P * (hp % 4):P * (hp % 4 + 1)], pair(src, hp), idf[:])
                last.then_inc(sem_, 1)

            def transpose_x(t):
                pe.wait_ge(s_xhat, t + 1)
                nc.tensor.transpose(ps[:, 3, 0:P], xhat[:], idf[:]).then_inc(s_xT, 1)

            def project(i, b0, sem_):
                for j in range(2):
                    c = i * INNER + j * 512
                    last = nc.tensor.matmul(ps[:, b0 + j, :], xnT[:], wq[:, c:c + 512], start=True, stop=True)
                last.then_inc(sem_, 1)

            def project_qk(t):
                project(0, 0, s_q)
                project(1, 2, s_k)

            def project_v(t):
                pe.wait_ge(s_xnT, t + 1)
                project(2, 6, s_v)

            def read_memory(i, t, g, b0, sem_):
                for hp in range(HP):
                    for b in range(BG):
                        rows = slice(SEG * b, SEG * (b + 1))
                        last = nc.tensor.matmul(ps[rows, b0 + hp // 2, (hp % 2) * 2 * MC:(hp % 2 + 1) * 2 * MC],
                                                sT[:, i, hp, rows], mem[:, g, hp, b, :],
                                                start=(hp % 2 == 0), stop=True, skip_group_check=True)
                last.then_inc(sem_, 1)

            def attend(t, g):
                pe.wait_ge(s_on, t + 1)
                for hp in range(HP):
                    nc.tensor.matmul(ps[:, 4 + hp // 4, P * (hp % 4):P * (hp % 4 + 1)], pair(on, hp), idf[:],
                                     start=(hp % 4 == 0), stop=False, is_transpose=True, skip_group_check=True)
                pe.wait_ge(s_pT, t + 1)
                for h in range(HA):
                    rows = slice(DA * (h % 2), DA * (h % 2 + 1))
                    hp = h // 2
                    last = nc.tensor.matmul(ps[rows, 4 + hp // 4, P * (hp % 4):P * (hp % 4 + 1)], v[:, g % 2, h * DA:(h + 1) * DA],
                                            pT[:, h, :], start=False, stop=True, skip_group_check=True)
                last.then_inc(s_oTp, 1)

            def update(t, g, half_, tv=None):
                if half_ == 0:
                    pe.wait_ge(s_ubd01, t + 1)
                    pe.wait_ge(s_ubd2, t + 1)
                    pe.wait_ge(s_ubd3, t + 1)
                    if tv is not None:
                        pe.wait_ge(s_vc, tv + 1)
                for k in (2 * half_, 2 * half_ + 1):
                    if k == 1:
                        output(t)
                    if half_:
                        pe.wait_ge(s_mem, t * 4 + 2)
                        pe.wait_ge(s_x1, t + 2)
                    for hp in (2 * k, 2 * k + 1):
                        for a in range(2):
                            h = 2 * hp + a
                            last = nc.tensor.matmul(ps[DA * a:DA * (a + 1), UPDATE_BANKS[k] + hp % 2, 0:BG * MC], sk[:, g % 2, h * DA:(h + 1) * DA],
                                                    ubd[:, :, h, :], start=True, stop=True)
                    last.then_inc(s_dm, 1)

            def transpose_rope(i, t):
                pe.wait_ge((s_qr, s_kr)[i], t + 1)
                transposes(rc[:, i, :], 2 * i, (s_tqr, s_tkr)[i])

            def transpose_elu(i, t, g):
                pe.wait_ge((s_sq, s_sk)[i], t + 1)
                transposes(sk[:, g % 2, :] if i else sq[:], 0, (s_tsq, s_tsk)[i])

            def scores(t):
                pe.wait_ge(s_krT, t + 1)
                nc.tensor.matmul(ps[:, 2, :], idb[:], maskb[:], start=True, stop=False, skip_group_check=True)
                for hp in range(HP):
                    for b in range(BG):
                        toks = slice(SEG * b, SEG * (b + 1))
                        last = nc.tensor.matmul(ps[toks, 2, hp * 2 * SEG:(hp + 1) * 2 * SEG], qT[:, hp, toks],
                                                kT[:, hp, b, :, :].rearrange("p a m -> p (a m)"), start=False, stop=True,
                                                skip_group_check=True)
                last.then_inc(s_S, 1)

            def output(t):
                pe.wait_ge(s_oT, t + 1)
                for hp in range(HP):
                    last = nc.tensor.matmul(ps[:, 5, 3 * P:], oT[:, hp, :], wo[:, hp, :], start=(hp == 0), stop=(hp == HP - 1))
                last.then_inc(s_y, 1)

            def stage_a(t, g, s):
                transpose_x(t)
                pe.wait_ge(s_xnT, t + 1)
                project_qk(t)
                project_v(t)
                for i in range(2):
                    transpose_rope(i, t)
                scores(t)
                transpose_x(t + 1)
                transpose_elu(0, t, g)
                pe.wait_ge(s_sqT, t + 1)
                transpose_elu(1, t, g)
                pe.wait_ge(s_vc, t + 1)
                for clear in s_clear:
                    pe.wait_ge(clear, 3)
                pe.wait_ge(s_fill, 3 + BG)
                pe.wait_ge(s_late, LATE_ALL)

            def read_num(t, g):
                pe.wait_ge(s_sqT, t + 1)
                pe.nop(nofuse=True)
                read_memory(0, t, g, 4, s_num)

            def read_prev(t, g):
                pe.wait_ge(s_xnT, (t + 1 if not isinstance(t, int) else min(t + 1, NT - 1)) + 1)
                pe.wait_ge(s_sub, t + 1)
                pe.wait_ge(s_skT, t + 1)
                pe.nop(nofuse=True)
                read_memory(1, t, g, 0, s_prev)

            def stage_b(t, g, s):
                read_num(t, g)
                read_prev(t, g)
                pe.wait_ge(s_on, t + 1)
                attend(t, g)
                update(t, g, 0)
                update(t, g, 1)

            def both(t, g, s, tn, gn, sn, ahead):
                read_num(t, g)
                read_prev(t, g)
                pe.wait_ge(s_on, t + 1)
                project_v(tn)
                pe.wait_ge(s_tk, t + 1)
                project_qk(tn)
                attend(t, g)
                update(t, g, 0, tn)
                transpose_rope(0, tn)
                transpose_rope(1, tn)
                update(t, g, 1)
                pe.wait_ge(s_qrT, tn + 1)
                transpose_elu(0, tn, gn)
                scores(tn)
                if ahead:
                    transpose_x(tn + 1)
                pe.wait_ge(s_sqT, tn + 1)
                transpose_elu(1, tn, gn)
                pe.wait_ge(s_mem, t * 4 + 4)

            run(both, stage_a, stage_b, pe)


NC = N // P
E = 8
DFF = 4 * D
NF = DFF // P
HB, DB = 16, 8
SPLIT = 6
SROW = SPLIT * DB
MROW = 3
HROW = 64
HG = 4
NHG = HB // HG
VC = 32
BANK = 512


def mlp_attn_mlp_layers(nc, x1, w_qkv, w_proj, b_proj, ln_g, ln_b, attn_w, attn_b, w1, b1, w2, b2,
                        next_w, next_b, rope_cos, rope_sin, causal, ident, out):
    ctx = ExitStack()
    with ctx:
        def sb(name, shape, dt=F32):
            return ctx.enter_context(nc.sbuf_tensor(name, shape, dt))

        def sem(name):
            return ctx.enter_context(nc.semaphore("b_" + name))

        X = sb("b_x", [P, B, NC, D])
        wb = sb("b_wqkv", [P, 3 * D])
        wp = sb("b_wproj", [P, D])
        wa = sb("b_attnw", [P, D])
        wn = sb("b_nextw", [P, D])
        bp = sb("b_bproj", [P, D])
        nb = sb("b_nextb", [P, D])
        NVEC = E * NF + E + 3
        vecs = sb("b_vecs", [NVEC, D])
        cols = sb("b_cols", [P, NVEC])
        C_B2, C_G, C_B, C_AB = E * NF, E * NF + E, E * NF + E + 1, E * NF + E + 2
        cosb = sb("b_cos", [P, NC, DB])
        sinb = sb("b_sin", [P, NC, DB])
        idf = sb("b_idf", [P, P])
        idb = sb("b_idb", [P, P], BF16)
        maskf = sb("b_maskf", [P, 2, P])
        maskb = sb("b_maskb", [P, 2, P], BF16)
        warm = sb("b_warm", [P, 1])
        half = sb("b_half", [P, NC])
        w1s = sb("b_w1", [P, 2, DFF])
        w2s = sb("b_w2", [P, 2, NF, D])
        fst = sb("b_fst", [P, NC, 6])
        fmv = sb("b_fmv", [P, NC, 2])
        ft = sb("b_ft", [P, 4, NC])
        z = sb("b_z", [P, NC, D])
        xl = sb("b_xl", [P, NC, D])
        xlT = sb("b_xlT", [P, N])
        xaT = sb("b_xaT", [P, N])
        hT = sb("b_hT", [P, NF, N])
        yT = sb("b_yT", [P, N])
        pre = sb("b_pre", [P, NC, D])
        fo = sb("b_fo", [P, NC, D])
        ast = sb("b_ast", [P, NC, 6])
        amv = sb("b_amv", [P, NC, 2])
        at_ = sb("b_at", [P, 2, NC])
        xn = sb("b_xn", [P, NC, D])
        xnT = sb("b_xnT", [P, N])
        qc = sb("b_qc", [P, NC, 2, HB, DB])
        qs = sb("b_qs", [P, NC, 2, HB, DB])
        r1 = sb("b_r1", [P, NC, 2, HB, DB])
        r2 = sb("b_r2", [P, NC, 2, HB, DB])
        st = sb("b_st", [P, NC, 2, HB, HROW], BF16)
        QT = sb("b_QT", [P, HB, N], BF16)
        KT = sb("b_KT", [P, HB // 2, N], BF16)
        va = sb("b_va", [P, NC, HB, VC])
        nm = sb("b_nm", [P, 3, NC, HB])
        mb = sb("b_mb", [P, 2, NC, 2, MROW, HB // 4], BF16)
        MB = 2 * MROW * HB // 4
        mT = sb("b_mT", [MB, 2, N], BF16)
        PT = sb("b_PT", [P, 2, HG, 1280])
        oTs = sb("b_oTs", [P, NHG, N])
        rec = sb("b_rec", [P, NC, HB])
        o2 = sb("b_o2", [P, NC, D])
        o2T = sb("b_o2T", [P, N])
        ps = ctx.enter_context(nc.psum_tensor("b_ps", [P, 8, BANK], F32))

        s_const, s_x, s_set, s_fill, s_cT, s_cols = (sem(n) for n in ("const", "x", "set", "fill", "cT", "cols"))
        s_w = [sem("w0"), sem("w1")]
        s_fst, s_fmv, s_frs, s_z, s_xl = (sem(n) for n in ("fst", "fmv", "frs", "z", "xl"))
        s_xlT, s_xlTc, s_xa, s_xac = (sem(n) for n in ("xlT", "xlTc", "xa", "xac"))
        s_h, s_hc = sem("h"), sem("hc")
        s_yT, s_yTc, s_fo, s_pre, s_foc, s_fx = (sem(n) for n in ("yT", "yTc", "fo", "pre", "foc", "fx"))
        s_ast, s_amv, s_ars, s_xn, s_xnT, s_xnTc = (sem(n) for n in ("ast", "amv", "ars", "xn", "xnT", "xnTc"))
        s_qkv, s_va, s_rp, s_rs, s_p1, s_r1, s_p2, s_r2, s_p3, s_p3a = (sem(n) for n in ("qkv", "va", "rp", "rs", "p1", "r1", "p2", "r2", "p3", "p3a"))
        s_kT, s_kTc, s_qT, s_qTe, s_qTo = (sem(n) for n in ("kT", "kTc", "qT", "qTe", "qTo"))
        s_S, s_Sc = sem("S"), sem("Sc")
        s_nm, s_m3, s_mT, s_mTc, s_mq = (sem(n) for n in ("nm", "m3", "mT", "mTc", "mq"))
        s_T, s_Tc, s_pv, s_pvc = (sem(n) for n in ("T", "Tc", "pv", "pvc"))
        s_oB, s_rec, s_o2, s_o2T, s_o2Tc, s_y, s_xb, s_x3 = (sem(n) for n in ("oB", "rec", "o2", "o2T", "o2Tc", "y", "xb", "x3"))
        s_out = sem("out")

        MAX_ITEMS = ([(c, h, nh, 2) for c, nh in ((3, 2), (2, 2), (1, 4), (0, 8)) for h in range(0, HB // 2, nh)]
                     + [(3, h, 2, 2) for h in range(HB // 2, HB, 2)] + [(2, h, 2, 2) for h in range(HB // 2, HB - 4, 2)]
                     + [(2, h, 1, 1) for h in range(HB - 4, HB)] + [(1, h, 2, 1) for h in range(HB // 2, HB, 2)]
                     + [(0, h, 4, 1) for h in range(HB // 2, HB, 4)])
        NMAX = len(MAX_ITEMS)
        MAX_HALF = 11
        MAX_LATE = NMAX - 10
        OVERLAP = 12
        MLP_AT = {1: 2, 2: 3, 4: 4, 5: 5, 6: 6, 7: 7, 9: 8, 10: 9, 11: 10, 12: 11, 14: 12}
        T_ITEMS = (((0, 0, 512),), ((1, 0, 384), (3, 384, 128)), ((2, 0, 256),))
        NTI = len(T_ITEMS)
        PT_AT = (0, 512, 1024)
        KEY_AT = {0: 0, 1: 512, 3: 896, 2: 1024}

        block = ctx.enter_context(nc.Block())

        def iteration(mlp, attn, i, first, second, nxt):
            def mlp_behind(*steps):
                if first is not None:
                    for step in steps:
                        mlp(step, 0, *first)

            def mlp_before(*steps):
                if second is not None:
                    for step in steps:
                        mlp(step, 1, *second)

            attn("rope", i)
            if second is not None:
                attn("add", i - 1)
            mlp_before(0)
            mlp_behind(4, 5)
            attn("part 1", i)
            mlp_behind(6, 7)
            attn("part 2", i)
            mlp_before(1)
            attn("part 3", i)
            mlp_behind(8, 9, 10, 11)
            attn("transpose", i)
            mlp_behind(12, 13)
            for m in range(MAX_LATE):
                attn("max", i, m)
                if m == MAX_HALF - 1:
                    attn("shift", i, 0)
                if m == MAX_HALF + 1:
                    attn("shift rows", i, 0)
                if m in MLP_AT:
                    mlp_before(MLP_AT[m])
            mlp_before(13)
            for n_ in range(HB * NTI):
                attn("scores", i, n_)
                if n_ < NMAX - MAX_LATE:
                    attn("max", i, MAX_LATE + n_)
                if n_ == OVERLAP:
                    attn("shift", i, 1)
                if n_ == OVERLAP + 3:
                    attn("shift rows", i, 1)
                if n_ % NTI == NTI - 1:
                    h = n_ // NTI
                    attn("outputs", i, h)
                    if first is not None and h == HG + 3:
                        attn("norm", i + 1, first[0])
                    if nxt is not None and h == 2 * HG + 2:
                        mlp(0, 0, *nxt)
                    if nxt is not None and h == 2 * HG + 3:
                        mlp(1, 0, *nxt)
            attn("last", i)
            if first is not None:
                attn("rows", i + 1)
            attn("gather", i)
            if nxt is not None:
                mlp(2, 0, *nxt)
            attn("output rows", i)
            if first is not None:
                attn("project", i + 1)
            if nxt is not None:
                mlp(3, 0, *nxt)
            attn("out", i)

        def batches(eng, mlp, attn):
            for step in range(14):
                mlp(step, 0, 0, 0, 0)
                if step == 1:
                    attn("fill", 0)
            attn("norm", 0, 0)
            attn("filled", 0)
            mlp(0, 0, 1, 1, 1)
            mlp(1, 0, 1, 1, 1)
            attn("rows", 0)
            mlp(2, 0, 1, 1, 1)
            attn("project", 0)
            mlp(3, 0, 1, 1, 1)
            iteration(mlp, attn, 0, (1, 1, 1), None, (2, 2, 0))
            with eng.Fori(1, B - 2) as i:
                iteration(mlp, attn, i, (i * 2, i + 1, 0), (i * 2 + 1, i - 1, 1), (i * 2 + 2, i + 2, 0))
            i = B - 2
            iteration(mlp, attn, i, (i * 2, i + 1, 0), (i * 2 + 1, i - 1, 1), None)
            i = B - 1
            iteration(mlp, attn, i, None, (i * 2, i - 1, 0), None)
            attn("add", i)
            for step in range(14):
                mlp(step, 1, 2 * B - 1, B - 1, 1)

        @block.sync
        def _(sp):
            sp.dma_start(X[:, 0], x1[0].rearrange("(c p) d -> p c d", p=P)).then_inc(s_x, 16)
            for dst, src in ((wb, w_qkv), (wp, w_proj), (wa, attn_w), (wn, next_w), (cosb, rope_cos), (sinb, rope_sin),
                             (idf, ident), (maskf, causal)):
                sp.dma_start(dst[:], src).then_inc(s_const, 16)
            for dst, src in ((bp, b_proj), (nb, next_b)):
                sp.dma_start(dst[:], src.unsqueeze(0).broadcast_to([P, D])).then_inc(s_const, 16)
            sp.dma_start(vecs[0:E * NF, :], b1.rearrange("e (j f) -> (e j) f", f=P)).then_inc(s_const, 16)
            sp.dma_start(vecs[C_B2:C_B2 + E, :], b2).then_inc(s_const, 16)
            for c, src in ((C_G, ln_g), (C_B, ln_b), (C_AB, attn_b)):
                sp.dma_start(vecs[c:c + 1, :], src.unsqueeze(0)).then_inc(s_const, 16)
            sp.dma_start(X[:, 1:B], x1[1:B].rearrange("b (c p) d -> p b c d", p=P)).then_inc(s_x, 16)

            def weights(n, e, par):
                if not (isinstance(n, int) and n < 2):
                    sp.wait_ge(s_yT, n - 1)
                sp.dma_start(w1s[:, par, :], w1[e]).then_inc(s_w[par], 16)
                sp.dma_start(w2s[:, par, :, :], w2[e].rearrange("(j f) d -> f j d", f=P)).then_inc(s_w[par], 16)

            def shift(i, half_):
                sp.wait_ge(s_mTc, i * 2 + (half_ + 1))
                for a in range(2):
                    row, of = HROW * a + SROW, a * (MB // 2)
                    sp.dma_start(QT[row:row + MROW, 8 * half_ + a:8 * half_ + 8:2, :],
                                 mT[of:of + MB // 2, half_, :]).then_inc(s_mq, 16)

            def store(n, i):
                sp.wait_ge(s_fx, n + 1)
                sp.dma_start(out[i].rearrange("(c p) d -> p c d", p=P), X[:, i]).then_inc(s_out, 16)

            for n, e in ((0, 0), (1, 1), (2, 2), (3, 0)):
                weights(n, e, n % 2)
            shift(0, 0)
            shift(0, 1)
            with sp.Fori(1, B - 2) as i:
                weights(i * 2 + 2, (i + 2) % E, 0)
                shift(i, 0)
                weights(i * 2 + 3, i % E, 1)
                shift(i, 1)
                store(i * 2 + 1, i - 1)
            weights(2 * B - 2, (B - 2) % E, 0)
            shift(B - 2, 0)
            weights(2 * B - 1, (B - 1) % E, 1)
            shift(B - 2, 1)
            store(2 * B - 3, B - 3)
            shift(B - 1, 0)
            shift(B - 1, 1)
            store(2 * B - 2, B - 2)
            store(2 * B - 1, B - 1)
            sp.wait_ge(s_out, 16 * B)

        CONSTS = 15 * 16

        def chunks(ap):
            return ap.rearrange("p c d -> p (c d)")

        K_BANKS, Q_BANKS = (2, 4), (6, 2)

        def tps(b0):
            return ps[:, b0:b0 + 2, :].rearrange("p b c -> p (b c)").bitcast(BF16).rearrange("p (n c) -> p n c", c=P)

        mps = ps[0:MB, 7, :].bitcast(BF16)[:, 0:N]

        def max_bank(m):
            return 4 - 2 * (m % 2) if m < MAX_LATE else 4 + (m - MAX_LATE) % 2

        def head_bank(n_):
            return 2 + n_ % 2 if n_ < OVERLAP else 2 + n_ % 4

        def q_rows(half_, a):
            return (QT[HROW * a:HROW * (a + 1), 8 * half_ + a:8 * half_ + 8:2, :].rearrange("p h (c k) -> p h c k", c=NC))

        def tps_rows(half_, a):
            return tps(Q_BANKS[half_])[HROW * a:HROW * (a + 1)].rearrange("p (h c) k -> p h c k", c=NC)

        @block.vector
        def _(dve):
            dve.wait_ge(s_const, CONSTS)
            nc.vector.tensor_copy(idb[:], idf[:]).then_inc(s_set, 1)
            nc.vector.tensor_copy(maskb[:], maskf[:]).then_inc(s_set, 1)
            nc.vector.memset(half[:], -0.5).then_inc(s_set, 1)
            dve.wait_ge(s_cT, 1)
            nc.vector.tensor_copy(cols[:], ps[:, 0, 0:NVEC]).then_inc(s_cols, 1)

            def fill():
                for zero in (va, st, QT):
                    nc.vector.memset(zero[:], 0.0).then_inc(s_fill, 1)
                dve.wait_ge(s_fill, 3)
                nc.vector.memset(va[:, :, :, DB:DB + 1].rearrange("p c h v -> p (c h) v"), 1.0).then_inc(s_fill, 1)
                for c in range(NC):
                    nc.vector.memset(st[:, c, 1, :, SROW:SROW + MROW], 1.0).then_inc(s_fill, 1)

            def row_stats(i, stats, mv, s_stats, s_mv, n):
                dve.nop(nofuse=True)
                for c in range(NC):
                    last = nc.vector.bn_stats(stats[:, c, :], X[:, i, c, :])
                last.then_inc(s_stats, 1)
                dve.wait_ge(s_stats, n + 1)
                dve.nop(nofuse=True)
                for c in range(NC):
                    last = nc.vector.bn_aggr(mv[:, c, :], stats[:, c, :])
                last.then_inc(s_mv, 1)

            def mlp(step, second, n, i, par):
                if step == 0:
                    if second:
                        dve.wait_ge(s_x3, i + 1)
                    elif isinstance(n, int) and n == 0:
                        dve.wait_ge(s_x, 16)
                    else:
                        dve.wait_ge(s_x, 32)
                    row_stats(i, fst, fmv, s_fst, s_fmv, n)
                elif step == 1:
                    dve.wait_ge(s_frs, n * 4 + 4)
                    if not (isinstance(n, int) and n == 0):
                        dve.wait_ge(s_xlT, n)
                    for c in range(NC):
                        last = nc.vector.tensor_scalar(z[:, c, :], X[:, i, c, :], fmv[:, c, 0:1], ft[:, 1, c:c + 1],
                                                       ALU.subtract, ALU.mult)
                    last.then_inc(s_z, 1)
                    for c in range(NC):
                        last = nc.vector.tensor_scalar(xl[:, c, :], X[:, i, c, :], fmv[:, c, 0:1], ft[:, 3, c:c + 1],
                                                       ALU.subtract, ALU.mult)
                    last.then_inc(s_xl, 1)
                elif step == 12:
                    if not (isinstance(n, int) and n == 0):
                        dve.wait_ge(s_foc, n)
                    dve.wait_ge(s_fo, n + 1)
                    nc.vector.tensor_tensor(pre[:], ps[:, 0, :].rearrange("p (c d) -> p c d", c=NC),
                                            nb[:].unsqueeze(1).broadcast_to([P, NC, D]), ALU.add).then_inc(s_pre, 1)

            def row_norm(i, n):
                dve.wait_ge(s_fx, n + 1)
                if not (isinstance(i, int) and i == 0):
                    dve.wait_ge(s_xnT, i)
                row_stats(i, ast, amv, s_ast, s_amv, i)
                dve.wait_ge(s_ars, i * 2 + 2)
                for c in range(NC):
                    last = nc.vector.tensor_scalar(xn[:, c, :], X[:, i, c, :], amv[:, c, 0:1], at_[:, 1, c:c + 1],
                                                   ALU.subtract, ALU.mult)
                last.then_inc(s_xn, 1)

            def rope(i):
                dve.wait_ge(s_va, i + 1)
                qk = ps[:, 2:6, 0:2 * D].rearrange("p c (h d) -> p c h d", d=DB)
                flat = lambda ap: ap.rearrange("p c a h d -> p c (a h) d")
                cs = cosb[:].unsqueeze(2).broadcast_to([P, NC, 2 * HB, DB])
                sn = sinb[:].unsqueeze(2).broadcast_to([P, NC, 2 * HB, DB])
                nc.vector.tensor_tensor(flat(qc[:]), qk, cs, ALU.mult)
                for a in range(2):
                    to, of = slice(4 * a, 4 * a + 4), slice(4 - 4 * a, 8 - 4 * a)
                    last = nc.vector.tensor_tensor(flat(qs[:])[:, :, :, to], qk[:, :, :, of], sn[:, :, :, to], ALU.mult)
                last.then_inc(s_rp, 1)
                dve.wait_ge(s_rp, i + 1)
                nc.vector.tensor_tensor(rows(qc[:]), rows(qc[:]), rows(qs[:]), ALU.add).then_inc(s_rs, 1)

            def rows(ap):
                return ap.rearrange("p c a h d -> p (c a h) d")

            q = lambda k: st[:, :, 0, :, k * DB:(k + 1) * DB]
            k_ = lambda k: st[:, :, 1, :, k * DB:(k + 1) * DB]

            def part_1(i):
                dve.wait_ge(s_p1, i + 1)
                nc.vector.tensor_tensor(rows(r1[:]), rows(qc[:]), rows(st[:, :, :, :, 0:DB]), ALU.subtract).then_inc(s_r1, 1)
                nc.vector.tensor_copy(q(1), q(0))
                nc.vector.tensor_copy(q(2), q(0))
                nc.vector.tensor_copy(k_(3), k_(0))
                nc.vector.tensor_copy(k_(5), k_(0))

            def part_2(i):
                dve.wait_ge(s_p2, i + 1)
                for a, k in ((0, 3), (1, 1)):
                    last = nc.vector.tensor_tensor(r2[:, :, a], r1[:, :, a], st[:, :, a, :, k * DB:(k + 1) * DB], ALU.subtract)
                last.then_inc(s_r2, 1)
                nc.vector.tensor_copy(q(4), q(3))
                nc.vector.tensor_copy(k_(4), k_(1)).then_inc(s_p3, 1)

            def keep_transposed(i):
                for half_ in range(2):
                    dve.wait_ge(s_kT, i * 2 + (half_ + 1))
                    nc.vector.tensor_copy(KT[:, 4 * half_:4 * half_ + 4, :].rearrange("p h (c k) -> p (h c) k", c=NC),
                                          tps(K_BANKS[half_])).then_inc(s_kTc, 1)
                for half_ in range(2):
                    dve.wait_ge(s_qT, i * 2 + (half_ + 1))
                    nc.vector.tensor_copy(q_rows(half_, 1), tps_rows(half_, 1)).then_inc(s_qTo, 1)

            def maximum(i, m):
                c, h, nh, banks = MAX_ITEMS[m]
                w = (c + 1) * P
                b0 = max_bank(m)
                dve.wait_ge(s_S, i * NMAX + (m + 1))
                S = ps[:, b0:b0 + banks, 0:nh // banks * w].rearrange("p b (h w) -> p b h w", w=w)
                nc.vector.tensor_reduce(nm[:, 0, c, h:h + nh].rearrange("p (b h) -> p b h", b=banks), S,
                                        AX.X, ALU.max, negate=True).then_inc(s_Sc, 1)

            def shift(i, half_):
                m = lambda k: mb[:, half_, :, :, k, :]
                f = lambda k: nm[:, k, :, 8 * half_:8 * half_ + 8].rearrange("p c (h a) -> p c a h", a=2)
                dve.wait_ge(s_Sc, i * NMAX + (MAX_HALF, NMAX)[half_])
                done = i * 8 + 4 * half_
                nc.vector.tensor_copy(m(0), f(0)).then_inc(s_nm, 1)
                dve.wait_ge(s_nm, done + 1)
                nc.vector.tensor_tensor(f(1), f(0), m(0), ALU.subtract).then_inc(s_nm, 1)
                dve.wait_ge(s_nm, done + 2)
                nc.vector.tensor_copy(m(1), f(1)).then_inc(s_nm, 1)
                dve.wait_ge(s_nm, done + 3)
                nc.vector.tensor_tensor(f(2), f(1), m(1), ALU.subtract).then_inc(s_nm, 1)
                dve.wait_ge(s_nm, done + 4)
                nc.vector.tensor_copy(m(2), f(2)).then_inc(s_m3, 1)

            def keep_output(i, G):
                dve.wait_ge(s_pv, i * NHG + (G + 1))
                nc.vector.tensor_copy(oTs[:, G, :], ps[:, 6 + G % 2, :]).then_inc(s_pvc, 1)

            def gather(i):
                dve.wait_ge(s_oB, i + 1)
                O = ps[:, 2:6, :].rearrange("p c (h v) -> p c h v", v=VC)
                nc.vector.reciprocal(rec[:], O[:, :, :, DB]).then_inc(s_rec, 1)
                dve.wait_ge(s_rec, i + 1)
                nc.vector.tensor_tensor(o2[:].rearrange("p c (h v) -> p c h v", h=HB), O[:, :, :, 0:DB],
                                        rec[:].unsqueeze(3).broadcast_to([P, NC, HB, DB]), ALU.mult).then_inc(s_o2, 1)

            def add(i):
                dve.wait_ge(s_y, i + 1)
                dve.wait_ge(s_xb, i + 1)
                nc.vector.tensor_tensor(chunks(X[:, i]), ps[:, 6, :], chunks(X[:, i]), ALU.add).then_inc(s_x3, 1)

            def attn(part, i, m=None):
                if part == "fill":
                    fill()
                elif part == "norm":
                    row_norm(i, m)
                elif part == "rope":
                    rope(i)
                elif part == "part 1":
                    part_1(i)
                elif part == "part 2":
                    part_2(i)
                elif part == "transpose":
                    keep_transposed(i)
                elif part == "max":
                    maximum(i, m)
                elif part == "shift":
                    shift(i, m)
                elif part == "outputs" and m > HG and m % HG == HG - 1:
                    keep_output(i, m // HG - 1)
                elif part == "last":
                    keep_output(i, NHG - 1)
                elif part == "gather":
                    gather(i)
                elif part == "add":
                    add(i)

            batches(dve, mlp, attn)

        @block.gpsimd
        def _(pool):
            pool.wait_ge(s_set, 3)

            def mlp(step, second, n, i, par):
                if step == 0:
                    pool.wait_ge(s_fmv, n + 1)
                    pool.nop(nofuse=True)
                    var = fmv[:, :, 1]
                    nc.gpsimd.tensor_scalar(ft[:, 0], var, EPS, None, ALU.add).then_inc(s_frs, 1)
                    nc.gpsimd.tensor_scalar(ft[:, 2], var, 1.0 + EPS, EPS * EPS, ALU.mult, ALU.add).then_inc(s_frs, 1)
                    for k in range(2):
                        pool.wait_ge(s_frs, n * 4 + 2)
                        pool.nop(nofuse=True)
                        nc.gpsimd.tensor_tensor(ft[:, 2 * k + 1], ft[:, 2 * k], half[:], ALU.pow).then_inc(s_frs, 1)
                elif step == 13:
                    pool.wait_ge(s_foc, n + 1)
                    pool.nop(nofuse=True)
                    nc.gpsimd.tensor_tensor(chunks(X[:, i]), chunks(X[:, i]), chunks(fo[:]), ALU.add).then_inc(s_fx, 1)

            def attn(part, i, m=None):
                if part == "norm":
                    pool.wait_ge(s_amv, i + 1)
                    pool.nop(nofuse=True)
                    nc.gpsimd.tensor_scalar(at_[:, 0], amv[:, :, 1], EPS, None, ALU.add).then_inc(s_ars, 1)
                    pool.wait_ge(s_ars, i * 2 + 1)
                    nc.gpsimd.tensor_tensor(at_[:, 1], at_[:, 0], half[:], ALU.pow).then_inc(s_ars, 1)
                    pool.wait_ge(s_xn, i + 1)
                    pool.nop(nofuse=True)
                    nc.gpsimd.tensor_tensor(X[:, i], X[:, i], bp[:].unsqueeze(1).broadcast_to([P, NC, D]), ALU.add).then_inc(s_xb, 1)

            batches(pool, mlp, attn)

        @block.scalar
        def _(act):
            act.wait_ge(s_cols, 1)

            def mlp(step, second, n, i, par):
                if step == 2:
                    act.wait_ge(s_xlT, n + 1)
                    nc.scalar.activation(xlT[:], ps[:, 1, :], ACT.Identity, bias=cols[:, C_B:C_B + 1], scale=cols[:, C_G:C_G + 1]).then_inc(s_xlTc, 1)
                elif step == 3:
                    act.wait_ge(s_xa, n + 1)
                    nc.scalar.activation(xaT[:], ps[:, 0, :], ACT.Identity, bias=cols[:, C_AB:C_AB + 1]).then_inc(s_xac, 1)
                elif 4 <= step <= 7:
                    j = step - 4
                    act.wait_ge(s_h, n * NF + (j + 1))
                    act.nop(nofuse=True)
                    nc.scalar.activation(hT[:, j, :], ps[:, (j + 1) % 2, :], ACT.Gelu,
                                         bias=cols[:, bass.ds(i % E * NF + j, 1)]).then_inc(s_hc, 1)
                elif step == 11:
                    act.wait_ge(s_yT, n + 1)
                    act.nop(nofuse=True)
                    nc.scalar.activation(yT[:], ps[:, 1, :], ACT.Identity, bias=cols[:, bass.ds(i % E + C_B2, 1)]).then_inc(s_yTc, 1)
                elif step == 13:
                    if not (isinstance(n, int) and n == 0):
                        act.wait_ge(s_fx, n)
                    act.wait_ge(s_pre, n + 1)
                    nc.scalar.activation(fo[:], pre[:], ACT.Gelu).then_inc(s_foc, 1)

            def gelu_table(i):
                nc.scalar.activation(warm[:], cols[:, 0:1], ACT.Gelu)

            def part(a, k):
                return st[:, :, a, :, k * DB:(k + 1) * DB]

            def rows(i):
                act.wait_ge(s_xnT, i + 1)
                nc.scalar.activation(xnT[:], ps[:, 6, :], ACT.Copy).then_inc(s_xnTc, 1)

            def project(i):
                act.wait_ge(s_qkv, i + 1)
                nc.scalar.activation(va[:, :, :, 0:DB], ps[:, 2:6, 2 * D:3 * D].rearrange("p c (h d) -> p c h d", d=DB),
                                     ACT.Copy).then_inc(s_va, 1)

            def part_1(i):
                act.wait_ge(s_rs, i + 1)
                for a in range(2):
                    last = nc.scalar.activation(part(a, 0), qc[:, :, a], ACT.Copy)
                last.then_inc(s_p1, 1)

            def part_2(i):
                act.wait_ge(s_r1, i + 1)
                nc.scalar.activation(part(0, 3), r1[:, :, 0], ACT.Copy)
                nc.scalar.activation(part(1, 1), r1[:, :, 1], ACT.Copy).then_inc(s_p2, 1)

            def part_3(i):
                act.wait_ge(s_r2, i + 1)
                nc.scalar.activation(part(0, 5), r2[:, :, 0], ACT.Copy)
                nc.scalar.activation(part(1, 2), r2[:, :, 1], ACT.Copy).then_inc(s_p3a, 1)

            def keep_transposed(i):
                for half_ in range(2):
                    act.wait_ge(s_qT, i * 2 + (half_ + 1))
                    nc.scalar.activation(q_rows(half_, 0), tps_rows(half_, 0), ACT.Copy).then_inc(s_qTe, 1)

            def shift(i, half_):
                act.wait_ge(s_mT, i * 2 + (half_ + 1))
                nc.scalar.activation(mT[:, half_, :], mps, ACT.Copy).then_inc(s_mTc, 1)

            def probabilities(i, n_):
                h, k = n_ // NTI, n_ % NTI
                w = sum(x[2] for x in T_ITEMS[k])
                act.wait_ge(s_T, i * (HB * NTI) + (n_ + 1))
                nc.scalar.activation(PT[:, h // HG % 2, h % HG, PT_AT[k]:PT_AT[k] + w], ps[:, head_bank(n_), 0:w],
                                     ACT.Exp, scale=float(DB) ** -0.5).then_inc(s_Tc, 1)

            def output_rows(i):
                act.wait_ge(s_o2T, i + 1)
                nc.scalar.activation(o2T[:], ps[:, 7, :], ACT.Copy).then_inc(s_o2Tc, 1)

            def attn(part, i, m=None):
                if part == "filled":
                    act.wait_ge(s_fill, 4 + NC)
                elif part == "rows":
                    rows(i)
                elif part == "project":
                    project(i)
                elif part == "rope":
                    gelu_table(i)
                elif part == "part 1":
                    part_1(i)
                elif part == "part 2":
                    part_2(i)
                elif part == "part 3":
                    part_3(i)
                elif part == "transpose":
                    keep_transposed(i)
                elif part == "shift rows":
                    shift(i, m)
                elif part == "scores":
                    probabilities(i, m)
                elif part == "output rows":
                    output_rows(i)

            batches(act, mlp, attn)

        @block.tensor
        def _(pe):
            pe.wait_ge(s_const, CONSTS)
            nc.tensor.transpose(ps[:, 0, 0:NVEC], vecs[:], idf[0:NVEC, 0:NVEC]).then_inc(s_cT, 1)
            pe.wait_ge(s_set, 3)
            pe.wait_ge(s_cols, 1)

            def cols_of(c):
                return slice(c * P, (c + 1) * P)

            def mlp(step, second, n, i, par):
                if step == 2:
                    if not (isinstance(n, int) and n == 0):
                        pe.wait_ge(s_pre, n)
                    pe.wait_ge(s_z, n + 1)
                    for c in range(NC):
                        last = nc.tensor.matmul(ps[:, 0, cols_of(c)], z[:, c, :], idf[:], start=(c == 0), stop=False,
                                                is_transpose=True, skip_group_check=True)
                    pe.wait_ge(s_xl, n + 1)
                    for c in range(NC):
                        last = nc.tensor.transpose(ps[:, 1, cols_of(c)], xl[:, c, :], idf[:])
                    last.then_inc(s_xlT, 1)
                elif step == 3:
                    pe.wait_ge(s_xlTc, n + 1)
                    nc.tensor.matmul(ps[:, 0, :], wa[:], xlT[:], start=False, stop=True, skip_group_check=True).then_inc(s_xa, 1)
                elif 4 <= step <= 7:
                    j = step - 4
                    if j == 0:
                        pe.wait_ge(s_w[par], (n - par) * 16 + 32)
                        pe.wait_ge(s_xac, n + 1)
                    if j >= 2:
                        pe.wait_ge(s_hc, n * NF + (j - 1))
                    nc.tensor.matmul(ps[:, (j + 1) % 2, :], w1s[:, par, cols_of(j)], xaT[:], start=True, stop=True).then_inc(s_h, 1)
                elif 8 <= step <= 11:
                    j = step - 8
                    pe.wait_ge(s_hc, n * NF + (max(j, 2) + 1))
                    last = nc.tensor.matmul(ps[:, 1, :], w2s[:, par, j, :], hT[:, j, :], start=(j == 0), stop=(j == NF - 1))
                    if j == NF - 1:
                        last.then_inc(s_yT, 1)
                elif step == 12:
                    pe.wait_ge(s_yTc, n + 1)
                    for c in range(NC):
                        last = nc.tensor.matmul(ps[:, 0, cols_of(c)], yT[:, cols_of(c)], wn[:], start=True, stop=True)
                    last.then_inc(s_fo, 1)

            def rows(i):
                pe.wait_ge(s_xn, i + 1)
                if not (isinstance(i, int) and i == 0):
                    pe.wait_ge(s_pvc, i * NHG - 1)
                for c in range(NC):
                    last = nc.tensor.transpose(ps[:, 6, cols_of(c)], xn[:, c, :], idf[:])
                last.then_inc(s_xnT, 1)

            def project(i):
                pe.wait_ge(s_xnTc, i + 1)
                for c in range(NC):
                    last = nc.tensor.matmul(ps[:, 2 + c, 0:3 * D], xnT[:, cols_of(c)], wb[:], start=True, stop=True)
                last.then_inc(s_qkv, 1)

            def transposed(a, half_, sem_):
                T = tps((Q_BANKS, K_BANKS)[a][half_])
                for hh in range(4):
                    hp = 4 * half_ + hh
                    for c in range(NC):
                        last = nc.tensor.transpose(T[:, hh * NC + c, :], st[:, c, a, 2 * hp:2 * hp + 2, :].rearrange("p h r -> p (h r)"), idb[:])
                last.then_inc(sem_, 1)

            def transpose(i):
                pe.wait_ge(s_p3, i + 1)
                pe.wait_ge(s_p3a, i + 1)
                transposed(1, 0, s_kT)
                transposed(1, 1, s_kT)
                if not (isinstance(i, int) and i == 0):
                    pe.wait_ge(s_x3, i)
                transposed(0, 0, s_qT)
                pe.wait_ge(s_kTc, i * 2 + 1)
                transposed(0, 1, s_qT)

            def maximum(i, m):
                c, h0, nh, banks = MAX_ITEMS[m]
                w = (c + 1) * P
                b0 = max_bank(m)
                if m == 0:
                    pe.wait_ge(s_kTc, i * 2 + 2)
                if m < 2:
                    pe.wait_ge(s_qTe, i * 2 + (m + 1))
                    pe.wait_ge(s_qTo, i * 2 + (m + 1))
                if 2 <= m < MAX_LATE or m >= MAX_LATE + 2:
                    pe.wait_ge(s_Sc, i * NMAX + (m - 1))
                elif m == MAX_LATE:
                    pe.wait_ge(s_Sc, i * NMAX + m)
                for b in range(banks):
                    each = [(h0 + b * (nh // banks) + k, k * w) for k in range(nh // banks)]
                    for h, at in each:
                        nc.tensor.matmul(ps[:, b0 + b, at:at + w], QT[:, h, cols_of(c)], KT[:, h // 2, 0:w],
                                         start=(at == 0), stop=False, skip_group_check=True)
                    for h, at in each:
                        last = nc.tensor.matmul(ps[:, b0 + b, at + c * P:at + w], idb[:], maskb[:, 0, :],
                                                start=False, stop=True, skip_group_check=True)
                last.then_inc(s_S, 1)

            def shift(i, half_):
                pe.wait_ge(s_m3, i * 2 + (half_ + 1))
                if half_:
                    pe.wait_ge(s_mTc, i * 2 + 1)
                pe.nop(nofuse=True)
                for c in range(NC):
                    last = nc.tensor.transpose(mps[:, cols_of(c)], mb[:, half_, c].rearrange("p a k h -> p (a k h)"), idb[:])
                last.then_inc(s_mT, 1)

            def pv(i, G, j):
                if j == 0:
                    if G >= 2:
                        pe.wait_ge(s_pvc, i * NHG + (G - 1))
                    pe.wait_ge(s_Tc, i * (HB * NTI) + (G + 1) * HG * NTI)
                for k in range(HG):
                    last = nc.tensor.matmul(ps[VC * k:VC * (k + 1), 6 + G % 2, j * P:N], va[:, j, G * HG + k, :],
                                            PT[:, G % 2, k, KEY_AT[j]:KEY_AT[j] + N - j * P], start=(j == 0), stop=(j == NC - 1),
                                            skip_group_check=True)
                if j == NC - 1:
                    last.then_inc(s_pv, 1)

            def scores(i, n_):
                h, k = n_ // NTI, n_ % NTI
                if n_ % (HB * NTI // 2) == 0:
                    pe.wait_ge(s_mq, i * 64 + 32 * (h // (HB // 2) + 1))
                if n_ == 0:
                    pe.wait_ge(s_Sc, i * NMAX + (MAX_LATE - 1))
                elif n_ == OVERLAP + 2:
                    pe.wait_ge(s_Sc, i * NMAX + NMAX)
                elif 2 <= n_ < OVERLAP + 2:
                    pe.wait_ge(s_Tc, i * (HB * NTI) + (n_ - 1))
                elif n_ >= OVERLAP + 4:
                    pe.wait_ge(s_Tc, i * (HB * NTI) + (n_ - 3))
                for m, (j, at, w) in enumerate(T_ITEMS[k]):
                    nc.tensor.matmul(ps[:, head_bank(n_), at:at + w], KT[:, h // 2, cols_of(j)], QT[:, h, j * P:N],
                                     start=(m == 0), stop=False, skip_group_check=True)
                for m, (j, at, w) in enumerate(T_ITEMS[k]):
                    last = nc.tensor.matmul(ps[:, head_bank(n_), at:at + P], idb[:], maskb[:, 1, :],
                                            start=False, stop=True, skip_group_check=True)
                last.then_inc(s_T, 1)

            def outputs(i, h):
                if h > HG:
                    for j in ((), (0,), (1,), (2, 3))[h % HG]:
                        pv(i, h // HG - 1, j)

            def last_outputs(i):
                for j in range(NC):
                    pv(i, NHG - 1, j)

            def gather(i):
                pe.wait_ge(s_pvc, i * NHG + NHG)
                for c in range(NC):
                    for G in range(NHG):
                        last = nc.tensor.transpose(ps[:, 2 + c, cols_of(G)], oTs[:, G, cols_of(c)], idf[:])
                last.then_inc(s_oB, 1)

            def output_rows(i):
                pe.wait_ge(s_o2, i + 1)
                for c in range(NC):
                    last = nc.tensor.transpose(ps[:, 7, cols_of(c)], o2[:, c, :], idf[:])
                last.then_inc(s_o2T, 1)

            def output(i):
                pe.wait_ge(s_o2Tc, i + 1)
                for c in range(NC):
                    last = nc.tensor.matmul(ps[:, 6, cols_of(c)], o2T[:, cols_of(c)], wp[:], start=True, stop=True)
                last.then_inc(s_y, 1)

            def attn(part, i, m=None):
                if part == "filled":
                    pe.wait_ge(s_fill, 4 + NC)
                elif part == "rows":
                    rows(i)
                elif part == "project":
                    project(i)
                elif part == "transpose":
                    transpose(i)
                elif part == "max":
                    maximum(i, m)
                elif part == "shift rows":
                    shift(i, m)
                elif part == "scores":
                    scores(i, m)
                elif part == "outputs":
                    outputs(i, m)
                elif part == "last":
                    last_outputs(i)
                elif part == "gather":
                    gather(i)
                elif part == "output rows":
                    output_rows(i)
                elif part == "out":
                    output(i)

            batches(pe, mlp, attn)


_INS = ["L0_attn_a_x", "L0_attn_a_w_qkv", "L0_attn_a_w_out", "L0_attn_a_ln_g", "L0_attn_a_ln_b", "L0_attn_a_mem_beta",
        "L0_attn_b_w_qkv", "L0_attn_b_w_proj", "L0_attn_b_b_proj", "L0_ffn_ln_g", "L0_ffn_ln_b", "L0_ffn_attn_w",
        "L0_ffn_attn_b", "L0_ffn_w1", "L0_ffn_b1", "L0_ffn_w2", "L0_ffn_b2", "L0_ffn_next_w", "L0_ffn_next_b"]
MASKED = -1e30


def shape_constants():
    f32 = np.float32
    freq = (f32(10000.0) ** (-np.arange(0, DA, 2, dtype=f32) / f32(DA))).astype(f32)
    angle = np.arange(N, dtype=f32)[:, None] * freq
    cos_a = np.repeat(np.cos(angle), 2, -1)
    sin_a = np.repeat(np.sin(angle), 2, -1) * np.tile(np.array([-1, 1], f32), DA // 2)

    def by_tile(t):
        return np.ascontiguousarray(np.tile(t.reshape(NSEG, SEG, DA).transpose(1, 0, 2), (BG, 1, 1)), dtype=f32)

    seg = np.arange(SEG)
    seg_mask = np.tile(np.where(seg[None] > seg[:, None], f32(MASKED), f32(0)), (BG, HP))
    freq_b = (f32(1.0) / f32(10000.0) ** (np.arange(0, DB, 2, dtype=f32) / f32(DB))).astype(f32)
    angle_b = np.arange(N, dtype=f32)[:, None] * freq_b
    cos_b = np.concatenate([np.cos(angle_b), np.cos(angle_b)], -1)
    sin_b = np.concatenate([-np.sin(angle_b), np.sin(angle_b)], -1)

    def by_chunk(t):
        return np.ascontiguousarray(t.reshape(NC, P, DB).transpose(1, 0, 2), dtype=f32)

    row = np.arange(P)
    causal = np.where(row[None] > row[:, None], f32(MASKED), f32(0))
    return {"rope_cos_a": by_tile(cos_a), "rope_sin_a": by_tile(sin_a), "seg_mask": seg_mask.astype(f32),
            "rope_cos_b": by_chunk(cos_b), "rope_sin_b": by_chunk(sin_b),
            "causal": np.ascontiguousarray(np.stack([causal, causal.T], 1)), "ident": np.eye(P, dtype=f32)}


def kernel(**inputs):
    import concourse.bacc as bacc
    from concourse.bass_utils import run_bass_kernel_spmd

    nc = bacc.Bacc("TRN2", target_bir_lowering=False, num_devices=1)
    arrays, ap = {}, {}
    for name, a in [(n, np.ascontiguousarray(inputs[n])) for n in _INS] + list(shape_constants().items()):
        arrays[f"in_{name}_dram"] = a
        ap[name] = nc.dram_tensor(f"in_{name}_dram", a.shape, mybir.dt.from_np(a.dtype), kind="ExternalInput").ap()
    x1 = nc.dram_tensor("x1_dram", (B, N, D), F32).ap()
    out = nc.dram_tensor("out_0_dram", (B, N, D), F32, kind="ExternalOutput").ap()
    a, b, f = "L0_attn_a_", "L0_attn_b_", "L0_ffn_"
    attn_a_layer(nc, ap[a + "x"], ap[a + "w_qkv"], ap[a + "w_out"], ap[a + "ln_g"], ap[a + "ln_b"], ap[a + "mem_beta"],
                 ap["rope_cos_a"], ap["rope_sin_a"], ap["seg_mask"], ap["ident"], x1)
    mlp_attn_mlp_layers(nc, x1, ap[b + "w_qkv"], ap[b + "w_proj"], ap[b + "b_proj"], ap[f + "ln_g"], ap[f + "ln_b"],
                        ap[f + "attn_w"], ap[f + "attn_b"], ap[f + "w1"], ap[f + "b1"], ap[f + "w2"], ap[f + "b2"],
                        ap[f + "next_w"], ap[f + "next_b"], ap["rope_cos_b"], ap["rope_sin_b"], ap["causal"], ap["ident"], out)
    r = run_bass_kernel_spmd(nc, [arrays], core_ids=[0])
    return r.results[0]["out_0_dram"]
```
